# Optimizing a Trainium2 kernel written in Bass

```python
import numpy as np
import jax
import jax.numpy as jnp

def _softmax(x, axis=-1):
    return jax.nn.softmax(x, axis=axis)

def _gelu(x):
    return jax.nn.gelu(x, approximate=True)

def _silu(x):
    return jax.nn.silu(x)

def _sigmoid(x):
    return jax.nn.sigmoid(x)

def _layernorm(x, axis=-1, eps=1e-05):
    m = jnp.mean(x, axis=axis, keepdims=True)
    v = jnp.var(x, axis=axis, keepdims=True)
    return (x - m) / jnp.sqrt(v + eps)

def _scatter_add(tgt, idx, src, axis=0):
    return tgt.at[idx].add(src)

def _segment_sum(src, seg, n):
    return jax.ops.segment_sum(src, seg, n)
kernel_name = 'mk_vit_tower_cls_d1_tok_img2048_r4_17b37c'

def setup_inputs(seed: int=0):
    np.random.seed(seed)
    _w = jnp.asarray

    def _rec_inputs():
        import jax
        import jax.numpy as jnp
        _rk = jax.random.key(seed)
        x = -0.00178296 + 0.498989 * jax.random.normal(jax.random.fold_in(_rk, 1), (8, 256, 64, 2), jnp.float32)
        cls_tok = 0.02 * jax.random.normal(jax.random.fold_in(_rk, 5), (1, 1, 512), jnp.float32)
        return (x, cls_tok)
    x, cls_tok = _rec_inputs()

    def _L0_tok_setup():
        import jax, jax.numpy as jnp
        import numpy as np
        H, N, CCH, LLEN = (256, 64, 1, 512)
        key = jax.random.key(seed)
        k1, k2 = jax.random.split(key, 2)
        log_dt = jax.random.uniform(k1, (H,), jnp.float32, float(np.log(0.001)), float(np.log(0.1)))
        C = 0.5 * jax.random.normal(k2, (CCH, H, N, 2), jnp.float32)
        log_w_real = jnp.full((H, N), float(np.log(0.5)), jnp.float32)
        w_imag = jnp.broadcast_to(np.pi * jnp.arange(N, dtype=jnp.float32), (H, N)) + jnp.zeros((H, N), jnp.float32)
        return {'C': C, 'log_dt': log_dt, 'log_w_real': log_w_real, 'w_imag': w_imag, 'L': LLEN}
    _L0_tok_all = _L0_tok_setup()
    _L0_tok_in = {k: v for k, v in _L0_tok_all.items() if k in ('log_dt', 'log_w_real', 'w_imag')}
    del _L0_tok_all

    def _L0_attn_setup():
        import jax, jax.numpy as jnp
        import numpy as np
        B, S, H_DIM = (2, 512, 512)
        N_HEADS, D_HEAD = (16, 128)
        key = jax.random.key(seed)
        k1, k2, k3 = jax.random.split(key, 3)
        x = jax.random.normal(k1, (B, S, H_DIM), dtype=jnp.float32)
        w_qkv = jax.random.normal(k2, (H_DIM, 3 * N_HEADS * D_HEAD), dtype=jnp.float32) * 0.02
        w_o = jax.random.normal(k3, (N_HEADS * D_HEAD, H_DIM), dtype=jnp.float32) * 0.02
        return {'x': x, 'w_qkv': w_qkv, 'w_o': w_o}
    _L0_attn_all = _L0_attn_setup()
    _L0_attn_in = {k: v for k, v in _L0_attn_all.items() if k in ('w_qkv', 'w_o')}
    del _L0_attn_all

    def _L0_ffn_setup():
        import jax, jax.numpy as jnp
        import numpy as np
        B, T, D = (2, 256, 512)
        H, K, DK = (4, 8, 64)
        E = 4096
        NK = 128
        key = jax.random.key(seed)
        k1, k2, k3, k4, k5 = jax.random.split(key, 5)
        x = jax.random.normal(k1, (B, T, D), dtype=jnp.float32)
        Wq = jax.random.normal(k2, (D, 2 * H * DK), dtype=jnp.float32) * 0.02
        keys = jax.random.normal(k3, (H, NK, 2, DK), dtype=jnp.float32) * 0.02
        e_down = jax.random.normal(k4, (E, D), dtype=jnp.float32) * 0.01
        e_up = jax.random.normal(k5, (E, D), dtype=jnp.float32) * 0.01
        return {'x': x, 'Wq': Wq, 'keys': keys, 'e_down': e_down, 'e_up': e_up}
    _L0_ffn_all = _L0_ffn_setup()
    _L0_ffn_in = {k: v for k, v in _L0_ffn_all.items() if k in ('Wq', 'keys', 'e_down', 'e_up')}
    del _L0_ffn_all
    return {'x': x, 'cls_tok': cls_tok, 'L0_tok_log_dt': _L0_tok_in['log_dt'], 'L0_tok_log_w_real': _L0_tok_in['log_w_real'], 'L0_tok_w_imag': _L0_tok_in['w_imag'], 'L0_attn_w_qkv': _L0_attn_in['w_qkv'], 'L0_attn_w_o': _L0_attn_in['w_o'], 'L0_ffn_Wq': _L0_ffn_in['Wq'], 'L0_ffn_keys': _L0_ffn_in['keys'], 'L0_ffn_e_down': _L0_ffn_in['e_down'], 'L0_ffn_e_up': _L0_ffn_in['e_up']}

def reference(x, cls_tok, L0_tok_log_dt, L0_tok_log_w_real, L0_tok_w_imag, L0_attn_w_qkv, L0_attn_w_o, L0_ffn_Wq, L0_ffn_keys, L0_ffn_e_down, L0_ffn_e_up):
    import jax
    import jax.numpy as jnp

    def _L0_tok_ref(C, log_dt, log_w_real, w_imag, L):
        import jax, jax.numpy as jnp
        import numpy as np
        H, N, CCH, LLEN = (256, 64, 1, 512)
        dt = jnp.exp(log_dt)
        Cc = C[..., 0] + 1j * C[..., 1]
        w = -jnp.exp(log_w_real) + 1j * w_imag
        dtA = w * dt[:, None]
        K = dtA[:, :, None] * jnp.arange(L)
        Cm = Cc * (jnp.exp(dtA) - 1.0) / w
        K = jnp.einsum('chn,hnl->chl', Cm, jnp.exp(K))
        return 2 * K.real

    def _L0_attn_ref(x, w_qkv, w_o):
        import jax, jax.numpy as jnp
        import numpy as np
        B, S, H_DIM = (2, 512, 512)
        N_HEADS, D_HEAD = (16, 128)
        b, s, _ = x.shape
        qkv = jnp.einsum('bsh,hf->bsf', x, w_qkv)
        qkv = qkv.reshape(b, s, 3, N_HEADS, D_HEAD)
        q, k, v = (qkv[:, :, 0], qkv[:, :, 1], qkv[:, :, 2])
        q = q.transpose(0, 2, 1, 3)
        k = k.transpose(0, 2, 1, 3)
        v = v.transpose(0, 2, 1, 3)
        scores = jnp.einsum('bhqd,bhkd->bhqk', q, k) / jnp.sqrt(jnp.float32(D_HEAD))
        probs = jax.nn.softmax(scores, axis=-1)
        values = jnp.einsum('bhqk,bhkd->bhkd', probs, v)
        values = values.transpose(0, 2, 1, 3).reshape(b, s, N_HEADS * D_HEAD)
        out = jnp.einsum('bsf,fh->bsh', values, w_o)
        return out

    def _L0_ffn_ref(x, Wq, keys, e_down, e_up):
        import jax, jax.numpy as jnp
        import numpy as np
        B, T, D = (2, 256, 512)
        H, K, DK = (4, 8, 64)
        E = 4096
        NK = 128
        b, t, d = x.shape
        q = (x @ Wq).reshape(b, t, H, 2, DK)
        q1, q2 = (q[..., 0, :], q[..., 1, :])
        sim1 = jnp.einsum('bthd,hkd->bthk', q1, keys[:, :, 0, :])
        sim2 = jnp.einsum('bthd,hkd->bthk', q2, keys[:, :, 1, :])
        s1, i1 = jax.lax.top_k(sim1, K)
        s2, i2 = jax.lax.top_k(sim2, K)
        all_scores = (s1[..., :, None] + s2[..., None, :]).reshape(b, t, H, K * K)
        all_indices = (i1[..., :, None] * NK + i2[..., None, :]).reshape(b, t, H, K * K)
        final_scores, pk_idx = jax.lax.top_k(all_scores, K)
        final_indices = jnp.take_along_axis(all_indices, pk_idx, axis=-1)
        w_down = e_down[final_indices]
        w_up = e_up[final_indices]
        hidden = jnp.einsum('btd,bthkd->bthk', x, w_down)
        hidden = jax.nn.silu(hidden)
        hidden = hidden * jax.nn.relu(final_scores)
        out = jnp.einsum('bthk,bthkd->btd', hidden, w_up)
        return out
    h = _L0_tok_ref(x, L0_tok_log_dt, L0_tok_log_w_real, L0_tok_w_imag, 512)
    h = jnp.concatenate([jnp.broadcast_to(cls_tok, (h.shape[0], 1, h.shape[2])), h], axis=1)
    h = h + _L0_attn_ref(_layernorm(h, axis=-1), L0_attn_w_qkv, L0_attn_w_o)
    h = h + _L0_ffn_ref(_layernorm(h, axis=-1), L0_ffn_Wq, L0_ffn_keys, L0_ffn_e_down, L0_ffn_e_up)
    return h

_drawn_inputs = setup_inputs


def setup_inputs(seed=0):
    import zlib

    import numpy as np

    out = dict(_drawn_inputs(seed))
    spreads = {'L0_tok_log_w_real': (-0.6931471824645996, 0.2)}
    factors = {'L0_ffn_Wq': 8.0, 'L0_ffn_keys': 8.0}
    for name, (base, spread) in spreads.items():
        noise = np.random.default_rng([zlib.crc32(name.encode()), seed]).standard_normal(out[name].shape)
        drawn = base * np.exp(spread * noise) if base else spread * noise
        out[name] = jnp.asarray(drawn.astype(out[name].dtype))
    for name, factor in factors.items():
        out[name] = (out[name] * factor).astype(out[name].dtype)
    return out
```

```python
import math
from contextlib import ExitStack

import concourse.bass as bass
from concourse import mybir

F32 = mybir.dt.float32
F32R = mybir.dt.float32r
I32 = mybir.dt.int32
U32 = mybir.dt.uint32
ALU = mybir.AluOpType
ACT = mybir.ActivationFunctionType
AX = mybir.AxisListType

P = 128
B = 8
NCH = 256
NST = 64
D = 512
DC = D // P
TR = B * NCH
T = TR + B
HEADS = 16
DH = 128
SCALE = DH ** -0.5
EPS = 1e-5
GRP = 512
NG = TR // GRP
GROUPS = [(g * GRP, GRP) for g in range(NG)] + [(TR, B)]

ROUND = 1.5 * 2.0 ** 23
TWO_PI = 6.283185
LN2_HI = 0.693145751953125
LN2_LO = 1.42860677e-06


class Chain:

    def __init__(self, eng, sem):
        self.eng, self.sem, self.n = eng, sem, 0

    def link(self, instruction):
        self.n += 1
        instruction.then_inc(self.sem, 1)
        self.eng.wait_ge(self.sem, self.n)


def signals(nc, ctx, tag=""):
    made = []

    def clear():
        with nc.Block() as blk:
            @blk.sync
            def _(sp):
                for s in made:
                    sp.sem_clear(s)
        for s in made:
            nc.release_semaphore(s)

    def make(name):
        made.append(nc.alloc_semaphore(tag + name))
        return made[-1]

    ctx.callback(clear)
    return make


def wide(ap, shape):
    return ap.to_broadcast(list(shape))


def mixer_factors(nc, x, cls_tok, log_dt, log_w_real, w_imag, k, m):
    NA = DC - 1
    HN = 2 * NST
    CH = 16
    with ExitStack() as ctx:
        sb = lambda n, s, d=F32: ctx.enter_context(nc.sbuf_tensor(n, s, d))
        sem = signals(nc, ctx)
        Y = sb("a_logs", [P, 2 + HN])
        WI = sb("a_wimag", [P, HN])
        X = sb("a_x", [P, 2, B, NST, 2])
        KK = sb("a_k", [P, 2 + HN])
        RR = sb("a_r", [P, 2 + HN])
        EE = sb("a_e", [P, 2 + HN])
        II = sb("a_pow2", [P, 2 + HN], I32)
        EX = sb("a_exp", [P, 2 + HN])
        DR = sb("a_dr", [P, HN])
        DI = sb("a_di", [P, HN])
        TURN = sb("a_turn", [P, HN])
        T1 = sb("a_t1", [P, 3, HN])
        ANG = sb("a_ang", [P, 9, HN])
        SN = sb("a_sin", [P, 9, HN])
        ER = sb("a_er", [P, NA, HN])
        TH = sb("a_tanh", [P, HN])
        Q1 = sb("a_q1", [P, HN])
        Q2 = sb("a_q2", [P, HN])
        NR = sb("a_nr", [P, HN])
        NI = sb("a_ni", [P, HN])
        BR = sb("a_br", [P, 2, NST])
        BI = sb("a_bi", [P, 2, NST])
        CR = sb("a_cr", [P, 2, B, NST])
        CI = sb("a_ci", [P, 2, B, NST])
        C1 = sb("a_c1", [P, 2, B, NST])
        C2 = sb("a_c2", [P, 2, B, NST])
        PR = sb("a_pr", [P, NA, 2, NST])
        PI = sb("a_pi", [P, NA, 2, NST])
        NPR = sb("a_npr", [P, NA, 2, NST])
        M1 = sb("a_m1", [P, B, NA, NST])
        M2 = sb("a_m2", [P, B, NA, NST])
        UH = sb("a_uh", [P, 2, B, DC, NST, 2])
        DUP = sb("a_dup", [P, 5, NST, 2])
        IOT = sb("a_iota", [P, P], I32)
        CLS = sb("a_cls", [P, DC])
        PS = k["PS"]
        load_par = sem("a_load_par")
        load_x = sem("a_load_x")
        load_cls = sem("a_load_cls")
        ident_zero = sem("a_ident_zero")
        consts = sem("a_consts")
        iota_made = sem("a_iota_made")
        dve_chain = sem("a_dve_chain")
        args_ready = sem("a_args_ready")
        exps_ready = sem("a_exps_ready")
        sins_ready = sem("a_sins_ready")
        dup_ready = sem("a_dup_ready")
        u_ready = sem("a_u_ready")
        rows_t = sem("a_rows_t")
        u_t = sem("a_u_t")
        copied_v = sem("a_copied_v")
        copied_s = sem("a_copied_s")
        done = sem("a_done")
        blk = ctx.enter_context(nc.Block())

        @blk.sync
        def _(sp):
            sp.dma_start(Y[:, 0:2], log_dt.rearrange("(g p) -> p g", p=P), allow_slow_non_contiguous=True).then_inc(load_par, 16)
            sp.dma_start(Y[:, 2:].rearrange("p (g n) -> p g n", g=2),
                         log_w_real.rearrange("(g p) n -> p g n", p=P)).then_inc(load_par, 16)
            sp.dma_start(WI[:, :].rearrange("p (g n) -> p g n", g=2),
                         w_imag.rearrange("(g p) n -> p g n", p=P)).then_inc(load_par, 16)
            for g in range(2):
                sp.dma_start(X[:, g].rearrange("p c n r -> p c (n r)"),
                             x[:, g * P:(g + 1) * P].rearrange("c p n r -> p c (n r)")).then_inc(load_x, 16)
            sp.dma_start(CLS[:, :], cls_tok[0, 0, :].rearrange("(a p) -> p a", p=P), allow_slow_non_contiguous=True).then_inc(load_cls, 16)

        @blk.gpsimd
        def _(pool):
            pool.memset(k["ident"][:, :], 0.0).then_inc(ident_zero, 1)
            pool.iota(IOT[:, :], pattern=[[1, P]], base=0, channel_multiplier=0).then_inc(iota_made, 1)
            pool.memset(k["mean_w"][:, :], 1.0 / D).then_inc(consts, 1)
            pool.memset(DUP[:, 4, :, 0], 0.25).then_inc(consts, 1)
            pool.memset(DUP[:, 4, :, 1], 0.0).then_inc(consts, 1)
            pool.wait_ge(ident_zero, 1)
            pool.affine_select(out=k["ident"][:, :], in_=k["ident"][:, :], compare_op=ALU.not_equal, fill=1.0,
                               base=0, pattern=[[-1, P]], channel_multiplier=1).then_inc(consts, 1)
            pool.wait_ge(iota_made, 1)
            pool.tensor_copy(m["iota"][:, :], IOT[:, :]).then_inc(consts, 1)
            pool.wait_ge(load_cls, 16)
            pool.tensor_copy(k["HT"][:, :, TR:T], wide(CLS[:, :, None], [P, DC, B])).then_inc(consts, 1)
            pool.wait_ge(consts, 6)

        @blk.vector
        def _(dve):
            link = Chain(dve, dve_chain).link
            dve.wait_ge(load_par, 48)
            link(dve.tensor_scalar(KK[:, :], Y[:, :], 1 / math.log(2), ROUND, ALU.mult, ALU.add))
            link(dve.tensor_scalar(KK[:, :], KK[:, :], ROUND, -126.0, ALU.subtract, ALU.max))
            link(dve.tensor_scalar(KK[:, :], KK[:, :], 127.0, None, ALU.min))
            link(dve.scalar_tensor_tensor(RR[:, :], KK[:, :], -LN2_HI, Y[:, :], ALU.mult, ALU.add))
            link(dve.scalar_tensor_tensor(RR[:, :], KK[:, :], -LN2_LO, RR[:, :], ALU.mult, ALU.add))
            link(dve.tensor_scalar(EE[:, :], RR[:, :], 1 / 5040, None, ALU.mult))
            for c in (1 / 720, 1 / 120, 1 / 24, 1 / 6, 0.5, 1.0):
                link(dve.scalar_tensor_tensor(EE[:, :], EE[:, :], c, RR[:, :], ALU.add, ALU.mult))
            link(dve.tensor_scalar(II[:, :], KK[:, :], 127.0, 2.0 ** 23, ALU.add, ALU.mult))
            link(dve.scalar_tensor_tensor(EX[:, :], EE[:, :], 1.0, II[:, :].bitcast(F32), ALU.add, ALU.mult))
            WR = EX[:, 2:]
            for g in range(2):
                s = slice(g * NST, (g + 1) * NST)
                dve.tensor_scalar(DR[:, s], EX[:, 2 + g * NST:2 + (g + 1) * NST], EX[:, g:g + 1], -1.0,
                                  ALU.mult, ALU.mult)
                link(dve.tensor_scalar(DI[:, s], WI[:, s], EX[:, g:g + 1], None, ALU.mult))
            for a in range(NA):
                dve.tensor_scalar(ER[:, a], DR[:, :], float(P * (a + 1)), None, ALU.mult).then_inc(args_ready, 1)
            link(dve.tensor_scalar(TURN[:, :], DI[:, :], 1 / (2 * math.pi), None, ALU.mult))
            link(dve.tensor_scalar(T1[:, 0], TURN[:, :], ROUND, ROUND, ALU.add, ALU.subtract))
            link(dve.tensor_tensor(ANG[:, 0], TURN[:, :], T1[:, 0], ALU.subtract))
            link(dve.tensor_scalar(TURN[:, :], TURN[:, :], 0.5, None, ALU.mult))
            link(dve.tensor_scalar(T1[:, 0], TURN[:, :], ROUND, ROUND, ALU.add, ALU.subtract))
            link(dve.tensor_tensor(ANG[:, 2], TURN[:, :], T1[:, 0], ALU.subtract))
            for a in range(NA):
                last = dve.tensor_scalar(ANG[:, 3 + a], ANG[:, 0], float(P * (a + 1)), None, ALU.mult)
            link(last)
            link(dve.tensor_scalar(T1[:, :], ANG[:, 3:6], ROUND, ROUND, ALU.add, ALU.subtract))
            link(dve.tensor_tensor(ANG[:, 3:6], ANG[:, 3:6], T1[:, :], ALU.subtract))
            dve.tensor_scalar(ANG[:, 1], ANG[:, 0], 0.25, None, ALU.add)
            link(dve.tensor_scalar(ANG[:, 6:9], ANG[:, 3:6], 0.25, None, ALU.add))
            dve.tensor_scalar(T1[:, 0], ANG[:, 1], ROUND, ROUND, ALU.add, ALU.subtract)
            link(dve.tensor_scalar(SN[:, 0:3], ANG[:, 6:9], ROUND, ROUND, ALU.add, ALU.subtract))
            dve.tensor_tensor(ANG[:, 1], ANG[:, 1], T1[:, 0], ALU.subtract).then_inc(args_ready, 1)
            dve.tensor_tensor(ANG[:, 6:9], ANG[:, 6:9], SN[:, 0:3], ALU.subtract).then_inc(args_ready, 1)
            for g in range(2):
                dve.tensor_copy(DUP[:, g], wide(ANG[:, 0, g * NST:(g + 1) * NST][:, :, None], [P, NST, 2])).then_inc(dup_ready, 1)
                dve.tensor_copy(DUP[:, 2 + g], wide(DR[:, g * NST:(g + 1) * NST][:, :, None], [P, NST, 2])).then_inc(dup_ready, 1)
            dve.wait_ge(exps_ready, 1)
            link(dve.tensor_scalar(Q1[:, :], TH[:, :], -1.0, 1.0, ALU.mult, ALU.add))
            link(dve.reciprocal(Q2[:, :], Q1[:, :]))
            link(dve.scalar_tensor_tensor(Q1[:, :], TH[:, :], 2.0, Q2[:, :], ALU.mult, ALU.mult))
            dve.wait_ge(sins_ready, 1)
            link(dve.scalar_tensor_tensor(Q2[:, :], SN[:, 2], -2.0, SN[:, 2], ALU.mult, ALU.mult))
            link(dve.tensor_tensor(NR[:, :], Q1[:, :], SN[:, 1], ALU.mult))
            link(dve.tensor_tensor(NR[:, :], NR[:, :], Q2[:, :], ALU.add))
            link(dve.scalar_tensor_tensor(NI[:, :], Q1[:, :], 1.0, SN[:, 0], ALU.add, ALU.mult))
            link(dve.tensor_tensor(Q1[:, :], WR, WR, ALU.mult))
            link(dve.tensor_tensor(Q2[:, :], WI[:, :], WI[:, :], ALU.mult))
            link(dve.tensor_tensor(Q1[:, :], Q1[:, :], Q2[:, :], ALU.add))
            link(dve.reciprocal(Q2[:, :], Q1[:, :]))
            br = BR[:, :, :].rearrange("p g n -> p (g n)")
            bi = BI[:, :, :].rearrange("p g n -> p (g n)")
            dve.tensor_tensor(T1[:, 0], NI[:, :], WI[:, :], ALU.mult)
            link(dve.tensor_tensor(T1[:, 1], NR[:, :], WR, ALU.mult))
            link(dve.tensor_tensor(T1[:, 0], T1[:, 0], T1[:, 1], ALU.subtract))
            link(dve.scalar_tensor_tensor(br, T1[:, 0], 2.0, Q2[:, :], ALU.mult, ALU.mult))
            dve.tensor_tensor(T1[:, 0], NI[:, :], WR, ALU.mult)
            link(dve.tensor_tensor(T1[:, 1], NR[:, :], WI[:, :], ALU.mult))
            link(dve.tensor_tensor(T1[:, 0], T1[:, 0], T1[:, 1], ALU.add))
            link(dve.scalar_tensor_tensor(bi, T1[:, 0], -2.0, Q2[:, :], ALU.mult, ALU.mult))
            em = ER[:, :, :]
            pr = PR[:, :, :, :].rearrange("p a g n -> p a (g n)")
            pi = PI[:, :, :, :].rearrange("p a g n -> p a (g n)")
            npr = NPR[:, :, :, :].rearrange("p a g n -> p a (g n)")
            link(dve.tensor_tensor(pr, em, SN[:, 6:9], ALU.mult))
            dve.tensor_tensor(pi, em, SN[:, 3:6], ALU.mult)
            link(dve.tensor_scalar(npr, pr, -1.0, None, ALU.mult))
            dve.wait_ge(load_x, 32)
            for g in range(2):
                xr, xi = X[:, g, :, :, 0], X[:, g, :, :, 1]
                b_r, b_i = wide(BR[:, g][:, None, :], [P, B, NST]), wide(BI[:, g][:, None, :], [P, B, NST])
                dve.tensor_tensor(CR[:, g], xr, b_r, ALU.mult)
                dve.tensor_tensor(C1[:, g], xi, b_i, ALU.mult)
                dve.tensor_tensor(CI[:, g], xr, b_i, ALU.mult)
                link(dve.tensor_tensor(C2[:, g], xi, b_r, ALU.mult))
                dve.tensor_tensor(CR[:, g], CR[:, g], C1[:, g], ALU.subtract)
                link(dve.tensor_tensor(CI[:, g], CI[:, g], C2[:, g], ALU.add))
            for g in range(2):
                dve.tensor_copy(UH[:, g, :, 0, :, 0], CR[:, g])
                dve.tensor_scalar(UH[:, g, :, 0, :, 1], CI[:, g], -1.0, None, ALU.mult)
                s = [P, B, NA, NST]
                cr, ci = wide(CR[:, g][:, :, None, :], s), wide(CI[:, g][:, :, None, :], s)
                p_r, p_i, np_r = (wide(t[:, :, g][:, None, :, :], s) for t in (PR, PI, NPR))
                if g:
                    dve.wait_ge(u_ready, 1)
                dve.tensor_tensor(M1[:, :, :, :], cr, p_r, ALU.mult)
                link(dve.tensor_tensor(M2[:, :, :, :], ci, p_i, ALU.mult))
                link(dve.tensor_tensor(UH[:, g, :, 1:, :, 0], M1[:, :, :, :], M2[:, :, :, :], ALU.subtract))
                dve.tensor_tensor(M1[:, :, :, :], ci, np_r, ALU.mult)
                link(dve.tensor_tensor(M2[:, :, :, :], cr, p_i, ALU.mult))
                dve.tensor_tensor(UH[:, g, :, 1:, :, 1], M1[:, :, :, :], M2[:, :, :, :], ALU.subtract).then_inc(u_ready, 1)
            dve.wait_ge(rows_t, 5)
            dve.tensor_copy(m["turn"][:, :], PS[:, 0, 0:NCH]).then_inc(done, 1)
            dve.tensor_copy(m["decay"][:, :], PS[:, 0, NCH:2 * NCH]).then_inc(done, 1)
            dve.tensor_copy(m["quarter"][:, :], PS[:, 1, 0:1]).then_inc(done, 1)
            dve.tensor_scalar(m["phase"][:, :], PS[:, 1, 0:1], TWO_PI, None, ALU.mult).then_inc(done, 1)
            for i in range(0, CH, 2):
                g, c = i // B, i % B
                dve.wait_ge(u_t, i + 1)
                dve.tensor_copy(m["U"][:, g * P:(g + 1) * P, c, :],
                                PS[:, 2 + i % 6, :].rearrange("p (a h) -> p h a", a=DC)).then_inc(copied_v, 1)
            dve.wait_ge(copied_v, CH // 2)
            dve.wait_ge(done, 4)

        @blk.scalar
        def _(act):
            act.wait_ge(args_ready, 3)
            act.activation(TH[:, :], DR[:, :], ACT.Tanh, scale=0.5).then_inc(exps_ready, 1)
            act.activation(ER[:, :, :], ER[:, :, :], ACT.Exp)
            act.wait_ge(args_ready, 5)
            act.activation(SN[:, :, :], ANG[:, :, :], ACT.Sin, scale=TWO_PI).then_inc(sins_ready, 1)
            for i in range(1, CH, 2):
                g, c = i // B, i % B
                act.wait_ge(u_t, i + 1)
                act.copy(m["U"][:, g * P:(g + 1) * P, c, :],
                         PS[:, 2 + i % 6, :].rearrange("p (a h) -> p h a", a=DC)).then_inc(copied_s, 1)
            act.wait_ge(copied_s, CH // 2)

        @blk.tensor
        def _(pe):
            pe.wait_ge(consts, 6)
            pe.wait_ge(dup_ready, 4)
            for i in range(4):
                pe.transpose(PS[:, 0, i * P:(i + 1) * P], DUP[:, i].rearrange("p n r -> p (n r)"), k["ident"][:, :]).then_inc(rows_t, 1)
            pe.transpose(PS[:, 1, 0:P], DUP[:, 4].rearrange("p n r -> p (n r)"), k["ident"][:, :]).then_inc(rows_t, 1)
            for i in range(CH):
                g, c = i // B, i % B
                pe.wait_ge(u_ready, g + 1)
                if i >= 6:
                    pe.wait_ge(copied_s if i % 2 else copied_v, (i - 6) // 2 + 1)
                for a in range(DC):
                    last = pe.transpose(PS[:, 2 + i % 6, a * P:(a + 1) * P],
                                        UH[:, g, c, a].rearrange("p n r -> p (n r)"), k["ident"][:, :])
                last.then_inc(u_t, 1)


def mixer_tokens(nc, k, m):
    CPC = 16
    SLOTS = 8
    HALF = CPC * SLOTS
    PS, HT = k["PS"], k["HT"]
    with ExitStack() as ctx:
        sb = lambda n, s, d=F32: ctx.enter_context(nc.sbuf_tensor(n, s, d))
        sem = signals(nc, ctx)
        Z = sb("z_pow", [P, SLOTS, CPC, P])
        A = sb("z_turn", [P, 2, CPC, P])
        K = sb("z_round", [P, 2, CPC, P])
        decay_arg = sem("z_decay_arg")
        decays = sem("z_decays")
        turns = sem("z_turns")
        turn_chain = sem("z_turn_chain")
        turns_reduced = sem("z_turns_reduced")
        rotations = sem("z_rotations")
        powers = sem("z_powers")
        summed = sem("z_summed")
        stored = sem("z_stored")
        blk = ctx.enter_context(nc.Block())

        @blk.gpsimd
        def _(pool):
            with pool.Fori(0, 2) as hf:
                for j in range(SLOTS):
                    pool.wait_ge(summed, hf * SLOTS + j + 1)
                    s = [P, CPC, P]
                    pool.tensor_tensor(Z[:, j], wide(m["decay"][:, bass.ds(hf * HALF + j * CPC, CPC)][:, :, None], s),
                                       wide(m["iota"][:, None, :], s), ALU.mult).then_inc(decay_arg, 1)

        @blk.scalar
        def _(act):
            with act.Fori(0, 2) as hf:
                for j in range(SLOTS):
                    act.wait_ge(decay_arg, hf * SLOTS + j + 1)
                    act.activation(Z[:, j], Z[:, j], ACT.Exp).then_inc(decays, 1)
                for j in range(SLOTS):
                    act.wait_ge(turns_reduced, hf * SLOTS + j + 1)
                    act.activation(A[:, j % 2], A[:, j % 2], ACT.Sin, bias=m["phase"][:, 0:1],
                                   scale=-TWO_PI).then_inc(rotations, 1)

        @blk.vector
        def _(dve):
            with dve.Fori(0, 2) as hf:
                def multiply(j):
                    dve.wait_ge(decays, hf * SLOTS + j + 1)
                    dve.wait_ge(rotations, hf * SLOTS + j + 1)
                    dve.tensor_tensor(Z[:, j], Z[:, j], A[:, j % 2], ALU.mult).then_inc(powers, 1)

                def store(j):
                    dve.wait_ge(summed, hf * SLOTS + SLOTS + j + 1)
                    h0 = hf * HALF + j * CPC
                    dst = HT[:, :, 0:TR].rearrange("p a (c h) -> p c a h", c=B)[:, :, :, bass.ds(h0, CPC)]
                    dve.tensor_copy(dst, PS[:, j % 4].rearrange("p (h c a) -> p c a h", c=B, a=DC)).then_inc(stored, 1)

                for j in range(SLOTS + 2):
                    if j < SLOTS:
                        dve.wait_ge(powers, hf * SLOTS + j + 1)
                        s = [P, CPC, P]
                        n = hf * 2 * SLOTS + 2 * j
                        dve.tensor_tensor(A[:, j % 2], wide(m["turn"][:, bass.ds(hf * HALF + j * CPC, CPC)][:, :, None], s),
                                          wide(m["iota"][:, None, :], s), ALU.mult).then_inc(turn_chain, 1)
                        dve.wait_ge(turn_chain, n + 1)
                        dve.tensor_scalar(K[:, j % 2], A[:, j % 2], m["quarter"][:, 0:1], ROUND, ALU.add, ALU.add).then_inc(turn_chain, 1)
                        dve.wait_ge(turn_chain, n + 2)
                        dve.scalar_tensor_tensor(A[:, j % 2].rearrange("p h b -> p (h b)"), K[:, j % 2].rearrange("p h b -> p (h b)"), ROUND,
                                                 A[:, j % 2].rearrange("p h b -> p (h b)"), ALU.subtract, ALU.subtract).then_inc(turns_reduced, 1)
                    if 1 <= j <= SLOTS:
                        multiply(j - 1)
                    if j >= 2:
                        store(j - 2)
            dve.wait_ge(stored, 2 * SLOTS + 4)

        @blk.tensor
        def _(pe):
            pe.sem_inc(summed, SLOTS)
            pe.sem_inc(stored, 4)
            pe.sem_inc(powers, 2)
            with pe.Fori(0, 2) as hf:
                for j in range(SLOTS):
                    pe.wait_ge(powers, hf * SLOTS + 2 + j + 1)
                    pe.wait_ge(stored, hf * SLOTS + j + 1)
                    for i in range(CPC):
                        last = pe.matmul(PS[:, j % 4, i * 32:(i + 1) * 32], Z[:, j, i],
                                         m["U"][:, hf * HALF + j * CPC + i].rearrange("p c a -> p (c a)"),
                                         start=True, stop=True)
                    last.then_inc(summed, 1)


def split_product(pe, out, terms):
    n = 0
    for w_hi, w_lo, x_hi, x_lo in terms:
        for w, v in ((w_hi, x_hi), (w_hi, x_lo), (w_lo, x_hi)):
            n += 1
            last = pe.matmul(out, w, v, start=n == 1, stop=n == 3 * len(terms))
    return last


def layernorm(nc, k, groups, XH, XL, tag, base=0, cls_copy=None):
    HT, PS = k["HT"], k["PS"]
    NGR = len(groups)
    with ExitStack() as ctx:
        sb = lambda n, s, d=F32: ctx.enter_context(nc.sbuf_tensor(tag + n, s, d))
        sem = signals(nc, ctx, tag)
        XC = sb("n_centred", [P, 2, DC, GRP])
        SQ = sb("n_squares", [P, 2, DC, GRP])
        VE = sb("n_var", [P, 2, GRP])
        RS = sb("n_rstd", [P, 2, GRP])
        RT = sb("n_newton", [P, 2, GRP])
        means = sem("n_means")
        centred = sem("n_centred_ready")
        squares = sem("n_squares_ready")
        variances = sem("n_variances")
        var_eps = sem("n_var_eps")
        guess = sem("n_guess")
        guess_sq = sem("n_guess_sq")
        dve_chain = sem("n_dve_chain")
        act_chain = sem("n_act_chain")
        normed = sem("n_normed")
        highs = sem("n_highs")
        lows = sem("n_lows")
        blk = ctx.enter_context(nc.Block())

        @blk.tensor
        def _(pe):
            for j in range(NGR + 1):
                if j < NGR:
                    c0, n = groups[j]
                    if j >= 2:
                        pe.wait_ge(centred, j - 1)
                    for a in range(DC):
                        last = pe.matmul(PS[:, j % 2, 0:n], k["mean_w"][:, :], HT[:, a, c0:c0 + n],
                                         start=a == 0, stop=a == DC - 1)
                    last.then_inc(means, 1)
                if j >= 1:
                    i = j - 1
                    n = groups[i][1]
                    pe.wait_ge(squares, i + 1)
                    if i >= 2:
                        pe.wait_ge(var_eps, i - 1)
                    for a in range(DC):
                        last = pe.matmul(PS[:, 2 + i % 2, 0:n], k["mean_w"][:, :], SQ[:, i % 2, a, 0:n],
                                         start=a == 0, stop=a == DC - 1)
                    last.then_inc(variances, 1)

        @blk.vector
        def _(dve):
            link = Chain(dve, dve_chain).link

            def centre(j):
                c0, n = groups[j]
                dve.wait_ge(means, j + 1)
                if j >= 2:
                    dve.wait_ge(lows, j - 1)
                dve.tensor_tensor(XC[:, j % 2, :, 0:n], HT[:, :, c0:c0 + n],
                                  wide(PS[:, j % 2, 0:n][:, None, :], [P, DC, n]), ALU.subtract).then_inc(centred, 1)

            def scale(j):
                c0, n = groups[j]
                ve, rs, rt = VE[:, j % 2, 0:n], RS[:, j % 2, 0:n], RT[:, j % 2, 0:n]
                dve.wait_ge(variances, j + 1)
                dve.tensor_scalar(ve, PS[:, 2 + j % 2, 0:n], EPS, None, ALU.add).then_inc(var_eps, 1)
                dve.wait_ge(guess_sq, j + 1)
                link(dve.tensor_tensor(rt, rt, ve, ALU.mult))
                link(dve.tensor_scalar(rt, rt, -0.5, 1.5, ALU.mult, ALU.add))
                link(dve.tensor_tensor(rs, rs, rt, ALU.mult))
                dve.tensor_tensor(XC[:, j % 2, :, 0:n], XC[:, j % 2, :, 0:n], wide(rs[:, None, :], [P, DC, n]),
                                  ALU.mult).then_inc(normed, 1)
                if c0 == TR and cls_copy is not None:
                    dve.wait_ge(normed, j + 1)
                    link(dve.tensor_copy(cls_copy, wide(XC[:, j % 2, :, 0:1], [P, DC, P])))

            for j in range(NGR + 1):
                if j < NGR:
                    centre(j)
                if j >= 1:
                    scale(j - 1)

        @blk.scalar
        def _(act):
            def high(j):
                c0, n = groups[j]
                act.wait_ge(normed, j + 1)
                act.copy(XH[:, :, c0 - base:c0 - base + n], XC[:, j % 2, :, 0:n]).then_inc(highs, 1)

            for j in range(NGR):
                n = groups[j][1]
                ve, rs, rt = VE[:, j % 2, 0:n], RS[:, j % 2, 0:n], RT[:, j % 2, 0:n]
                act.wait_ge(centred, j + 1)
                if j >= 2:
                    act.wait_ge(variances, j - 1)
                act.activation(SQ[:, j % 2, :, 0:n], XC[:, j % 2, :, 0:n], ACT.Square).then_inc(squares, 1)
                if j >= 1:
                    high(j - 1)
                act.wait_ge(var_eps, j + 1)
                act.activation(rs, ve, ACT.Ln).then_inc(act_chain, 1)
                act.wait_ge(act_chain, 2 * j + 1)
                act.activation(rs, rs, ACT.Exp, scale=-0.5).then_inc(act_chain, 1)
                act.wait_ge(act_chain, 2 * j + 2)
                act.activation(rt, rs, ACT.Square).then_inc(guess_sq, 1)
            high(NGR - 1)

        @blk.gpsimd
        def _(pool):
            for j in range(NGR):
                c0, n = groups[j]
                pool.wait_ge(highs, j + 1)
                pool.tensor_tensor(XL[:, :, c0 - base:c0 - base + n], XC[:, j % 2, :, 0:n],
                                   XH[:, :, c0 - base:c0 - base + n].bitcast(F32), ALU.subtract).then_inc(lows, 1)
            pool.wait_ge(lows, NGR)


def class_rows(nc, w_qkv, k, XB):
    XH, XL, PS = k["XH"], k["XL"], k["PS"]
    HD = HEADS * DH
    with ExitStack() as ctx:
        sb = lambda n, s, d=F32: ctx.enter_context(nc.sbuf_tensor(n, s, d))
        sem = signals(nc, ctx)
        WQ = sb("c_wq", [P, DC, HD])
        WK = sb("c_wk", [P, DC, HD])
        UQ = sb("c_u", [P, DC, P])
        UQH = sb("c_uh", [P, DC, P], F32R)
        UQL = sb("c_ul", [P, DC, P], F32R)
        SC = sb("c_scores", [P, B, NCH + 2])
        MX = sb("c_max", [P, B])
        RC = sb("c_sum", [P, B])
        load_q, load_k = sem("c_load_q"), sem("c_load_k")
        q_ready = sem("c_q_ready")
        dve_chain = sem("c_dve_chain")
        u_high = sem("c_u_high")
        u_ready = sem("c_u_ready")
        scored = sem("c_scored")
        scores_in = sem("c_scores_in")
        shifted = sem("c_shifted")
        exps = sem("c_exps")
        probs = sem("c_probs")
        highs = sem("c_highs")
        lows = sem("c_lows")
        blk = ctx.enter_context(nc.Block())

        @blk.sync
        def _(sp):
            sp.dma_start(WQ[:, :, :], w_qkv[:, 0:HD].rearrange("(a p) n -> p a n", p=P)).then_inc(load_q, 16)
            sp.dma_start(WK[:, :, :], w_qkv[:, HD:2 * HD].rearrange("(a p) n -> p a n", p=P)).then_inc(load_k, 16)

        @blk.tensor
        def _(pe):
            pe.wait_ge(load_q, 16)
            for n in range(DC):
                for a in range(DC):
                    last = pe.matmul(PS[:, 4 + n], XB[:, a], WQ[:, a, n * GRP:(n + 1) * GRP], start=a == 0, stop=a == DC - 1)
            last.then_inc(q_ready, 1)
            pe.wait_ge(u_ready, 1)
            for j, (c0, n) in enumerate(GROUPS):
                if j >= 4:
                    pe.wait_ge(scores_in, j - 3)
                split_product(pe, PS[:, j % 4, 0:n], [(UQH[:, a], UQL[:, a], XH[:, a, c0:c0 + n], XL[:, a, c0:c0 + n])
                                                      for a in range(DC)]).then_inc(scored, 1)

        @blk.vector
        def _(dve):
            link = Chain(dve, dve_chain).link
            link(dve.memset(UQ[:, :, :], 0.0))
            dve.wait_ge(q_ready, 1)
            dve.wait_ge(load_k, 16)
            for a in range(DC):
                link(dve.tensor_tensor(WK[:, a], WK[:, a], PS[:, 4:8].rearrange("p b n -> p (b n)"), ALU.mult))
                link(dve.reduce_sum(UQ[:, a, 0:HEADS], WK[:, a].rearrange("p (h d) -> p h d", h=HEADS), AX.X))
            link(dve.tensor_copy(UQH[:, :, :], UQ[:, :, :]))
            dve.tensor_tensor(UQL[:, :, :], UQ[:, :, :], UQH[:, :, :].bitcast(F32), ALU.subtract).then_inc(u_ready, 1)
            dve.wait_ge(scores_in, NG + 1)
            link(dve.reduce_max(MX[:, :], SC[:, :, 0:NCH + 1], AX.X))
            dve.tensor_tensor(SC[:, :, 0:NCH + 1], SC[:, :, 0:NCH + 1], wide(MX[:, :, None], [P, B, NCH + 1]),
                              ALU.subtract).then_inc(shifted, 1)
            dve.wait_ge(exps, 1)
            link(dve.reduce_sum(RC[:, :], SC[:, :, 0:NCH + 1], AX.X))
            link(dve.reciprocal(MX[:, :], RC[:, :]))
            dve.tensor_tensor(SC[:, :, :], SC[:, :, :], wide(MX[:, :, None], [P, B, NCH + 2]), ALU.mult).then_inc(probs, 1)
            dve.wait_ge(highs, 1)
            dve.tensor_tensor(k["PCL"][:, :, :], SC[:, :, :], k["PCH"][:, :, :].bitcast(F32), ALU.subtract).then_inc(lows, 1)
            dve.wait_ge(lows, 1)

        @blk.scalar
        def _(act):
            for j, (c0, n) in enumerate(GROUPS):
                act.wait_ge(scored, j + 1)
                if n == GRP:
                    act.copy(SC[:, 2 * j:2 * j + 2, 0:NCH], PS[:, j % 4].rearrange("p (b n) -> p b n", b=2)).then_inc(scores_in, 1)
                else:
                    act.copy(SC[:, :, NCH:NCH + 2], wide(PS[:, j % 4, 0:n][:, :, None], [P, B, 2])).then_inc(scores_in, 1)
            act.wait_ge(shifted, 1)
            act.activation(SC[:, :, 0:NCH + 1], SC[:, :, 0:NCH + 1], ACT.Exp, scale=SCALE).then_inc(exps, 1)
            act.wait_ge(probs, 1)
            act.copy(k["PCH"][:, :, :], SC[:, :, :]).then_inc(highs, 1)
            act.wait_ge(highs, 1)


def attention(nc, w_qkv, w_o, k):
    HT, XH, XL, PS = k["HT"], k["XH"], k["XL"], k["PS"]
    HD = HEADS * DH
    R = NCH + 2
    UNITS = 2 * NG
    ROUNDS = HEADS // 2
    OUTS = DC * (NG + 1)
    QB, KB, VB, CB, SB = 0, 1, 2, 3, 4
    PARTS = [(1, 0), (1, 1), (1, 2), (0, 3), (1, 3), (0, 0), (0, 1), (0, 2)]
    FIRST = [(0, 0), (0, 1), (0, 2)]
    NP, NF = len(PARTS), len(FIRST)
    PREP = {0: [0, 1], 1: [2, 3], 2: [4], 4: [5], 5: [6], 6: [7]}
    with ExitStack() as ctx:
        sb = lambda n, s, d=F32: ctx.enter_context(nc.sbuf_tensor(n, s, d))
        sem = signals(nc, ctx)
        RAW = sb("t_wraw", [P, 2, D])
        WH = sb("t_wh", [P, 2, 4, D], F32R)
        WL = sb("t_wl", [P, 2, 4, D], F32R)
        QH = sb("t_qh", [P, GRP], F32R)
        QL = sb("t_ql", [P, GRP], F32R)
        KH = sb("t_kh", [P, 2, R], F32R)
        KL = sb("t_kl", [P, 2, R], F32R)
        KVC = sb("t_kvc", [P, 2, 4])
        VS = sb("t_v", [P, 2, 2, NCH])
        E = sb("t_e", [P, 4, R])
        EPH = sb("t_eph", [P, 2, R], F32R)
        EPL = sb("t_epl", [P, 2, R], F32R)
        VT = sb("t_vt", [P, 2, NCH + 1])
        VTH = sb("t_vth", [P, 2, B, R], F32R)
        VTL = sb("t_vtl", [P, 2, B, R], F32R)
        SEL = sb("t_sel", [P, 2, P], F32R)
        ONES = sb("t_ones", [P, P], F32R)
        MX = sb("t_max", [P, 4])
        NB = sb("t_bias", [P, 4])
        RS = sb("t_rowsum", [P, 4])
        RC = sb("t_rowinv", [P, 4])
        loads = [sem("t_load0"), sem("t_load1")]
        wh, wl = sem("t_wh_ready"), sem("t_wl_ready")
        setup = sem("t_setup")
        sel_ready = sem("t_sel_ready")
        kvc_done, kvc_in = sem("t_kvc_done"), sem("t_kvc_in")
        q_done, k_done, v_done = sem("t_q_done"), sem("t_k_done"), sem("t_v_done")
        qh, ql, kh, kl, vs = sem("t_qh_ready"), sem("t_ql_ready"), sem("t_kh_ready"), sem("t_kl_ready"), sem("t_v_in")
        s_done, maxed, nmax, exps = sem("t_s_done"), sem("t_maxed"), sem("t_bias_ready"), sem("t_exps")
        inv, scaled, ep, eph, epl = sem("t_inv"), sem("t_scaled"), sem("t_ep"), sem("t_eph_ready"), sem("t_epl_ready")
        c_done, vt, vth, vtl = sem("t_c_done"), sem("t_vt_ready"), sem("t_vth_ready"), sem("t_vtl_ready")
        wo_done, hadd = sem("t_wo_done"), sem("t_hadd")
        blk = ctx.enter_context(nc.Block())

        def source(part, head):
            if part < 3:
                return w_qkv[:, bass.ds(head * DH + part * HD, DH)].rearrange("(a p) n -> p a n", p=P)
            return w_o[bass.ds(head * DH, DH), :]

        def raw(slot, part):
            return RAW[:, slot].rearrange("p (a n) -> p a n", a=DC) if part < 3 else RAW[:, slot]

        @blk.sync
        def _(sp):
            for x, (s, part) in enumerate(FIRST):
                if x >= 2:
                    sp.wait_ge(wl, x - 1)
                sp.dma_start(raw(x % 2, part), source(part, 0)).then_inc(loads[x % 2], 16)
            with sp.Fori(0, ROUNDS) as i:
                for x, (s, part) in enumerate(PARTS):
                    slot = (NF + x) % 2
                    head = (2 * i + 2) % HEADS if x >= NP - NF else 2 * i + s
                    sp.wait_ge(wl, i * NP + NF + x - 1)
                    sp.dma_start(raw(slot, part), source(part, head)).then_inc(loads[slot], 16)

        def loaded(eng, i, x):
            if i is None:
                eng.wait_ge(loads[x % 2], 16 * (x // 2 + 1))
            else:
                slot = (NF + x) % 2
                eng.wait_ge(loads[slot], i * 16 * NP // 2 + 16 * ((NF + x) // 2 + 1))

        def slot_free(eng, i, x):
            if x < 3:
                eng.wait_ge(v_done, i * UNITS)
            elif x < 5:
                eng.wait_ge(wo_done, i * OUTS)
            else:
                eng.wait_ge(v_done, i * UNITS + NG)

        @blk.gpsimd
        def _(pool):
            def low(i, x, s, part):
                if i is None:
                    pool.wait_ge(wh, x + 1)
                    slot = x % 2
                else:
                    pool.wait_ge(wh, i * NP + NF + x + 1)
                    slot_free(pool, i, x)
                    slot = (NF + x) % 2
                pool.tensor_tensor(WL[:, s, part], RAW[:, slot], WH[:, s, part].bitcast(F32), ALU.subtract).then_inc(wl, 1)

            pool.memset(ONES[:, :].bitcast(F32), 1.0).then_inc(setup, 1)
            pool.memset(E[:, :, R - 1:R], 0.0).then_inc(setup, 1)
            for x, (s, part) in enumerate(FIRST):
                low(None, x, s, part)
            with pool.Fori(0, ROUNDS) as i:
                def value_low(u, b):
                    s, g = u // NG, u % NG
                    n = i * 2 * UNITS + 2 * u + b
                    pool.wait_ge(vth, n + 1)
                    pool.wait_ge(wo_done, i * OUTS)
                    pool.tensor_tensor(VTL[:, s, 2 * g + b, 0:NCH + 1], VT[:, b], VTH[:, s, 2 * g + b, 0:NCH + 1].bitcast(F32),
                                       ALU.subtract).then_inc(vtl, 1)

                pool.wait_ge(c_done, i * 2 * UNITS + 2)
                for s in range(2):
                    pool.tensor_copy(SEL[:, s], wide(k["ident"][:, bass.ds(2 * i + s, 1)], [P, P])).then_inc(sel_ready, 1)
                for u in range(UNITS + 1):
                    for x in PREP.get(u, []):
                        low(i, x, *PARTS[x])
                    if u >= 1:
                        value_low(u - 1, 0)
                        value_low(u - 1, 1)

        @blk.scalar
        def _(act):
            def high(i, x, s, part):
                loaded(act, i, x)
                if i is not None:
                    slot_free(act, i, x)
                slot = x % 2 if i is None else (NF + x) % 2
                act.copy(WH[:, s, part], RAW[:, slot]).then_inc(wh, 1)

            act.wait_ge(setup, 2)
            for x, (s, part) in enumerate(FIRST):
                high(None, x, s, part)
            with act.Fori(0, ROUNDS) as i:
                def value_high(u, b):
                    s, g = u // NG, u % NG
                    act.wait_ge(vt, i * 2 * UNITS + 2 * u + b + 1)
                    act.wait_ge(wo_done, i * OUTS)
                    act.copy(VTH[:, s, 2 * g + b, 0:NCH + 1], VT[:, b]).then_inc(vth, 1)

                for u in range(UNITS):
                    n = i * UNITS + u
                    for x in PREP.get(u, []):
                        high(i, x, *PARTS[x])
                    act.wait_ge(q_done, n + 1)
                    act.wait_ge(s_done, 4 * n)
                    act.copy(QH[:, :], PS[:, QB]).then_inc(qh, 1)
                    if u % NG == 0:
                        act.wait_ge(kvc_done, i * 2 + u // NG + 1)
                        act.copy(KVC[:, u // NG], PS[:, KB, 0:4]).then_inc(kvc_in, 1)
                        act.wait_ge(kvc_in, i * 2 + u // NG + 1)
                        act.copy(KH[:, :, NCH:R], wide(KVC[:, u // NG, 0:1][:, :, None], [P, 2, 2]))
                    act.wait_ge(k_done, n + 1)
                    act.copy(KH[:, :, 0:NCH], PS[:, KB].rearrange("p (b n) -> p b n", b=2)).then_inc(kh, 1)
                    if u >= 1:
                        value_high(u - 1, 0)
                    act.wait_ge(v_done, n + 1)
                    act.copy(VS[:, u % 2], PS[:, VB].rearrange("p (b n) -> p b n", b=2)).then_inc(vs, 1)
                    if u >= 1:
                        value_high(u - 1, 1)

                    def exp(t):
                        act.wait_ge(nmax, 4 * n + t + 1)
                        act.wait_ge(epl, 2 * n)
                        act.activation(E[:, t, 0:NCH + 1], PS[:, SB + t, 0:NCH + 1], ACT.Exp, bias=NB[:, t:t + 1],
                                       scale=SCALE, accum_out=RS[:, t:t + 1]).then_inc(exps, 1)

                    def high_probs(b):
                        act.wait_ge(ep, 2 * n + b + 1)
                        act.wait_ge(c_done, 2 * n + b + 1)
                        act.copy(EPH[:, b], E[:, 2 * b]).then_inc(eph, 1)

                    exp(0), exp(1), exp(2), high_probs(0), exp(3), high_probs(1)
                value_high(UNITS - 1, 0)
                value_high(UNITS - 1, 1)

        @blk.vector
        def _(dve):
            with dve.Fori(0, ROUNDS) as i:
                def values(u, b):
                    n = i * 2 * UNITS + 2 * u + b
                    dve.wait_ge(c_done, n + 3)
                    dve.wait_ge(vs, i * UNITS + u + 1)
                    dve.wait_ge(vtl, n + 1)
                    dve.tensor_tensor(VT[:, b, 0:NCH], VS[:, u % 2, b], PS[:, CB, 0:NCH], ALU.mult)
                    dve.tensor_tensor(VT[:, b, NCH:NCH + 1], KVC[:, u // NG, 2:3], PS[:, CB, NCH:NCH + 1], ALU.mult).then_inc(vt, 1)

                def add_output(j):
                    g, f = j // DC, j % DC
                    c0, n = GROUPS[g]
                    dve.wait_ge(wo_done, i * OUTS + j + 1)
                    dve.tensor_tensor(HT[:, f, c0:c0 + n], HT[:, f, c0:c0 + n], PS[:, j % 2, 0:n], ALU.add).then_inc(hadd, 1)

                for u in range(UNITS):
                    n = i * UNITS + u
                    dve.wait_ge(qh, n + 1)
                    dve.wait_ge(s_done, 4 * n)
                    dve.tensor_tensor(QL[:, :], PS[:, QB], QH[:, :].bitcast(F32), ALU.subtract).then_inc(ql, 1)
                    dve.wait_ge(kh, n + 1)
                    if u % NG == 0:
                        dve.tensor_tensor(KL[:, :, NCH:R], wide(KVC[:, u // NG, 0:1][:, :, None], [P, 2, 2]), KH[:, :, NCH:R].bitcast(F32), ALU.subtract)
                    dve.tensor_tensor(KL[:, :, 0:NCH], PS[:, KB].rearrange("p (b n) -> p b n", b=2),
                                      KH[:, :, 0:NCH].bitcast(F32), ALU.subtract).then_inc(kl, 1)
                    if u >= 1:
                        values(u - 1, 0)
                        values(u - 1, 1)

                    def row_max(t):
                        dve.wait_ge(s_done, 4 * n + t + 1)
                        dve.reduce_max(MX[:, t:t + 1], PS[:, SB + t, 0:NCH + 1], AX.X).then_inc(maxed, 1)
                        dve.wait_ge(maxed, 4 * n + t + 1)
                        dve.tensor_scalar(NB[:, t:t + 1], MX[:, t:t + 1], -SCALE, None, ALU.mult).then_inc(nmax, 1)

                    def merge(b):
                        dve.wait_ge(exps, 4 * n + 2 * b + 2 + 4)
                        dve.reciprocal(RC[:, 2 * b:2 * b + 2], RS[:, 2 * b:2 * b + 2]).then_inc(inv, 1)
                        dve.wait_ge(inv, 2 * n + b + 1)
                        dve.tensor_scalar(E[:, 2 * b], E[:, 2 * b], RC[:, 2 * b:2 * b + 1], None, ALU.mult).then_inc(scaled, 1)
                        dve.wait_ge(scaled, 2 * n + b + 1)
                        dve.scalar_tensor_tensor(E[:, 2 * b], E[:, 2 * b + 1], RC[:, 2 * b + 1:2 * b + 2], E[:, 2 * b],
                                                 ALU.mult, ALU.add).then_inc(ep, 1)

                    def low_probs(b):
                        dve.wait_ge(eph, 2 * n + b + 1)
                        dve.tensor_tensor(EPL[:, b], E[:, 2 * b], EPH[:, b].bitcast(F32), ALU.subtract).then_inc(epl, 1)

                    row_max(0), row_max(1), row_max(2), merge(0), row_max(3), low_probs(0), merge(1), low_probs(1)
                for j in range(DC * (NG - 1)):
                    add_output(j)
                values(UNITS - 1, 0)
                values(UNITS - 1, 1)
                for j in range(DC * (NG - 1), OUTS):
                    add_output(j)
            dve.wait_ge(hadd, ROUNDS * OUTS)

        @blk.tensor
        def _(pe):
            pe.sem_inc(exps, 4)
            pe.sem_inc(c_done, 2)
            pe.sem_inc(vtl, 2)
            pe.wait_ge(setup, 2)
            with pe.Fori(0, ROUNDS) as i:
                def project(u, part, bank, done):
                    s, g = u // NG, u % NG
                    c = slice(g * GRP, (g + 1) * GRP)
                    split_product(pe, PS[:, bank], [(WH[:, s, part, a * P:(a + 1) * P], WL[:, s, part, a * P:(a + 1) * P],
                                                     XH[:, a, c], XL[:, a, c]) for a in range(DC)]).then_inc(done, 1)

                def column_sums(u, b):
                    s, g = u // NG, u % NG
                    n = i * 2 * UNITS + 2 * u + b
                    pe.wait_ge(epl, n + 1)
                    pe.wait_ge(sel_ready, i * 2 + s + 1)
                    pe.wait_ge(vt, n)
                    out = PS[:, CB, 0:R]
                    pe.matmul(out, ONES[:, :], EPH[:, b], start=True, stop=False)
                    pe.matmul(out, ONES[:, :], EPL[:, b], start=False, stop=False)
                    pe.matmul(out, SEL[:, s], k["PCH"][:, 2 * g + b], start=False, stop=False)
                    pe.matmul(out, SEL[:, s], k["PCL"][:, 2 * g + b], start=False, stop=True).then_inc(c_done, 1)

                def output(j):
                    g, f = j // DC, j % DC
                    c0, n = GROUPS[g]
                    last_unit = UNITS - 1 if g >= NG - 1 else NG + g
                    pe.wait_ge(vtl, i * 2 * UNITS + 2 * (last_unit + 1) + 2)
                    if j >= 2:
                        pe.wait_ge(hadd, i * OUTS + j - 1)
                    v = [(t[:, s, 2 * g:2 * g + 2, 0:NCH] if n == GRP else t[:, s, :, NCH]) for s in range(2) for t in (VTH, VTL)]
                    fs = slice(f * P, (f + 1) * P)
                    split_product(pe, PS[:, j % 2, 0:n], [(WH[:, s, 3, fs], WL[:, s, 3, fs], v[2 * s], v[2 * s + 1])
                                                          for s in range(2)]).then_inc(wo_done, 1)

                for u in range(UNITS):
                    n = i * UNITS + u
                    s = u // NG
                    if u % NG == 0:
                        pe.wait_ge(wl, i * NP + (NF if s == 0 else NF + 3))
                        pe.wait_ge(kl, n)
                        if u == 0:
                            pe.wait_ge(hadd, i * OUTS)
                        c = slice(TR, TR + 2)
                        for part in (1, 2):
                            last = split_product(pe, PS[:, KB, 2 * (part - 1):2 * part],
                                                 [(WH[:, s, part, a * P:(a + 1) * P], WL[:, s, part, a * P:(a + 1) * P],
                                                   XH[:, a, c], XL[:, a, c]) for a in range(DC)])
                        last.then_inc(kvc_done, 1)
                    pe.wait_ge(ql, n)
                    project(u, 0, QB, q_done)
                    pe.wait_ge(kl, n)
                    if u % NG == 0:
                        pe.wait_ge(kvc_in, i * 2 + s + 1)
                    project(u, 1, KB, k_done)
                    if u >= 1:
                        column_sums(u - 1, 0)
                    pe.wait_ge(vs, n)
                    project(u, 2, VB, v_done)
                    if u >= 1:
                        column_sums(u - 1, 1)
                    pe.wait_ge(ql, n + 1)
                    pe.wait_ge(kl, n + 1)
                    for t in range(4):
                        b = t // 2
                        pe.wait_ge(exps, 4 * n + t + 1)
                        split_product(pe, PS[:, SB + t, 0:R], [(QH[:, t * P:(t + 1) * P], QL[:, t * P:(t + 1) * P],
                                                                KH[:, b], KL[:, b])]).then_inc(s_done, 1)
                pe.wait_ge(wl, i * NP + NF + 5)
                pe.wait_ge(kl, (i + 1) * UNITS)
                for j in range(DC * (NG - 1)):
                    output(j)
                column_sums(UNITS - 1, 0)
                column_sums(UNITS - 1, 1)
                for j in range(DC * (NG - 1), OUTS):
                    output(j)


KH_ = 4
NK = 128
TOPK = 8
EXPERTS = 4096
ROWS_IN = EXPERTS // NK
EC = 512
CHUNKS = EXPERTS // EC
RPC = EC // NK


def key_scores(nc, w_q, keys, k, e, groups, base, tag):
    PS, XH, XL = k["PS"], e["XH"], e["XL"]
    tiles = [(g, t) for g, (c0, n) in enumerate(groups) for t in range(max(1, n // P))]
    rows = [min(P, groups[g][1]) for g, t in tiles]
    NGR = len(groups)
    with ExitStack() as ctx:
        sb = lambda n, s, d=F32: ctx.enter_context(nc.sbuf_tensor(tag + n, s, d))
        sem = signals(nc, ctx, tag)
        WR = sb("s_wraw", [P, DC, D])
        WH = sb("s_wh", [P, DC, D], F32R)
        WL = sb("s_wl", [P, DC, D], F32R)
        KR = sb("s_keys", [P, KH_, 2, NST])
        KT = sb("s_keys_t", [P, KH_, 2, NK])
        QF = sb("s_q", [P, 2, KH_, GRP])
        SF = sb("s_first", [P, 2, KH_, NK])
        TOP = sb("s_top", [P, 2, KH_, 2, TOPK])
        IDX = sb("s_index", [P, 2, KH_, TOPK], U32)
        BEYOND = sb("s_beyond", [P, 2, KH_, TOPK])
        CAND = sb("s_pairs", [P, KH_, TOPK, TOPK])
        CHOSEN = sb("s_chosen", [P, KH_, TOPK, TOPK])
        BEST = sb("s_best", [P, KH_, TOPK])
        load_w, load_k = sem("s_load_w"), sem("s_load_k")
        zeroed = sem("s_zeroed")
        w_high, w_low = sem("s_w_high"), sem("s_w_low")
        keys_t, keys_in = sem("s_keys_t_done"), sem("s_keys_in")
        q_done, q_in = sem("s_q_done"), sem("s_q_in")
        sims, sims_in, sims_read = sem("s_sims"), sem("s_sims_in"), sem("s_sims_read")
        dve_chain = sem("s_dve_chain")
        blk = ctx.enter_context(nc.Block())

        @blk.sync
        def _(sp):
            sp.dma_start(KR[:, :, :, :], keys.rearrange("h k j d -> k h j d")).then_inc(load_k, 16)
            sp.dma_start(WR[:, :, :], w_q.rearrange("(a p) n -> p a n", p=P)).then_inc(load_w, 16)

        @blk.gpsimd
        def _(pool):
            pool.memset(KT[:, :, :, :], 0.0).then_inc(zeroed, 1)
            pool.memset(e["EXT"][:, :, :], 0.0).then_inc(zeroed, 1)
            pool.memset(e["S1"][:, :, :, ROWS_IN:], 0.0).then_inc(zeroed, 1)
            pool.wait_ge(w_high, 1)
            pool.tensor_tensor(WL[:, :, :], WR[:, :, :], WH[:, :, :].bitcast(F32), ALU.subtract).then_inc(w_low, 1)
            pool.wait_ge(w_low, 1)

        @blk.tensor
        def _(pe):
            pe.wait_ge(load_k, 16)
            for h in range(KH_):
                last = pe.transpose(PS[:, 4, h * P:(h + 1) * P], KR[:, h].rearrange("p j d -> p (j d)"), k["ident"][:, :])
            last.then_inc(keys_t, 1)
            pe.wait_ge(w_low, 1)
            pe.wait_ge(keys_in, 2)
            for g, (c0, n) in enumerate(groups):
                for h in range(KH_):
                    if g:
                        pe.wait_ge(q_in, (g - 1) * KH_ + h + 1)
                    split_product(pe, PS[:, h, 0:n], [(WH[:, a, h * P:(h + 1) * P], WL[:, a, h * P:(h + 1) * P],
                                                       XH[:, a, c0 - base:c0 - base + n], XL[:, a, c0 - base:c0 - base + n])
                                                      for a in range(DC)]).then_inc(q_done, 1)
                pe.wait_ge(q_in, (g + 1) * KH_)
                for y, (gt, t) in enumerate(tiles):
                    if gt != g:
                        continue
                    if y >= 2:
                        pe.wait_ge(sims_in, y - 1)
                    for h in range(KH_):
                        last = pe.matmul(PS[0:rows[y], 4 + 2 * (y % 2) + h // 2, (h % 2) * 2 * NK:(h % 2 + 1) * 2 * NK],
                                         QF[:, g % 2, h, t * P:t * P + rows[y]], KT[:, h].rearrange("p j k -> p (j k)"),
                                         start=True, stop=True)
                    last.then_inc(sims, 1)

        def sim_rows(y):
            b = 4 + 2 * (y % 2)
            return PS[0:rows[y], b:b + 2].rearrange("p b (h j k) -> p (b h) j k", h=2, j=2)

        @blk.scalar
        def _(act):
            act.wait_ge(load_w, 16)
            act.copy(WH[:, :, :], WR[:, :, :]).then_inc(w_high, 1)

            def queries(g):
                n = groups[g][1]
                for h in range(KH_):
                    act.wait_ge(q_done, g * KH_ + h + 1)
                    act.copy(QF[:, g % 2, h, 0:n], PS[:, h, 0:n]).then_inc(q_in, 1)

            for g in range(NGR):
                queries(g)
                for y, (gt, t) in enumerate(tiles):
                    if gt == g:
                        act.wait_ge(sims, y + 1)
                        r = rows[y]
                        if y >= 2:
                            act.wait_ge(sims_read, y - 1)
                        act.copy(SF[0:r, y % 2], sim_rows(y)[:, :, 0, :])
                        act.copy(e["S2"][0:r, y], sim_rows(y)[:, :, 1, :]).then_inc(sims_in, 1)
            act.wait_ge(sims_in, len(tiles))

        @blk.vector
        def _(dve):
            link = Chain(dve, dve_chain).link
            dve.wait_ge(zeroed, 3)
            dve.wait_ge(keys_t, 1)
            for j in range(2):
                r = slice(j * NST, (j + 1) * NST)
                dve.tensor_copy(KT[r, :, j, :], PS[r, 4, :].rearrange("p (h k) -> p h k", h=KH_)).then_inc(keys_in, 1)
            for y in range(len(tiles)):
                r, p = rows[y], y % 2
                dve.wait_ge(sims_in, y + 1)
                dve.tensor_copy(e["S1"][0:r, y, :, 0:ROWS_IN], SF[0:r, p, :, 0:ROWS_IN])
                for h in range(KH_):
                    dve.max(out=TOP[0:r, p, h, 1], in_=e["S2"][0:r, y, h])
                    last = dve.max(out=TOP[0:r, p, h, 0], in_=SF[0:r, p, h])
                link(last)
                for h in range(KH_):
                    last = dve.max_index(out=IDX[0:r, p, h], in_max=TOP[0:r, p, h, 0], in_values=SF[0:r, p, h])
                last.then_inc(sims_read, 1)
                dve.wait_ge(sims_read, y + 1)
                dve.tensor_scalar(BEYOND[0:r, p], IDX[0:r, p], float(ROWS_IN), None, ALU.is_ge)
                s = [r, KH_, TOPK, TOPK]
                link(dve.tensor_tensor(CAND[0:r], wide(TOP[0:r, p, :, 0][:, :, :, None], s),
                                       wide(TOP[0:r, p, :, 1][:, :, None, :], s), ALU.add))
                for h in range(KH_):
                    last = dve.max(out=BEST[0:r, h], in_=CAND[0:r, h].rearrange("p a b -> p (a b)"))
                link(last)
                link(dve.tensor_scalar(e["TAU"][0:r, y], BEST[0:r, :, TOPK - 1], 0.0, None, ALU.max))
                f = "p h a b -> p h (a b)"
                link(dve.tensor_tensor(CHOSEN[0:r].rearrange(f), CAND[0:r].rearrange(f),
                                       wide(e["TAU"][0:r, y][:, :, None], [r, KH_, TOPK * TOPK]), ALU.is_ge))
                link(dve.tensor_tensor(CHOSEN[0:r], CHOSEN[0:r], CAND[0:r], ALU.mult))
                link(dve.tensor_tensor(CHOSEN[0:r], CHOSEN[0:r], wide(BEYOND[0:r, p][:, :, :, None], s), ALU.mult))
                link(dve.reduce_sum(e["EXT"][0:r, y, CHUNKS - 1:CHUNKS], CHOSEN[0:r].rearrange("p h a b -> p (h a b)"), AX.X))


def expert_layer(nc, e_down, e_up, k, e, groups, base, tag):
    PS, HT, XH, XL, S1, S2, TAU, EXT = (k["PS"], k["HT"], e["XH"], e["XL"], e["S1"], e["S2"], e["TAU"], e["EXT"])
    NG_ = len(groups)
    ET = EC // P
    NQ = 2 * NG_
    NZ = ET * NQ
    first_tile = [sum(max(1, n // P) for _, n in groups[:g]) for g in range(NG_ + 1)]
    tiles_of = lambda q: [first_tile[q % NG_] + t for t in range(first_tile[q % NG_ + 1] - first_tile[q % NG_])]
    NY = 2 * first_tile[NG_]
    ROUNDS = CHUNKS // 2
    DB, GB, TB, OB = 0, 2, 3, 4
    rows_of = lambda y: P if y < first_tile[NG_] - 1 or groups[-1][1] >= P else groups[-1][1]
    seq = {q: [] for q in range(NQ + 1)}
    count = 0
    for q in range(NQ + 1):
        seq[q] = [(count + t, y) for t, y in enumerate(tiles_of(q))]
        count += len(seq[q])
    upto = [sum(len(seq[x]) for x in range(q + 1)) for q in range(NQ + 1)]
    with ExitStack() as ctx:
        sb = lambda n, s, d=F32: ctx.enter_context(nc.sbuf_tensor(tag + n, s, d))
        sem = signals(nc, ctx, tag)
        DR = sb("down_raw", [P, 2, D])
        UR = sb("up_raw", [P, 2, D])
        DH_ = sb("down_h", [P, 2, ET, DC, P], F32R)
        DL = sb("down_l", [P, 2, ET, DC, P], F32R)
        UH = sb("up_h", [P, 2, ET, D], F32R)
        UL = sb("up_l", [P, 2, ET, D], F32R)
        V0 = sb("v0", [P, 2, 2, EC])
        V1 = sb("v1", [P, 2, EC])
        G = sb("g", [P, 2, GRP // P, EC])
        S = sb("silu", [P, 2, GRP])
        WF = sb("w", [P, 2, GRP])
        WH = sb("wh", [P, 2, GRP], F32R)
        WL = sb("wl", [P, 2, GRP], F32R)
        load_d, load_u = [sem("load_d0"), sem("load_d1")], [sem("load_u0"), sem("load_u1")]
        table_t, down_h, down_l, up_h, up_l = sem("table_t"), sem("down_hr"), sem("down_lr"), sem("up_hr"), sem("up_lr")
        sums0, sums1, masked0, masked1 = sem("sums0"), sem("sums1"), sem("masked0"), sem("masked1")
        pool_chain, g_ready = sem("pool_chain"), sem("g_ready")
        d_done, t_done, silus, w_ready, w_high, w_low = (sem("d_done"), sem("t_done"), sem("silus"), sem("w_ready"),
                                                         sem("w_high"), sem("w_low"))
        up_done, added = sem("up_done"), sem("added")
        blk = ctx.enter_context(nc.Block())

        def table_at(q, j):
            z = (q % NG_) * ET + j
            return (q // NG_) * ET + z // 2 if z % 2 and z < 2 * ET else None

        def table_free(eng, i, x):
            eng.wait_ge(up_done, i * NZ + (NZ // 2 if x >= ET else 0) + 2)

        @blk.sync
        def _(sp):
            def load(n, x, chunk):
                r = bass.ds(chunk * EC + (x % ET) * P, P)
                sp.dma_start(DR[:, x % 2], e_down[r, :]).then_inc(load_d[x % 2], 16)
                sp.dma_start(UR[:, x % 2], e_up[r, :]).then_inc(load_u[x % 2], 16)

            for x in range(ET):
                if x >= 2:
                    sp.wait_ge(table_t, x - 1)
                    sp.wait_ge(up_l, x - 1)
                load(0, x, 0)
            with sp.Fori(0, ROUNDS) as i:
                for x in range(2 * ET):
                    n = i * 2 * ET + ET + x
                    sp.wait_ge(table_t, n - 1)
                    sp.wait_ge(up_l, n - 1)
                    load(n, x, 2 * i + 1 if x < ET else (2 * i + 2) % CHUNKS)

        def number(i, x):
            return x if i is None else i * 2 * ET + ET + x

        def arrived(eng, sems, i, x):
            eng.wait_ge(sems[x % 2], 16 * (x // 2 + 1) if i is None else i * 16 * ET + 16 * (ET // 2 + x // 2 + 1))

        def slot(i, x):
            return 0 if i is None or x >= ET else 1

        @blk.tensor
        def _(pe):
            pe.sem_inc(silus, 2)
            pe.sem_inc(w_ready, 2)
            pe.sem_inc(w_low, 2)
            pe.sem_inc(up_done, 2)
            pe.sem_inc(added, DC)
            pe.sem_inc(g_ready, 2)

            def table(i, x):
                n = number(i, x)
                arrived(pe, load_d, i, x)
                pe.wait_ge(down_l, n)
                for a in range(DC):
                    last = pe.transpose(PS[:, TB, a * P:(a + 1) * P], DR[:, x % 2, a * P:(a + 1) * P], k["ident"][:, :])
                last.then_inc(table_t, 1)

            for x in range(ET):
                table(None, x)
            with pe.Fori(0, ROUNDS) as i:
                def up(q, j):
                    s, (c0, n) = q // NG_, groups[q % NG_]
                    z = i * NZ + q * ET + j
                    pe.wait_ge(w_low, z + 3)
                    pe.wait_ge(up_l, i * 2 * ET + s * ET + j + 1)
                    for f in range(DC):
                        if j == 0:
                            pe.wait_ge(added, DC * (i * NQ + q) + f + 1)
                        out = PS[:, OB + f, 0:n]
                        fs = slice(f * P, (f + 1) * P)
                        pe.matmul(out, UH[:, s, j, fs], WH[:, j % 2, 0:n], start=j == 0, stop=False)
                        pe.matmul(out, UH[:, s, j, fs], WL[:, j % 2, 0:n], start=False, stop=False)
                        last = pe.matmul(out, UL[:, s, j, fs], WH[:, j % 2, 0:n], start=False, stop=j == ET - 1)
                    last.then_inc(up_done, 1)

                before = None
                for q in range(NQ):
                    s, (c0, n) = q // NG_, groups[q % NG_]
                    for j in range(ET):
                        z = i * NZ + q * ET + j
                        pe.wait_ge(down_l, i * 2 * ET + s * ET + j + 1)
                        pe.wait_ge(silus, z + 1)
                        if n < P:
                            pe.wait_ge(g_ready, i * NY + upto[q] + 2)
                            pe.wait_ge(w_ready, z + 2)
                        split_product(pe, PS[:, DB + j % 2, 0:n],
                                      [(DH_[:, s, j, a], DL[:, s, j, a], XH[:, a, c0 - base:c0 - base + n],
                                        XL[:, a, c0 - base:c0 - base + n]) for a in range(DC)]).then_inc(d_done, 1)
                        if n >= P:
                            pe.wait_ge(g_ready, i * NY + upto[q] + 2)
                            pe.wait_ge(w_ready, z + 2)
                        for t in range(max(1, n // P)):
                            r = min(P, n)
                            last = pe.transpose(PS[:, GB, t * P:t * P + r], G[0:r, q % 2, t, j * P:(j + 1) * P],
                                                k["ident"][0:r, 0:r])
                        last.then_inc(t_done, 1)
                        if before:
                            up(*before)
                        before = q, j
                        if table_at(q, j) is not None:
                            table(i, table_at(q, j))
                up(*before)

        @blk.scalar
        def _(act):
            def table(i, x):
                n = number(i, x)
                act.wait_ge(table_t, n + 1)
                if i is not None:
                    table_free(act, i, x)
                act.copy(DH_[:, slot(i, x), x % ET].rearrange("p a e -> p (a e)"), PS[:, TB]).then_inc(down_h, 1)
                arrived(act, load_u, i, x)
                act.copy(UH[:, slot(i, x), x % ET], UR[:, x % 2]).then_inc(up_h, 1)

            def pair_sums(n, y, m, chunk):
                r = rows_of(y)
                act.wait_ge(g_ready, n + 1)
                for h in range(2):
                    for c in range(RPC):
                        last = act.activation(V0[0:r, m % 2, h, c * NK:(c + 1) * NK], S2[0:r, y, h], ACT.Identity,
                                              bias=S1[0:r, y, h, bass.ds(chunk * RPC + c, 1)])
                last.then_inc(sums0, 1)

            for x in range(ET):
                table(None, x)
            for m, y in seq[0]:
                pair_sums(m, y, m, 0)
            with act.Fori(0, ROUNDS) as i:
                def high(q, j):
                    n = groups[q % NG_][1]
                    z = i * NZ + q * ET + j
                    act.wait_ge(w_ready, z + 3)
                    act.wait_ge(up_done, z + 1)
                    act.copy(WH[:, j % 2, 0:n], WF[:, j % 2, 0:n]).then_inc(w_high, 1)

                for q in range(NQ):
                    n = groups[q % NG_][1]
                    for j in range(ET):
                        z = i * NZ + q * ET + j
                        act.wait_ge(d_done, z + 1)
                        act.wait_ge(w_ready, z + 1)
                        act.activation(S[:, j % 2, 0:n], PS[:, DB + j % 2, 0:n], ACT.Silu).then_inc(silus, 1)
                        if j < len(seq[q + 1]):
                            m, y = seq[q + 1][j]
                            pair_sums(i * NY + m, y, m, 2 * i + (q + 1) // NG_)
                        high(q, j)
                        if table_at(q, j) is not None:
                            table(i, table_at(q, j))

        @blk.vector
        def _(dve):
            def table(i, x):
                n = number(i, x)
                dve.wait_ge(down_h, n + 1)
                sl = slot(i, x)
                dve.tensor_tensor(DL[:, sl, x % ET].rearrange("p a e -> p (a e)"), PS[:, TB],
                                  DH_[:, sl, x % ET].rearrange("p a e -> p (a e)").bitcast(F32), ALU.subtract).then_inc(down_l, 1)

            def choose(n, y, m, chunk):
                r = rows_of(y)
                dve.wait_ge(sums0, n + 1)
                for h in range(2):
                    v = V0[0:r, m % 2, h]
                    last = dve.scalar_tensor_tensor(v, v, TAU[0:r, y, h:h + 1], v, ALU.is_ge, ALU.mult)
                last.then_inc(masked0, 1)
                dve.wait_ge(g_ready, n + 2)
                s = [r, 2, RPC, NK]
                dve.tensor_tensor(V1[0:r].rearrange("p h (c k) -> p h c k", c=RPC), wide(S2[0:r, y, 2:4][:, :, None, :], s),
                                  wide(S1[0:r, y, 2:4, bass.ds(chunk * RPC, RPC)][:, :, :, None], s), ALU.add).then_inc(sums1, 1)
                dve.wait_ge(sums1, n + 1)
                for h in range(2):
                    v = V1[0:r, h]
                    last = dve.scalar_tensor_tensor(v, v, TAU[0:r, y, 2 + h:3 + h], v, ALU.is_ge, ALU.mult)
                last.then_inc(masked1, 1)

            for x in range(ET):
                table(None, x)
            for m, y in seq[0]:
                choose(m, y, m, 0)
            with dve.Fori(0, ROUNDS) as i:
                def add(q):
                    c0, n = groups[q % NG_]
                    dve.wait_ge(up_done, i * NZ + (q + 1) * ET + 2)
                    for f in range(DC):
                        dve.tensor_tensor(HT[:, f, c0:c0 + n], HT[:, f, c0:c0 + n], PS[:, OB + f, 0:n], ALU.add).then_inc(added, 1)

                for q in range(NQ):
                    n = groups[q % NG_][1]
                    for j in range(ET):
                        z = i * NZ + q * ET + j
                        dve.wait_ge(silus, z + 3)
                        dve.wait_ge(t_done, z + 1)
                        dve.wait_ge(w_low, z + 1)
                        dve.tensor_tensor(WF[:, j % 2, 0:n], S[:, j % 2, 0:n], PS[:, GB, 0:n], ALU.mult).then_inc(w_ready, 1)
                        if j == 0 and q:
                            add(q - 1)
                        if j < len(seq[q + 1]):
                            m, y = seq[q + 1][j]
                            choose(i * NY + m, y, m, 2 * i + (q + 1) // NG_)
                        if table_at(q, j) is not None:
                            table(i, table_at(q, j))
                add(NQ - 1)
            dve.wait_ge(added, DC * (ROUNDS * NQ + 1))

        @blk.gpsimd
        def _(pool):
            def table(i, x):
                n = number(i, x)
                pool.wait_ge(up_h, n + 1)
                sl = slot(i, x)
                pool.tensor_tensor(UL[:, sl, x % ET], UR[:, x % 2], UH[:, sl, x % ET].bitcast(F32), ALU.subtract).then_inc(up_l, 1)

            def add_heads(n, y, m, chunk, sl, t):
                r = rows_of(y)
                v0 = V0[0:r, m % 2]
                pool.wait_ge(masked0, n + 1)
                pool.wait_ge(masked1, n + 1)
                pool.tensor_tensor(v0, v0, V1[0:r], ALU.add).then_inc(pool_chain, 1)
                pool.wait_ge(pool_chain, 2 * n + 1)
                last = V0[0:r, m % 2, 0, EC - 1:EC]
                pool.tensor_tensor(last, last, EXT[0:r, y, bass.ds(chunk, 1)], ALU.add).then_inc(pool_chain, 1)
                pool.wait_ge(pool_chain, 2 * n + 2)
                pool.tensor_tensor(G[0:r, sl, t], V0[0:r, m % 2, 0], V0[0:r, m % 2, 1], ALU.add).then_inc(g_ready, 1)

            for x in range(ET):
                table(None, x)
            for t, (m, y) in enumerate(seq[0]):
                add_heads(m, y, m, 0, 0, t)
            with pool.Fori(0, ROUNDS) as i:
                for q in range(NQ):
                    n = groups[q % NG_][1]
                    for j in range(ET):
                        z = i * NZ + q * ET + j
                        if j < len(seq[q + 1]):
                            m, y = seq[q + 1][j]
                            pool.wait_ge(t_done, i * NZ + q * ET)
                            add_heads(i * NY + m, y, m, 2 * i + (q + 1) // NG_, (q + 1) % 2, j)
                        pool.wait_ge(w_high, z + 1)
                        pool.tensor_tensor(WL[:, j % 2, 0:n], WF[:, j % 2, 0:n], WH[:, j % 2, 0:n].bitcast(F32), ALU.subtract).then_inc(w_low, 1)
                        if table_at(q, j) is not None:
                            table(i, table_at(q, j))
            pool.wait_ge(up_l, ROUNDS * 2 * ET + ET)
            pool.wait_ge(g_ready, ROUNDS * NY + upto[0] + 2)


def store_tokens(nc, out, k):
    PS, HT = k["PS"], k["HT"]
    NT = TR // P
    OUTS = 4
    with ExitStack() as ctx:
        OUT = ctx.enter_context(nc.sbuf_tensor("o_rows", [P, OUTS, D], F32))
        sem = signals(nc, ctx)
        turned, copied = sem("o_turned"), sem("o_copied")
        stored = [sem(f"o_stored{n}") for n in range(OUTS)]
        blk = ctx.enter_context(nc.Block())

        @blk.tensor
        def _(pe):
            for y in range(NT + 1):
                r = P if y < NT else B
                if y >= 4:
                    pe.wait_ge(copied, y - 3)
                for f in range(DC):
                    last = pe.transpose(PS[0:r, y % 4, f * P:(f + 1) * P], HT[:, f, y * P:y * P + r], k["ident"][:, :])
                last.then_inc(turned, 1)

        @blk.vector
        def _(dve):
            for y in range(NT + 1):
                r = P if y < NT else B
                dve.wait_ge(turned, y + 1)
                if y >= OUTS:
                    dve.wait_ge(stored[y % OUTS], 16 * (y // OUTS))
                dve.tensor_copy(OUT[0:r, y % OUTS], PS[0:r, y % 4]).then_inc(copied, 1)

        @blk.sync
        def _(sp):
            for y in range(NT + 1):
                sp.wait_ge(copied, y + 1)
                c0 = y * P
                dst = out[c0 // NCH, 1 + c0 % NCH:1 + c0 % NCH + P, :] if y < NT else out[:, 0, :]
                sp.dma_start(dst, OUT[0:P if y < NT else B, y % OUTS]).then_inc(stored[y % OUTS], 16)
            for n in range(OUTS):
                sp.wait_ge(stored[n], 16 * ((NT + OUTS - n) // OUTS))


def tower(nc, x, cls_tok, log_dt, log_w_real, w_imag, w_qkv, w_o, w_q, keys, e_down, e_up, out):
    with ExitStack() as life:
        sb = lambda ctx, n, s, d=F32: ctx.enter_context(nc.sbuf_tensor(n, s, d))
        k = {"ident": sb(life, "ident", [P, P]), "mean_w": sb(life, "mean_w", [P, P]),
             "HT": sb(life, "tokens", [P, DC, T]),
             "PS": life.enter_context(nc.psum_tensor("psum", [P, 8, GRP], F32))}
        with ExitStack() as ctx:
            m = {"U": sb(ctx, "m_u", [P, NCH, B, DC]), "turn": sb(ctx, "m_turn", [P, NCH]),
                 "decay": sb(ctx, "m_decay", [P, NCH]), "phase": sb(ctx, "m_phase", [P, 1]),
                 "quarter": sb(ctx, "m_quarter", [P, 1]), "iota": sb(ctx, "m_iota", [P, P])}
            mixer_factors(nc, x, cls_tok, log_dt, log_w_real, w_imag, k, m)
            mixer_tokens(nc, k, m)
        with ExitStack() as ctx:
            k["XH"], k["XL"] = sb(ctx, "xh", [P, DC, T], F32R), sb(ctx, "xl", [P, DC, T], F32R)
            k["PCH"], k["PCL"] = sb(ctx, "class_ph", [P, B, NCH + 2], F32R), sb(ctx, "class_pl", [P, B, NCH + 2], F32R)
            with nc.sbuf_tensor("class_x", [P, DC, P], F32) as XB:
                layernorm(nc, k, [GROUPS[-1]] + GROUPS[:-1], k["XH"], k["XL"], "l1_", cls_copy=XB[:, :, :])
                class_rows(nc, w_qkv, k, XB)
            attention(nc, w_qkv, w_o, k)
        expert_halves(nc, w_q, keys, e_down, e_up, k)
        store_tokens(nc, out, k)


def expert_halves(nc, w_q, keys, e_down, e_up, k):
    for half, groups in enumerate((GROUPS[:NG // 2], GROUPS[NG // 2:])):
        with ExitStack() as ctx:
            sb = lambda n, s, d=F32: ctx.enter_context(nc.sbuf_tensor(f"h{half}_{n}", s, d))
            n = sum(n for _, n in groups)
            nt = sum(max(1, n // P) for _, n in groups)
            base = groups[0][0]
            e = {"XH": sb("xh", [P, DC, n], F32R), "XL": sb("xl", [P, DC, n], F32R),
                 "S1": sb("s1", [P, nt, KH_, ROWS_IN + RPC]), "S2": sb("s2", [P, nt, KH_, NK]),
                 "TAU": sb("tau", [P, nt, KH_]), "EXT": sb("beyond", [P, nt, CHUNKS + 1])}
            layernorm(nc, k, groups, e["XH"], e["XL"], f"l2{half}_", base)
            key_scores(nc, w_q, keys, k, e, groups, base, f"e{half}_")
            expert_layer(nc, e_down, e_up, k, e, groups, base, f"e{half}_")


def kernel(x, cls_tok, L0_tok_log_dt, L0_tok_log_w_real, L0_tok_w_imag, L0_attn_w_qkv, L0_attn_w_o,
           L0_ffn_Wq, L0_ffn_keys, L0_ffn_e_down, L0_ffn_e_up):
    import numpy as np
    import concourse.bacc as bacc
    from concourse.bass_utils import run_bass_kernel_spmd

    given = {"x": x, "cls_tok": cls_tok, "log_dt": L0_tok_log_dt, "log_w_real": L0_tok_log_w_real,
             "w_imag": L0_tok_w_imag, "w_qkv": L0_attn_w_qkv, "w_o": L0_attn_w_o, "w_q": L0_ffn_Wq,
             "keys": L0_ffn_keys, "e_down": L0_ffn_e_down, "e_up": L0_ffn_e_up}
    nc = bacc.Bacc("TRN2", target_bir_lowering=False, num_devices=1)
    arrays = {n: np.ascontiguousarray(a) for n, a in given.items()}
    ins = [nc.dram_tensor(n, a.shape, mybir.dt.from_np(a.dtype), kind="ExternalInput").ap() for n, a in arrays.items()]
    out = nc.dram_tensor("out", (B, NCH + 1, D), F32, kind="ExternalOutput").ap()
    tower(nc, *ins, out)
    r = run_bass_kernel_spmd(nc, [arrays], core_ids=[0])
    return r.results[0]["out"]
```

```python
import math
from contextlib import ExitStack

import concourse.bass as bass
from concourse import mybir

F32 = mybir.dt.float32
F32R = mybir.dt.float32r
I32 = mybir.dt.int32
U32 = mybir.dt.uint32
ALU = mybir.AluOpType
ACT = mybir.ActivationFunctionType
AX = mybir.AxisListType

P = 128
B = 8
NCH = 256
NST = 64
D = 512
DC = D // P
TR = B * NCH
T = TR + B
HEADS = 16
DH = 128
SCALE = DH ** -0.5
EPS = 1e-5
GRP = 512
NG = TR // GRP
GROUPS = [(g * GRP, GRP) for g in range(NG)] + [(TR, B)]

ROUND = 1.5 * 2.0 ** 23
TWO_PI = 6.283185
LN2_HI = 0.693145751953125
LN2_LO = 1.42860677e-06


class Chain:

    def __init__(self, eng, sem):
        self.eng, self.sem, self.n = eng, sem, 0

    def link(self, instruction):
        self.n += 1
        instruction.then_inc(self.sem, 1)
        self.eng.wait_ge(self.sem, self.n)


def signals(nc, ctx, tag=""):
    made = []

    def clear():
        with nc.Block() as blk:
            @blk.sync
            def _(sp):
                for s in made:
                    sp.sem_clear(s)
        for s in made:
            nc.release_semaphore(s)

    def make(name):
        made.append(nc.alloc_semaphore(tag + name))
        return made[-1]

    ctx.callback(clear)
    return make


def wide(ap, shape):
    return ap.to_broadcast(list(shape))


def mixer_factors(nc, x, cls_tok, log_dt, log_w_real, w_imag, k, m):
    NA = DC - 1
    HN = 2 * NST
    CH = 16
    with ExitStack() as ctx:
        sb = lambda n, s, d=F32: ctx.enter_context(nc.sbuf_tensor(n, s, d))
        sem = signals(nc, ctx)
        Y = sb("a_logs", [P, 2 + HN])
        WI = sb("a_wimag", [P, HN])
        X = sb("a_x", [P, 2, B, NST, 2])
        KK = sb("a_k", [P, 2 + HN])
        RR = sb("a_r", [P, 2 + HN])
        EE = sb("a_e", [P, 2 + HN])
        II = sb("a_pow2", [P, 2 + HN], I32)
        EX = sb("a_exp", [P, 2 + HN])
        DR = sb("a_dr", [P, HN])
        DI = sb("a_di", [P, HN])
        TURN = sb("a_turn", [P, HN])
        T1 = sb("a_t1", [P, 3, HN])
        ANG = sb("a_ang", [P, 9, HN])
        SN = sb("a_sin", [P, 9, HN])
        ER = sb("a_er", [P, NA, HN])
        TH = sb("a_tanh", [P, HN])
        Q1 = sb("a_q1", [P, HN])
        Q2 = sb("a_q2", [P, HN])
        NR = sb("a_nr", [P, HN])
        NI = sb("a_ni", [P, HN])
        BR = sb("a_br", [P, 2, NST])
        BI = sb("a_bi", [P, 2, NST])
        CR = sb("a_cr", [P, 2, B, NST])
        CI = sb("a_ci", [P, 2, B, NST])
        C1 = sb("a_c1", [P, 2, B, NST])
        C2 = sb("a_c2", [P, 2, B, NST])
        PR = sb("a_pr", [P, NA, 2, NST])
        PI = sb("a_pi", [P, NA, 2, NST])
        NPR = sb("a_npr", [P, NA, 2, NST])
        M1 = sb("a_m1", [P, B, NA, NST])
        M2 = sb("a_m2", [P, B, NA, NST])
        UH = sb("a_uh", [P, 2, B, DC, NST, 2])
        DUP = sb("a_dup", [P, 5, NST, 2])
        IOT = sb("a_iota", [P, P], I32)
        CLS = sb("a_cls", [P, DC])
        PS = k["PS"]
        load_par = sem("a_load_par")
        load_x = sem("a_load_x")
        load_cls = sem("a_load_cls")
        ident_zero = sem("a_ident_zero")
        consts = sem("a_consts")
        iota_made = sem("a_iota_made")
        dve_chain = sem("a_dve_chain")
        args_ready = sem("a_args_ready")
        exps_ready = sem("a_exps_ready")
        sins_ready = sem("a_sins_ready")
        dup_ready = sem("a_dup_ready")
        u_ready = sem("a_u_ready")
        rows_t = sem("a_rows_t")
        u_t = sem("a_u_t")
        copied_v = sem("a_copied_v")
        copied_s = sem("a_copied_s")
        done = sem("a_done")
        blk = ctx.enter_context(nc.Block())

        @blk.sync
        def _(sp):
            sp.dma_start(Y[:, 0:2], log_dt.rearrange("(g p) -> p g", p=P), allow_slow_non_contiguous=True).then_inc(load_par, 16)
            sp.dma_start(Y[:, 2:].rearrange("p (g n) -> p g n", g=2),
                         log_w_real.rearrange("(g p) n -> p g n", p=P)).then_inc(load_par, 16)
            sp.dma_start(WI[:, :].rearrange("p (g n) -> p g n", g=2),
                         w_imag.rearrange("(g p) n -> p g n", p=P)).then_inc(load_par, 16)
            for g in range(2):
                sp.dma_start(X[:, g].rearrange("p c n r -> p c (n r)"),
                             x[:, g * P:(g + 1) * P].rearrange("c p n r -> p c (n r)")).then_inc(load_x, 16)
            sp.dma_start(CLS[:, :], cls_tok[0, 0, :].rearrange("(a p) -> p a", p=P), allow_slow_non_contiguous=True).then_inc(load_cls, 16)

        @blk.gpsimd
        def _(pool):
            pool.memset(k["ident"][:, :], 0.0).then_inc(ident_zero, 1)
            pool.iota(IOT[:, :], pattern=[[1, P]], base=0, channel_multiplier=0).then_inc(iota_made, 1)
            pool.memset(k["mean_w"][:, :], 1.0 / D).then_inc(consts, 1)
            pool.memset(DUP[:, 4, :, 0], 0.25).then_inc(consts, 1)
            pool.memset(DUP[:, 4, :, 1], 0.0).then_inc(consts, 1)
            pool.wait_ge(ident_zero, 1)
            pool.affine_select(out=k["ident"][:, :], in_=k["ident"][:, :], compare_op=ALU.not_equal, fill=1.0,
                               base=0, pattern=[[-1, P]], channel_multiplier=1).then_inc(consts, 1)
            pool.wait_ge(iota_made, 1)
            pool.tensor_copy(m["iota"][:, :], IOT[:, :]).then_inc(consts, 1)
            pool.wait_ge(load_cls, 16)
            pool.tensor_copy(k["HT"][:, :, TR:T], wide(CLS[:, :, None], [P, DC, B])).then_inc(consts, 1)
            pool.wait_ge(consts, 6)

        @blk.vector
        def _(dve):
            link = Chain(dve, dve_chain).link
            dve.wait_ge(load_par, 48)
            link(dve.tensor_scalar(KK[:, :], Y[:, :], 1 / math.log(2), ROUND, ALU.mult, ALU.add))
            link(dve.tensor_scalar(KK[:, :], KK[:, :], ROUND, -126.0, ALU.subtract, ALU.max))
            link(dve.tensor_scalar(KK[:, :], KK[:, :], 127.0, None, ALU.min))
            link(dve.scalar_tensor_tensor(RR[:, :], KK[:, :], -LN2_HI, Y[:, :], ALU.mult, ALU.add))
            link(dve.scalar_tensor_tensor(RR[:, :], KK[:, :], -LN2_LO, RR[:, :], ALU.mult, ALU.add))
            link(dve.tensor_scalar(EE[:, :], RR[:, :], 1 / 5040, None, ALU.mult))
            for c in (1 / 720, 1 / 120, 1 / 24, 1 / 6, 0.5, 1.0):
                link(dve.scalar_tensor_tensor(EE[:, :], EE[:, :], c, RR[:, :], ALU.add, ALU.mult))
            link(dve.tensor_scalar(II[:, :], KK[:, :], 127.0, 2.0 ** 23, ALU.add, ALU.mult))
            link(dve.scalar_tensor_tensor(EX[:, :], EE[:, :], 1.0, II[:, :].bitcast(F32), ALU.add, ALU.mult))
            WR = EX[:, 2:]
            for g in range(2):
                s = slice(g * NST, (g + 1) * NST)
                dve.tensor_scalar(DR[:, s], EX[:, 2 + g * NST:2 + (g + 1) * NST], EX[:, g:g + 1], -1.0,
                                  ALU.mult, ALU.mult)
                link(dve.tensor_scalar(DI[:, s], WI[:, s], EX[:, g:g + 1], None, ALU.mult))
            for a in range(NA):
                dve.tensor_scalar(ER[:, a], DR[:, :], float(P * (a + 1)), None, ALU.mult).then_inc(args_ready, 1)
            link(dve.tensor_scalar(TURN[:, :], DI[:, :], 1 / (2 * math.pi), None, ALU.mult))
            link(dve.tensor_scalar(T1[:, 0], TURN[:, :], ROUND, ROUND, ALU.add, ALU.subtract))
            link(dve.tensor_tensor(ANG[:, 0], TURN[:, :], T1[:, 0], ALU.subtract))
            link(dve.tensor_scalar(TURN[:, :], TURN[:, :], 0.5, None, ALU.mult))
            link(dve.tensor_scalar(T1[:, 0], TURN[:, :], ROUND, ROUND, ALU.add, ALU.subtract))
            link(dve.tensor_tensor(ANG[:, 2], TURN[:, :], T1[:, 0], ALU.subtract))
            for a in range(NA):
                last = dve.tensor_scalar(ANG[:, 3 + a], ANG[:, 0], float(P * (a + 1)), None, ALU.mult)
            link(last)
            link(dve.tensor_scalar(T1[:, :], ANG[:, 3:6], ROUND, ROUND, ALU.add, ALU.subtract))
            link(dve.tensor_tensor(ANG[:, 3:6], ANG[:, 3:6], T1[:, :], ALU.subtract))
            dve.tensor_scalar(ANG[:, 1], ANG[:, 0], 0.25, None, ALU.add)
            link(dve.tensor_scalar(ANG[:, 6:9], ANG[:, 3:6], 0.25, None, ALU.add))
            dve.tensor_scalar(T1[:, 0], ANG[:, 1], ROUND, ROUND, ALU.add, ALU.subtract)
            link(dve.tensor_scalar(SN[:, 0:3], ANG[:, 6:9], ROUND, ROUND, ALU.add, ALU.subtract))
            dve.tensor_tensor(ANG[:, 1], ANG[:, 1], T1[:, 0], ALU.subtract).then_inc(args_ready, 1)
            dve.tensor_tensor(ANG[:, 6:9], ANG[:, 6:9], SN[:, 0:3], ALU.subtract).then_inc(args_ready, 1)
            for g in range(2):
                dve.tensor_copy(DUP[:, g], wide(ANG[:, 0, g * NST:(g + 1) * NST][:, :, None], [P, NST, 2])).then_inc(dup_ready, 1)
                dve.tensor_copy(DUP[:, 2 + g], wide(DR[:, g * NST:(g + 1) * NST][:, :, None], [P, NST, 2])).then_inc(dup_ready, 1)
            dve.wait_ge(exps_ready, 1)
            link(dve.tensor_scalar(Q1[:, :], TH[:, :], -1.0, 1.0, ALU.mult, ALU.add))
            link(dve.reciprocal(Q2[:, :], Q1[:, :]))
            link(dve.scalar_tensor_tensor(Q1[:, :], TH[:, :], 2.0, Q2[:, :], ALU.mult, ALU.mult))
            dve.wait_ge(sins_ready, 1)
            link(dve.scalar_tensor_tensor(Q2[:, :], SN[:, 2], -2.0, SN[:, 2], ALU.mult, ALU.mult))
            link(dve.tensor_tensor(NR[:, :], Q1[:, :], SN[:, 1], ALU.mult))
            link(dve.tensor_tensor(NR[:, :], NR[:, :], Q2[:, :], ALU.add))
            link(dve.scalar_tensor_tensor(NI[:, :], Q1[:, :], 1.0, SN[:, 0], ALU.add, ALU.mult))
            link(dve.tensor_tensor(Q1[:, :], WR, WR, ALU.mult))
            link(dve.tensor_tensor(Q2[:, :], WI[:, :], WI[:, :], ALU.mult))
            link(dve.tensor_tensor(Q1[:, :], Q1[:, :], Q2[:, :], ALU.add))
            link(dve.reciprocal(Q2[:, :], Q1[:, :]))
            br = BR[:, :, :].rearrange("p g n -> p (g n)")
            bi = BI[:, :, :].rearrange("p g n -> p (g n)")
            dve.tensor_tensor(T1[:, 0], NI[:, :], WI[:, :], ALU.mult)
            link(dve.tensor_tensor(T1[:, 1], NR[:, :], WR, ALU.mult))
            link(dve.tensor_tensor(T1[:, 0], T1[:, 0], T1[:, 1], ALU.subtract))
            link(dve.scalar_tensor_tensor(br, T1[:, 0], 2.0, Q2[:, :], ALU.mult, ALU.mult))
            dve.tensor_tensor(T1[:, 0], NI[:, :], WR, ALU.mult)
            link(dve.tensor_tensor(T1[:, 1], NR[:, :], WI[:, :], ALU.mult))
            link(dve.tensor_tensor(T1[:, 0], T1[:, 0], T1[:, 1], ALU.add))
            link(dve.scalar_tensor_tensor(bi, T1[:, 0], -2.0, Q2[:, :], ALU.mult, ALU.mult))
            em = ER[:, :, :]
            pr = PR[:, :, :, :].rearrange("p a g n -> p a (g n)")
            pi = PI[:, :, :, :].rearrange("p a g n -> p a (g n)")
            npr = NPR[:, :, :, :].rearrange("p a g n -> p a (g n)")
            link(dve.tensor_tensor(pr, em, SN[:, 6:9], ALU.mult))
            dve.tensor_tensor(pi, em, SN[:, 3:6], ALU.mult)
            link(dve.tensor_scalar(npr, pr, -1.0, None, ALU.mult))
            dve.wait_ge(load_x, 32)
            for g in range(2):
                xr, xi = X[:, g, :, :, 0], X[:, g, :, :, 1]
                b_r, b_i = wide(BR[:, g][:, None, :], [P, B, NST]), wide(BI[:, g][:, None, :], [P, B, NST])
                dve.tensor_tensor(CR[:, g], xr, b_r, ALU.mult)
                dve.tensor_tensor(C1[:, g], xi, b_i, ALU.mult)
                dve.tensor_tensor(CI[:, g], xr, b_i, ALU.mult)
                link(dve.tensor_tensor(C2[:, g], xi, b_r, ALU.mult))
                dve.tensor_tensor(CR[:, g], CR[:, g], C1[:, g], ALU.subtract)
                link(dve.tensor_tensor(CI[:, g], CI[:, g], C2[:, g], ALU.add))
            for g in range(2):
                dve.tensor_copy(UH[:, g, :, 0, :, 0], CR[:, g])
                dve.tensor_scalar(UH[:, g, :, 0, :, 1], CI[:, g], -1.0, None, ALU.mult)
                s = [P, B, NA, NST]
                cr, ci = wide(CR[:, g][:, :, None, :], s), wide(CI[:, g][:, :, None, :], s)
                p_r, p_i, np_r = (wide(t[:, :, g][:, None, :, :], s) for t in (PR, PI, NPR))
                if g:
                    dve.wait_ge(u_ready, 1)
                dve.tensor_tensor(M1[:, :, :, :], cr, p_r, ALU.mult)
                link(dve.tensor_tensor(M2[:, :, :, :], ci, p_i, ALU.mult))
                link(dve.tensor_tensor(UH[:, g, :, 1:, :, 0], M1[:, :, :, :], M2[:, :, :, :], ALU.subtract))
                dve.tensor_tensor(M1[:, :, :, :], ci, np_r, ALU.mult)
                link(dve.tensor_tensor(M2[:, :, :, :], cr, p_i, ALU.mult))
                dve.tensor_tensor(UH[:, g, :, 1:, :, 1], M1[:, :, :, :], M2[:, :, :, :], ALU.subtract).then_inc(u_ready, 1)
            dve.wait_ge(rows_t, 5)
            dve.tensor_copy(m["turn"][:, :], PS[:, 0, 0:NCH]).then_inc(done, 1)
            dve.tensor_copy(m["decay"][:, :], PS[:, 0, NCH:2 * NCH]).then_inc(done, 1)
            dve.tensor_copy(m["quarter"][:, :], PS[:, 1, 0:1]).then_inc(done, 1)
            dve.tensor_scalar(m["phase"][:, :], PS[:, 1, 0:1], TWO_PI, None, ALU.mult).then_inc(done, 1)
            for i in range(0, CH, 2):
                g, c = i // B, i % B
                dve.wait_ge(u_t, i + 1)
                dve.tensor_copy(m["U"][:, g * P:(g + 1) * P, c, :],
                                PS[:, 2 + i % 6, :].rearrange("p (a h) -> p h a", a=DC)).then_inc(copied_v, 1)
            dve.wait_ge(copied_v, CH // 2)
            dve.wait_ge(done, 4)

        @blk.scalar
        def _(act):
            act.wait_ge(args_ready, 3)
            act.activation(TH[:, :], DR[:, :], ACT.Tanh, scale=0.5).then_inc(exps_ready, 1)
            act.activation(ER[:, :, :], ER[:, :, :], ACT.Exp)
            act.wait_ge(args_ready, 5)
            act.activation(SN[:, :, :], ANG[:, :, :], ACT.Sin, scale=TWO_PI).then_inc(sins_ready, 1)
            for i in range(1, CH, 2):
                g, c = i // B, i % B
                act.wait_ge(u_t, i + 1)
                act.copy(m["U"][:, g * P:(g + 1) * P, c, :],
                         PS[:, 2 + i % 6, :].rearrange("p (a h) -> p h a", a=DC)).then_inc(copied_s, 1)
            act.wait_ge(copied_s, CH // 2)

        @blk.tensor
        def _(pe):
            pe.wait_ge(consts, 6)
            pe.wait_ge(dup_ready, 4)
            for i in range(4):
                pe.transpose(PS[:, 0, i * P:(i + 1) * P], DUP[:, i].rearrange("p n r -> p (n r)"), k["ident"][:, :]).then_inc(rows_t, 1)
            pe.transpose(PS[:, 1, 0:P], DUP[:, 4].rearrange("p n r -> p (n r)"), k["ident"][:, :]).then_inc(rows_t, 1)
            for i in range(CH):
                g, c = i // B, i % B
                pe.wait_ge(u_ready, g + 1)
                if i >= 6:
                    pe.wait_ge(copied_s if i % 2 else copied_v, (i - 6) // 2 + 1)
                for a in range(DC):
                    last = pe.transpose(PS[:, 2 + i % 6, a * P:(a + 1) * P],
                                        UH[:, g, c, a].rearrange("p n r -> p (n r)"), k["ident"][:, :])
                last.then_inc(u_t, 1)


def mixer_tokens(nc, k, m):
    CPC = 16
    SLOTS = 8
    HALF = CPC * SLOTS
    PS, HT = k["PS"], k["HT"]
    with ExitStack() as ctx:
        sb = lambda n, s, d=F32: ctx.enter_context(nc.sbuf_tensor(n, s, d))
        sem = signals(nc, ctx)
        Z = sb("z_pow", [P, SLOTS, CPC, P])
        A = sb("z_turn", [P, 2, CPC, P])
        K = sb("z_round", [P, 2, CPC, P])
        decay_arg = sem("z_decay_arg")
        decays = sem("z_decays")
        turns = sem("z_turns")
        turn_chain = sem("z_turn_chain")
        turns_reduced = sem("z_turns_reduced")
        rotations = sem("z_rotations")
        powers = sem("z_powers")
        summed = sem("z_summed")
        stored = sem("z_stored")
        blk = ctx.enter_context(nc.Block())

        @blk.gpsimd
        def _(pool):
            with pool.Fori(0, 2) as hf:
                for j in range(SLOTS):
                    pool.wait_ge(summed, hf * SLOTS + j + 1)
                    s = [P, CPC, P]
                    pool.tensor_tensor(Z[:, j], wide(m["decay"][:, bass.ds(hf * HALF + j * CPC, CPC)][:, :, None], s),
                                       wide(m["iota"][:, None, :], s), ALU.mult).then_inc(decay_arg, 1)

        @blk.scalar
        def _(act):
            with act.Fori(0, 2) as hf:
                for j in range(SLOTS):
                    act.wait_ge(decay_arg, hf * SLOTS + j + 1)
                    act.activation(Z[:, j], Z[:, j], ACT.Exp).then_inc(decays, 1)
                for j in range(SLOTS):
                    act.wait_ge(turns_reduced, hf * SLOTS + j + 1)
                    act.activation(A[:, j % 2], A[:, j % 2], ACT.Sin, bias=m["phase"][:, 0:1],
                                   scale=-TWO_PI).then_inc(rotations, 1)

        @blk.vector
        def _(dve):
            with dve.Fori(0, 2) as hf:
                def multiply(j):
                    dve.wait_ge(decays, hf * SLOTS + j + 1)
                    dve.wait_ge(rotations, hf * SLOTS + j + 1)
                    dve.tensor_tensor(Z[:, j], Z[:, j], A[:, j % 2], ALU.mult).then_inc(powers, 1)

                def store(j):
                    dve.wait_ge(summed, hf * SLOTS + SLOTS + j + 1)
                    h0 = hf * HALF + j * CPC
                    dst = HT[:, :, 0:TR].rearrange("p a (c h) -> p c a h", c=B)[:, :, :, bass.ds(h0, CPC)]
                    dve.tensor_copy(dst, PS[:, j % 4].rearrange("p (h c a) -> p c a h", c=B, a=DC)).then_inc(stored, 1)

                for j in range(SLOTS + 2):
                    if j < SLOTS:
                        dve.wait_ge(powers, hf * SLOTS + j + 1)
                        s = [P, CPC, P]
                        n = hf * 2 * SLOTS + 2 * j
                        dve.tensor_tensor(A[:, j % 2], wide(m["turn"][:, bass.ds(hf * HALF + j * CPC, CPC)][:, :, None], s),
                                          wide(m["iota"][:, None, :], s), ALU.mult).then_inc(turn_chain, 1)
                        dve.wait_ge(turn_chain, n + 1)
                        dve.tensor_scalar(K[:, j % 2], A[:, j % 2], m["quarter"][:, 0:1], ROUND, ALU.add, ALU.add).then_inc(turn_chain, 1)
                        dve.wait_ge(turn_chain, n + 2)
                        dve.scalar_tensor_tensor(A[:, j % 2].rearrange("p h b -> p (h b)"), K[:, j % 2].rearrange("p h b -> p (h b)"), ROUND,
                                                 A[:, j % 2].rearrange("p h b -> p (h b)"), ALU.subtract, ALU.subtract).then_inc(turns_reduced, 1)
                    if 1 <= j <= SLOTS:
                        multiply(j - 1)
                    if j >= 2:
                        store(j - 2)
            dve.wait_ge(stored, 2 * SLOTS + 4)

        @blk.tensor
        def _(pe):
            pe.sem_inc(summed, SLOTS)
            pe.sem_inc(stored, 4)
            pe.sem_inc(powers, 2)
            with pe.Fori(0, 2) as hf:
                for j in range(SLOTS):
                    pe.wait_ge(powers, hf * SLOTS + 2 + j + 1)
                    pe.wait_ge(stored, hf * SLOTS + j + 1)
                    for i in range(CPC):
                        last = pe.matmul(PS[:, j % 4, i * 32:(i + 1) * 32], Z[:, j, i],
                                         m["U"][:, hf * HALF + j * CPC + i].rearrange("p c a -> p (c a)"),
                                         start=True, stop=True)
                    last.then_inc(summed, 1)


def split_product(pe, out, terms):
    n = 0
    for w_hi, w_lo, x_hi, x_lo in terms:
        for w, v in ((w_hi, x_hi), (w_hi, x_lo), (w_lo, x_hi)):
            n += 1
            last = pe.matmul(out, w, v, start=n == 1, stop=n == 3 * len(terms))
    return last


def layernorm(nc, k, groups, XH, XL, tag, base=0, cls_copy=None):
    HT, PS = k["HT"], k["PS"]
    NGR = len(groups)
    with ExitStack() as ctx:
        sb = lambda n, s, d=F32: ctx.enter_context(nc.sbuf_tensor(tag + n, s, d))
        sem = signals(nc, ctx, tag)
        XC = sb("n_centred", [P, 2, DC, GRP])
        SQ = sb("n_squares", [P, 2, DC, GRP])
        VE = sb("n_var", [P, 2, GRP])
        RS = sb("n_rstd", [P, 2, GRP])
        RT = sb("n_newton", [P, 2, GRP])
        means = sem("n_means")
        centred = sem("n_centred_ready")
        squares = sem("n_squares_ready")
        variances = sem("n_variances")
        var_eps = sem("n_var_eps")
        guess = sem("n_guess")
        guess_sq = sem("n_guess_sq")
        dve_chain = sem("n_dve_chain")
        act_chain = sem("n_act_chain")
        normed = sem("n_normed")
        highs = sem("n_highs")
        lows = sem("n_lows")
        blk = ctx.enter_context(nc.Block())

        @blk.tensor
        def _(pe):
            for j in range(NGR + 1):
                if j < NGR:
                    c0, n = groups[j]
                    if j >= 2:
                        pe.wait_ge(centred, j - 1)
                    for a in range(DC):
                        last = pe.matmul(PS[:, j % 2, 0:n], k["mean_w"][:, :], HT[:, a, c0:c0 + n],
                                         start=a == 0, stop=a == DC - 1)
                    last.then_inc(means, 1)
                if j >= 1:
                    i = j - 1
                    n = groups[i][1]
                    pe.wait_ge(squares, i + 1)
                    if i >= 2:
                        pe.wait_ge(var_eps, i - 1)
                    for a in range(DC):
                        last = pe.matmul(PS[:, 2 + i % 2, 0:n], k["mean_w"][:, :], SQ[:, i % 2, a, 0:n],
                                         start=a == 0, stop=a == DC - 1)
                    last.then_inc(variances, 1)

        @blk.vector
        def _(dve):
            link = Chain(dve, dve_chain).link

            def centre(j):
                c0, n = groups[j]
                dve.wait_ge(means, j + 1)
                if j >= 2:
                    dve.wait_ge(lows, j - 1)
                dve.tensor_tensor(XC[:, j % 2, :, 0:n], HT[:, :, c0:c0 + n],
                                  wide(PS[:, j % 2, 0:n][:, None, :], [P, DC, n]), ALU.subtract).then_inc(centred, 1)

            def scale(j):
                c0, n = groups[j]
                ve, rs, rt = VE[:, j % 2, 0:n], RS[:, j % 2, 0:n], RT[:, j % 2, 0:n]
                dve.wait_ge(variances, j + 1)
                dve.tensor_scalar(ve, PS[:, 2 + j % 2, 0:n], EPS, None, ALU.add).then_inc(var_eps, 1)
                dve.wait_ge(guess_sq, j + 1)
                link(dve.tensor_tensor(rt, rt, ve, ALU.mult))
                link(dve.tensor_scalar(rt, rt, -0.5, 1.5, ALU.mult, ALU.add))
                link(dve.tensor_tensor(rs, rs, rt, ALU.mult))
                dve.tensor_tensor(XC[:, j % 2, :, 0:n], XC[:, j % 2, :, 0:n], wide(rs[:, None, :], [P, DC, n]),
                                  ALU.mult).then_inc(normed, 1)
                if c0 == TR and cls_copy is not None:
                    dve.wait_ge(normed, j + 1)
                    link(dve.tensor_copy(cls_copy, wide(XC[:, j % 2, :, 0:1], [P, DC, P])))

            for j in range(NGR + 1):
                if j < NGR:
                    centre(j)
                if j >= 1:
                    scale(j - 1)

        @blk.scalar
        def _(act):
            def high(j):
                c0, n = groups[j]
                act.wait_ge(normed, j + 1)
                act.copy(XH[:, :, c0 - base:c0 - base + n], XC[:, j % 2, :, 0:n]).then_inc(highs, 1)

            for j in range(NGR):
                n = groups[j][1]
                ve, rs, rt = VE[:, j % 2, 0:n], RS[:, j % 2, 0:n], RT[:, j % 2, 0:n]
                act.wait_ge(centred, j + 1)
                if j >= 2:
                    act.wait_ge(variances, j - 1)
                act.activation(SQ[:, j % 2, :, 0:n], XC[:, j % 2, :, 0:n], ACT.Square).then_inc(squares, 1)
                if j >= 1:
                    high(j - 1)
                act.wait_ge(var_eps, j + 1)
                act.activation(rs, ve, ACT.Ln).then_inc(act_chain, 1)
                act.wait_ge(act_chain, 2 * j + 1)
                act.activation(rs, rs, ACT.Exp, scale=-0.5).then_inc(act_chain, 1)
                act.wait_ge(act_chain, 2 * j + 2)
                act.activation(rt, rs, ACT.Square).then_inc(guess_sq, 1)
            high(NGR - 1)

        @blk.gpsimd
        def _(pool):
            for j in range(NGR):
                c0, n = groups[j]
                pool.wait_ge(highs, j + 1)
                pool.tensor_tensor(XL[:, :, c0 - base:c0 - base + n], XC[:, j % 2, :, 0:n],
                                   XH[:, :, c0 - base:c0 - base + n].bitcast(F32), ALU.subtract).then_inc(lows, 1)
            pool.wait_ge(lows, NGR)


def class_rows(nc, w_qkv, k, XB):
    XH, XL, PS = k["XH"], k["XL"], k["PS"]
    HD = HEADS * DH
    with ExitStack() as ctx:
        sb = lambda n, s, d=F32: ctx.enter_context(nc.sbuf_tensor(n, s, d))
        sem = signals(nc, ctx)
        WQ = sb("c_wq", [P, DC, HD])
        WK = sb("c_wk", [P, DC, HD])
        UQ = sb("c_u", [P, DC, P])
        UQH = sb("c_uh", [P, DC, P], F32R)
        UQL = sb("c_ul", [P, DC, P], F32R)
        SC = sb("c_scores", [P, B, NCH + 2])
        MX = sb("c_max", [P, B])
        RC = sb("c_sum", [P, B])
        load_q, load_k = sem("c_load_q"), sem("c_load_k")
        q_ready = sem("c_q_ready")
        dve_chain = sem("c_dve_chain")
        u_high = sem("c_u_high")
        u_ready = sem("c_u_ready")
        scored = sem("c_scored")
        scores_in = sem("c_scores_in")
        shifted = sem("c_shifted")
        exps = sem("c_exps")
        probs = sem("c_probs")
        highs = sem("c_highs")
        lows = sem("c_lows")
        blk = ctx.enter_context(nc.Block())

        @blk.sync
        def _(sp):
            sp.dma_start(WQ[:, :, :], w_qkv[:, 0:HD].rearrange("(a p) n -> p a n", p=P)).then_inc(load_q, 16)
            sp.dma_start(WK[:, :, :], w_qkv[:, HD:2 * HD].rearrange("(a p) n -> p a n", p=P)).then_inc(load_k, 16)

        @blk.tensor
        def _(pe):
            pe.wait_ge(load_q, 16)
            for n in range(DC):
                for a in range(DC):
                    last = pe.matmul(PS[:, 4 + n], XB[:, a], WQ[:, a, n * GRP:(n + 1) * GRP], start=a == 0, stop=a == DC - 1)
            last.then_inc(q_ready, 1)
            pe.wait_ge(u_ready, 1)
            for j, (c0, n) in enumerate(GROUPS):
                if j >= 4:
                    pe.wait_ge(scores_in, j - 3)
                split_product(pe, PS[:, j % 4, 0:n], [(UQH[:, a], UQL[:, a], XH[:, a, c0:c0 + n], XL[:, a, c0:c0 + n])
                                                      for a in range(DC)]).then_inc(scored, 1)

        @blk.vector
        def _(dve):
            link = Chain(dve, dve_chain).link
            link(dve.memset(UQ[:, :, :], 0.0))
            dve.wait_ge(q_ready, 1)
            dve.wait_ge(load_k, 16)
            for a in range(DC):
                link(dve.tensor_tensor(WK[:, a], WK[:, a], PS[:, 4:8].rearrange("p b n -> p (b n)"), ALU.mult))
                link(dve.reduce_sum(UQ[:, a, 0:HEADS], WK[:, a].rearrange("p (h d) -> p h d", h=HEADS), AX.X))
            link(dve.tensor_copy(UQH[:, :, :], UQ[:, :, :]))
            dve.tensor_tensor(UQL[:, :, :], UQ[:, :, :], UQH[:, :, :].bitcast(F32), ALU.subtract).then_inc(u_ready, 1)
            dve.wait_ge(scores_in, NG + 1)
            link(dve.reduce_max(MX[:, :], SC[:, :, 0:NCH + 1], AX.X))
            dve.tensor_tensor(SC[:, :, 0:NCH + 1], SC[:, :, 0:NCH + 1], wide(MX[:, :, None], [P, B, NCH + 1]),
                              ALU.subtract).then_inc(shifted, 1)
            dve.wait_ge(exps, 1)
            link(dve.reduce_sum(RC[:, :], SC[:, :, 0:NCH + 1], AX.X))
            link(dve.reciprocal(MX[:, :], RC[:, :]))
            dve.tensor_tensor(SC[:, :, :], SC[:, :, :], wide(MX[:, :, None], [P, B, NCH + 2]), ALU.mult).then_inc(probs, 1)
            dve.wait_ge(highs, 1)
            dve.tensor_tensor(k["PCL"][:, :, :], SC[:, :, :], k["PCH"][:, :, :].bitcast(F32), ALU.subtract).then_inc(lows, 1)
            dve.wait_ge(lows, 1)

        @blk.scalar
        def _(act):
            for j, (c0, n) in enumerate(GROUPS):
                act.wait_ge(scored, j + 1)
                if n == GRP:
                    act.copy(SC[:, 2 * j:2 * j + 2, 0:NCH], PS[:, j % 4].rearrange("p (b n) -> p b n", b=2)).then_inc(scores_in, 1)
                else:
                    act.copy(SC[:, :, NCH:NCH + 2], wide(PS[:, j % 4, 0:n][:, :, None], [P, B, 2])).then_inc(scores_in, 1)
            act.wait_ge(shifted, 1)
            act.activation(SC[:, :, 0:NCH + 1], SC[:, :, 0:NCH + 1], ACT.Exp, scale=SCALE).then_inc(exps, 1)
            act.wait_ge(probs, 1)
            act.copy(k["PCH"][:, :, :], SC[:, :, :]).then_inc(highs, 1)
            act.wait_ge(highs, 1)


def attention(nc, w_qkv, w_o, k):
    HT, XH, XL, PS = k["HT"], k["XH"], k["XL"], k["PS"]
    HD = HEADS * DH
    R = NCH + 2
    UNITS = 2 * NG
    ROUNDS = HEADS // 2
    OUTS = DC * (NG + 1)
    QB, KB, VB, CB, SB = 0, 1, 2, 3, 4
    PARTS = [(1, 0), (1, 1), (1, 2), (0, 3), (1, 3), (0, 0), (0, 1), (0, 2)]
    FIRST = [(0, 0), (0, 1), (0, 2)]
    NP, NF = len(PARTS), len(FIRST)
    PREP = {0: [0, 1], 1: [2, 3], 2: [4], 4: [5], 5: [6], 6: [7]}
    with ExitStack() as ctx:
        sb = lambda n, s, d=F32: ctx.enter_context(nc.sbuf_tensor(n, s, d))
        sem = signals(nc, ctx)
        RAW = sb("t_wraw", [P, 2, D])
        WH = sb("t_wh", [P, 2, 4, D], F32R)
        WL = sb("t_wl", [P, 2, 4, D], F32R)
        QH = sb("t_qh", [P, GRP], F32R)
        QL = sb("t_ql", [P, GRP], F32R)
        KH = sb("t_kh", [P, 2, R], F32R)
        KL = sb("t_kl", [P, 2, R], F32R)
        KVC = sb("t_kvc", [P, 2, 4])
        VS = sb("t_v", [P, 2, 2, NCH])
        E = sb("t_e", [P, 4, R])
        EPH = sb("t_eph", [P, 2, R], F32R)
        EPL = sb("t_epl", [P, 2, R], F32R)
        VT = sb("t_vt", [P, 2, NCH + 1])
        VTH = sb("t_vth", [P, 2, B, R], F32R)
        VTL = sb("t_vtl", [P, 2, B, R], F32R)
        SEL = sb("t_sel", [P, 2, P], F32R)
        ONES = sb("t_ones", [P, P], F32R)
        MX = sb("t_max", [P, 4])
        NB = sb("t_bias", [P, 4])
        RS = sb("t_rowsum", [P, 4])
        RC = sb("t_rowinv", [P, 4])
        loads = [sem("t_load0"), sem("t_load1")]
        wh, wl = sem("t_wh_ready"), sem("t_wl_ready")
        setup = sem("t_setup")
        sel_ready = sem("t_sel_ready")
        kvc_done, kvc_in = sem("t_kvc_done"), sem("t_kvc_in")
        q_done, k_done, v_done = sem("t_q_done"), sem("t_k_done"), sem("t_v_done")
        qh, ql, kh, kl, vs = sem("t_qh_ready"), sem("t_ql_ready"), sem("t_kh_ready"), sem("t_kl_ready"), sem("t_v_in")
        s_done, maxed, nmax, exps = sem("t_s_done"), sem("t_maxed"), sem("t_bias_ready"), sem("t_exps")
        inv, scaled, ep, eph, epl = sem("t_inv"), sem("t_scaled"), sem("t_ep"), sem("t_eph_ready"), sem("t_epl_ready")
        c_done, vt, vth, vtl = sem("t_c_done"), sem("t_vt_ready"), sem("t_vth_ready"), sem("t_vtl_ready")
        wo_done, hadd = sem("t_wo_done"), sem("t_hadd")
        blk = ctx.enter_context(nc.Block())

        def source(part, head):
            if part < 3:
                return w_qkv[:, bass.ds(head * DH + part * HD, DH)].rearrange("(a p) n -> p a n", p=P)
            return w_o[bass.ds(head * DH, DH), :]

        def raw(slot, part):
            return RAW[:, slot].rearrange("p (a n) -> p a n", a=DC) if part < 3 else RAW[:, slot]

        @blk.sync
        def _(sp):
            for x, (s, part) in enumerate(FIRST):
                if x >= 2:
                    sp.wait_ge(wl, x - 1)
                sp.dma_start(raw(x % 2, part), source(part, 0)).then_inc(loads[x % 2], 16)
            with sp.Fori(0, ROUNDS) as i:
                for x, (s, part) in enumerate(PARTS):
                    slot = (NF + x) % 2
                    head = (2 * i + 2) % HEADS if x >= NP - NF else 2 * i + s
                    sp.wait_ge(wl, i * NP + NF + x - 1)
                    sp.dma_start(raw(slot, part), source(part, head)).then_inc(loads[slot], 16)

        def loaded(eng, i, x):
            if i is None:
                eng.wait_ge(loads[x % 2], 16 * (x // 2 + 1))
            else:
                slot = (NF + x) % 2
                eng.wait_ge(loads[slot], i * 16 * NP // 2 + 16 * ((NF + x) // 2 + 1))

        def slot_free(eng, i, x):
            if x < 3:
                eng.wait_ge(v_done, i * UNITS + 1)
            elif x < 5:
                eng.wait_ge(wo_done, i * OUTS + 1)
            else:
                eng.wait_ge(v_done, i * UNITS + NG + 1)

        @blk.gpsimd
        def _(pool):
            def low(i, x, s, part):
                if i is None:
                    pool.wait_ge(wh, x + 1)
                    slot = x % 2
                else:
                    pool.wait_ge(wh, i * NP + NF + x + 1)
                    slot_free(pool, i, x)
                    slot = (NF + x) % 2
                pool.tensor_tensor(WL[:, s, part], RAW[:, slot], WH[:, s, part].bitcast(F32), ALU.subtract).then_inc(wl, 1)

            pool.memset(ONES[:, :].bitcast(F32), 1.0).then_inc(setup, 1)
            pool.memset(E[:, :, R - 1:R], 0.0).then_inc(setup, 1)
            for x, (s, part) in enumerate(FIRST):
                low(None, x, s, part)
            with pool.Fori(0, ROUNDS) as i:
                def value_low(u, b):
                    s, g = u // NG, u % NG
                    n = i * 2 * UNITS + 2 * u + b
                    pool.wait_ge(vth, n + 1)
                    pool.wait_ge(wo_done, i * OUTS + 1)
                    pool.tensor_tensor(VTL[:, s, 2 * g + b, 0:NCH + 1], VT[:, b], VTH[:, s, 2 * g + b, 0:NCH + 1].bitcast(F32),
                                       ALU.subtract).then_inc(vtl, 1)

                pool.wait_ge(c_done, i * 2 * UNITS + 2)
                for s in range(2):
                    pool.tensor_copy(SEL[:, s], wide(k["ident"][:, bass.ds(2 * i + s, 1)], [P, P])).then_inc(sel_ready, 1)
                for u in range(UNITS + 1):
                    for x in PREP.get(u, []):
                        low(i, x, *PARTS[x])
                    if u >= 1:
                        value_low(u - 1, 0)
                        value_low(u - 1, 1)

        @blk.scalar
        def _(act):
            def high(i, x, s, part):
                loaded(act, i, x)
                if i is not None:
                    slot_free(act, i, x)
                slot = x % 2 if i is None else (NF + x) % 2
                act.copy(WH[:, s, part], RAW[:, slot]).then_inc(wh, 1)

            act.wait_ge(setup, 2)
            for x, (s, part) in enumerate(FIRST):
                high(None, x, s, part)
            with act.Fori(0, ROUNDS) as i:
                def value_high(u, b):
                    s, g = u // NG, u % NG
                    act.wait_ge(vt, i * 2 * UNITS + 2 * u + b + 2)
                    act.wait_ge(wo_done, i * OUTS + 1)
                    act.copy(VTH[:, s, 2 * g + b, 0:NCH + 1], VT[:, b]).then_inc(vth, 1)

                for u in range(UNITS):
                    n = i * UNITS + u
                    for x in PREP.get(u, []):
                        high(i, x, *PARTS[x])
                    act.wait_ge(q_done, n + 1)
                    act.wait_ge(s_done, 4 * n + 1)
                    act.copy(QH[:, :], PS[:, QB]).then_inc(qh, 1)
                    if u % NG == 0:
                        act.wait_ge(kvc_done, i * 2 + u // NG + 1)
                        act.copy(KVC[:, u // NG], PS[:, KB, 0:4]).then_inc(kvc_in, 1)
                        act.wait_ge(kvc_in, i * 2 + u // NG + 1)
                        act.copy(KH[:, :, NCH:R], wide(KVC[:, u // NG, 0:1][:, :, None], [P, 2, 2]))
                    act.wait_ge(k_done, n + 1)
                    act.copy(KH[:, :, 0:NCH], PS[:, KB].rearrange("p (b n) -> p b n", b=2)).then_inc(kh, 1)
                    if u >= 1:
                        value_high(u - 1, 0)
                    act.wait_ge(v_done, n + 2)
                    act.copy(VS[:, u % 2], PS[:, VB].rearrange("p (b n) -> p b n", b=2)).then_inc(vs, 1)
                    if u >= 1:
                        value_high(u - 1, 1)

                    def exp(t):
                        act.wait_ge(nmax, 4 * n + t + 1)
                        act.wait_ge(epl, 2 * n + 1)
                        act.activation(E[:, t, 0:NCH + 1], PS[:, SB + t, 0:NCH + 1], ACT.Exp, bias=NB[:, t:t + 1],
                                       scale=SCALE, accum_out=RS[:, t:t + 1]).then_inc(exps, 1)

                    def high_probs(b):
                        act.wait_ge(ep, 2 * n + b + 1)
                        act.wait_ge(c_done, 2 * n + b + 1)
                        act.copy(EPH[:, b], E[:, 2 * b]).then_inc(eph, 1)

                    exp(0), exp(1), exp(2), high_probs(0), exp(3), high_probs(1)
                value_high(UNITS - 1, 0)
                value_high(UNITS - 1, 1)

        @blk.vector
        def _(dve):
            with dve.Fori(0, ROUNDS) as i:
                def values(u, b):
                    n = i * 2 * UNITS + 2 * u + b
                    dve.wait_ge(c_done, n + 3)
                    dve.wait_ge(vs, i * UNITS + u + 2)
                    dve.wait_ge(vtl, n + 1)
                    dve.tensor_tensor(VT[:, b, 0:NCH], VS[:, u % 2, b], PS[:, CB, 0:NCH], ALU.mult)
                    dve.tensor_tensor(VT[:, b, NCH:NCH + 1], KVC[:, u // NG, 2:3], PS[:, CB, NCH:NCH + 1], ALU.mult).then_inc(vt, 1)

                def add_output(j):
                    g, f = j // DC, j % DC
                    c0, n = GROUPS[g]
                    dve.wait_ge(wo_done, i * OUTS + j + 2)
                    dve.tensor_tensor(HT[:, f, c0:c0 + n], HT[:, f, c0:c0 + n], PS[:, j % 2, 0:n], ALU.add).then_inc(hadd, 1)

                for u in range(UNITS):
                    n = i * UNITS + u
                    dve.wait_ge(qh, n + 1)
                    dve.wait_ge(s_done, 4 * n + 1)
                    dve.tensor_tensor(QL[:, :], PS[:, QB], QH[:, :].bitcast(F32), ALU.subtract).then_inc(ql, 1)
                    dve.wait_ge(kh, n + 1)
                    if u % NG == 0:
                        dve.tensor_tensor(KL[:, :, NCH:R], wide(KVC[:, u // NG, 0:1][:, :, None], [P, 2, 2]), KH[:, :, NCH:R].bitcast(F32), ALU.subtract)
                    dve.tensor_tensor(KL[:, :, 0:NCH], PS[:, KB].rearrange("p (b n) -> p b n", b=2),
                                      KH[:, :, 0:NCH].bitcast(F32), ALU.subtract).then_inc(kl, 1)
                    if u >= 1:
                        values(u - 1, 0)
                        values(u - 1, 1)

                    def row_max(t):
                        dve.wait_ge(s_done, 4 * n + t + 2)
                        dve.reduce_max(MX[:, t:t + 1], PS[:, SB + t, 0:NCH + 1], AX.X).then_inc(maxed, 1)
                        dve.wait_ge(maxed, 4 * n + t + 1)
                        dve.tensor_scalar(NB[:, t:t + 1], MX[:, t:t + 1], -SCALE, None, ALU.mult).then_inc(nmax, 1)

                    def merge(b):
                        dve.wait_ge(exps, 4 * n + 2 * b + 2 + 4)
                        dve.reciprocal(RC[:, 2 * b:2 * b + 2], RS[:, 2 * b:2 * b + 2]).then_inc(inv, 1)
                        dve.wait_ge(inv, 2 * n + b + 1)
                        dve.tensor_scalar(E[:, 2 * b], E[:, 2 * b], RC[:, 2 * b:2 * b + 1], None, ALU.mult).then_inc(scaled, 1)
                        dve.wait_ge(scaled, 2 * n + b + 1)
                        dve.scalar_tensor_tensor(E[:, 2 * b], E[:, 2 * b + 1], RC[:, 2 * b + 1:2 * b + 2], E[:, 2 * b],
                                                 ALU.mult, ALU.add).then_inc(ep, 1)

                    def low_probs(b):
                        dve.wait_ge(eph, 2 * n + b + 1)
                        dve.tensor_tensor(EPL[:, b], E[:, 2 * b], EPH[:, b].bitcast(F32), ALU.subtract).then_inc(epl, 1)

                    row_max(0), row_max(1), row_max(2), merge(0), row_max(3), low_probs(0), merge(1), low_probs(1)
                for j in range(DC * (NG - 1)):
                    add_output(j)
                values(UNITS - 1, 0)
                values(UNITS - 1, 1)
                for j in range(DC * (NG - 1), OUTS):
                    add_output(j)
            dve.wait_ge(hadd, ROUNDS * OUTS + 1)

        @blk.tensor
        def _(pe):
            pe.sem_inc(exps, 4)
            pe.sem_inc(c_done, 2)
            pe.sem_inc(vtl, 2)
            for s in (epl, s_done, v_done, wo_done, hadd, kl, ql, vs, vt):
                pe.sem_inc(s, 1)
            pe.wait_ge(setup, 2)
            with pe.Fori(0, ROUNDS) as i:
                def project(u, part, bank, done):
                    s, g = u // NG, u % NG
                    c = slice(g * GRP, (g + 1) * GRP)
                    split_product(pe, PS[:, bank], [(WH[:, s, part, a * P:(a + 1) * P], WL[:, s, part, a * P:(a + 1) * P],
                                                     XH[:, a, c], XL[:, a, c]) for a in range(DC)]).then_inc(done, 1)

                def column_sums(u, b):
                    s, g = u // NG, u % NG
                    n = i * 2 * UNITS + 2 * u + b
                    pe.wait_ge(epl, n + 2)
                    pe.wait_ge(sel_ready, i * 2 + s + 1)
                    pe.wait_ge(vt, n + 1)
                    out = PS[:, CB, 0:R]
                    pe.matmul(out, ONES[:, :], EPH[:, b], start=True, stop=False)
                    pe.matmul(out, ONES[:, :], EPL[:, b], start=False, stop=False)
                    pe.matmul(out, SEL[:, s], k["PCH"][:, 2 * g + b], start=False, stop=False)
                    pe.matmul(out, SEL[:, s], k["PCL"][:, 2 * g + b], start=False, stop=True).then_inc(c_done, 1)

                def output(j):
                    g, f = j // DC, j % DC
                    c0, n = GROUPS[g]
                    last_unit = UNITS - 1 if g >= NG - 1 else NG + g
                    pe.wait_ge(vtl, i * 2 * UNITS + 2 * (last_unit + 1) + 2)
                    if j >= 2:
                        pe.wait_ge(hadd, i * OUTS + j - 1 + 1)
                    v = [(t[:, s, 2 * g:2 * g + 2, 0:NCH] if n == GRP else t[:, s, :, NCH]) for s in range(2) for t in (VTH, VTL)]
                    fs = slice(f * P, (f + 1) * P)
                    split_product(pe, PS[:, j % 2, 0:n], [(WH[:, s, 3, fs], WL[:, s, 3, fs], v[2 * s], v[2 * s + 1])
                                                          for s in range(2)]).then_inc(wo_done, 1)

                for u in range(UNITS):
                    n = i * UNITS + u
                    s = u // NG
                    if u % NG == 0:
                        pe.wait_ge(wl, i * NP + (NF if s == 0 else NF + 3))
                        pe.wait_ge(kl, n + 1)
                        if u == 0:
                            pe.wait_ge(hadd, i * OUTS + 1)
                        c = slice(TR, TR + 2)
                        for part in (1, 2):
                            last = split_product(pe, PS[:, KB, 2 * (part - 1):2 * part],
                                                 [(WH[:, s, part, a * P:(a + 1) * P], WL[:, s, part, a * P:(a + 1) * P],
                                                   XH[:, a, c], XL[:, a, c]) for a in range(DC)])
                        last.then_inc(kvc_done, 1)
                    pe.wait_ge(ql, n + 1)
                    project(u, 0, QB, q_done)
                    pe.wait_ge(kl, n + 1)
                    if u % NG == 0:
                        pe.wait_ge(kvc_in, i * 2 + s + 1)
                    project(u, 1, KB, k_done)
                    if u >= 1:
                        column_sums(u - 1, 0)
                    pe.wait_ge(vs, n + 1)
                    project(u, 2, VB, v_done)
                    if u >= 1:
                        column_sums(u - 1, 1)
                    pe.wait_ge(ql, n + 2)
                    pe.wait_ge(kl, n + 2)
                    for t in range(4):
                        b = t // 2
                        pe.wait_ge(exps, 4 * n + t + 1)
                        split_product(pe, PS[:, SB + t, 0:R], [(QH[:, t * P:(t + 1) * P], QL[:, t * P:(t + 1) * P],
                                                                KH[:, b], KL[:, b])]).then_inc(s_done, 1)
                pe.wait_ge(wl, i * NP + NF + 5)
                pe.wait_ge(kl, (i + 1) * UNITS + 1)
                for j in range(DC * (NG - 1)):
                    output(j)
                column_sums(UNITS - 1, 0)
                column_sums(UNITS - 1, 1)
                for j in range(DC * (NG - 1), OUTS):
                    output(j)


KH_ = 4
NK = 128
TOPK = 8
EXPERTS = 4096
ROWS_IN = EXPERTS // NK
EC = 512
CHUNKS = EXPERTS // EC
RPC = EC // NK


def key_scores(nc, w_q, keys, k, e, groups, base, tag):
    PS, XH, XL = k["PS"], e["XH"], e["XL"]
    tiles = [(g, t) for g, (c0, n) in enumerate(groups) for t in range(max(1, n // P))]
    rows = [min(P, groups[g][1]) for g, t in tiles]
    NGR = len(groups)
    with ExitStack() as ctx:
        sb = lambda n, s, d=F32: ctx.enter_context(nc.sbuf_tensor(tag + n, s, d))
        sem = signals(nc, ctx, tag)
        WR = sb("s_wraw", [P, DC, D])
        WH = sb("s_wh", [P, DC, D], F32R)
        WL = sb("s_wl", [P, DC, D], F32R)
        KR = sb("s_keys", [P, KH_, 2, NST])
        KT = sb("s_keys_t", [P, KH_, 2, NK])
        QF = sb("s_q", [P, 2, KH_, GRP])
        SF = sb("s_first", [P, 2, KH_, NK])
        TOP = sb("s_top", [P, 2, KH_, 2, TOPK])
        IDX = sb("s_index", [P, 2, KH_, TOPK], U32)
        BEYOND = sb("s_beyond", [P, 2, KH_, TOPK])
        CAND = sb("s_pairs", [P, KH_, TOPK, TOPK])
        CHOSEN = sb("s_chosen", [P, KH_, TOPK, TOPK])
        BEST = sb("s_best", [P, KH_, TOPK])
        load_w, load_k = sem("s_load_w"), sem("s_load_k")
        zeroed = sem("s_zeroed")
        w_high, w_low = sem("s_w_high"), sem("s_w_low")
        keys_t, keys_in = sem("s_keys_t_done"), sem("s_keys_in")
        q_done, q_in = sem("s_q_done"), sem("s_q_in")
        sims, sims_in, sims_read = sem("s_sims"), sem("s_sims_in"), sem("s_sims_read")
        dve_chain = sem("s_dve_chain")
        blk = ctx.enter_context(nc.Block())

        @blk.sync
        def _(sp):
            sp.dma_start(KR[:, :, :, :], keys.rearrange("h k j d -> k h j d")).then_inc(load_k, 16)
            sp.dma_start(WR[:, :, :], w_q.rearrange("(a p) n -> p a n", p=P)).then_inc(load_w, 16)

        @blk.gpsimd
        def _(pool):
            pool.memset(KT[:, :, :, :], 0.0).then_inc(zeroed, 1)
            pool.memset(e["EXT"][:, :, :], 0.0).then_inc(zeroed, 1)
            pool.memset(e["S1"][:, :, :, ROWS_IN:], 0.0).then_inc(zeroed, 1)
            pool.wait_ge(w_high, 1)
            pool.tensor_tensor(WL[:, :, :], WR[:, :, :], WH[:, :, :].bitcast(F32), ALU.subtract).then_inc(w_low, 1)
            pool.wait_ge(w_low, 1)

        @blk.tensor
        def _(pe):
            pe.wait_ge(load_k, 16)
            for h in range(KH_):
                last = pe.transpose(PS[:, 4, h * P:(h + 1) * P], KR[:, h].rearrange("p j d -> p (j d)"), k["ident"][:, :])
            last.then_inc(keys_t, 1)
            pe.wait_ge(w_low, 1)
            pe.wait_ge(keys_in, 2)
            for g, (c0, n) in enumerate(groups):
                for h in range(KH_):
                    if g:
                        pe.wait_ge(q_in, (g - 1) * KH_ + h + 1)
                    split_product(pe, PS[:, h, 0:n], [(WH[:, a, h * P:(h + 1) * P], WL[:, a, h * P:(h + 1) * P],
                                                       XH[:, a, c0 - base:c0 - base + n], XL[:, a, c0 - base:c0 - base + n])
                                                      for a in range(DC)]).then_inc(q_done, 1)
                pe.wait_ge(q_in, (g + 1) * KH_)
                for y, (gt, t) in enumerate(tiles):
                    if gt != g:
                        continue
                    if y >= 2:
                        pe.wait_ge(sims_in, y - 1)
                    for h in range(KH_):
                        last = pe.matmul(PS[0:rows[y], 4 + 2 * (y % 2) + h // 2, (h % 2) * 2 * NK:(h % 2 + 1) * 2 * NK],
                                         QF[:, g % 2, h, t * P:t * P + rows[y]], KT[:, h].rearrange("p j k -> p (j k)"),
                                         start=True, stop=True)
                    last.then_inc(sims, 1)

        def sim_rows(y):
            b = 4 + 2 * (y % 2)
            return PS[0:rows[y], b:b + 2].rearrange("p b (h j k) -> p (b h) j k", h=2, j=2)

        @blk.scalar
        def _(act):
            act.wait_ge(load_w, 16)
            act.copy(WH[:, :, :], WR[:, :, :]).then_inc(w_high, 1)

            def queries(g):
                n = groups[g][1]
                for h in range(KH_):
                    act.wait_ge(q_done, g * KH_ + h + 1)
                    act.copy(QF[:, g % 2, h, 0:n], PS[:, h, 0:n]).then_inc(q_in, 1)

            for g in range(NGR):
                queries(g)
                for y, (gt, t) in enumerate(tiles):
                    if gt == g:
                        act.wait_ge(sims, y + 1)
                        r = rows[y]
                        if y >= 2:
                            act.wait_ge(sims_read, y - 1)
                        act.copy(SF[0:r, y % 2], sim_rows(y)[:, :, 0, :])
                        act.copy(e["S2"][0:r, y], sim_rows(y)[:, :, 1, :]).then_inc(sims_in, 1)
            act.wait_ge(sims_in, len(tiles))

        @blk.vector
        def _(dve):
            link = Chain(dve, dve_chain).link
            dve.wait_ge(zeroed, 3)
            dve.wait_ge(keys_t, 1)
            for j in range(2):
                r = slice(j * NST, (j + 1) * NST)
                dve.tensor_copy(KT[r, :, j, :], PS[r, 4, :].rearrange("p (h k) -> p h k", h=KH_)).then_inc(keys_in, 1)
            for y in range(len(tiles)):
                r, p = rows[y], y % 2
                dve.wait_ge(sims_in, y + 1)
                dve.tensor_copy(e["S1"][0:r, y, :, 0:ROWS_IN], SF[0:r, p, :, 0:ROWS_IN])
                for h in range(KH_):
                    dve.max(out=TOP[0:r, p, h, 1], in_=e["S2"][0:r, y, h])
                    last = dve.max(out=TOP[0:r, p, h, 0], in_=SF[0:r, p, h])
                link(last)
                for h in range(KH_):
                    last = dve.max_index(out=IDX[0:r, p, h], in_max=TOP[0:r, p, h, 0], in_values=SF[0:r, p, h])
                last.then_inc(sims_read, 1)
                dve.wait_ge(sims_read, y + 1)
                dve.tensor_scalar(BEYOND[0:r, p], IDX[0:r, p], float(ROWS_IN), None, ALU.is_ge)
                s = [r, KH_, TOPK, TOPK]
                link(dve.tensor_tensor(CAND[0:r], wide(TOP[0:r, p, :, 0][:, :, :, None], s),
                                       wide(TOP[0:r, p, :, 1][:, :, None, :], s), ALU.add))
                for h in range(KH_):
                    last = dve.max(out=BEST[0:r, h], in_=CAND[0:r, h].rearrange("p a b -> p (a b)"))
                link(last)
                link(dve.tensor_scalar(e["TAU"][0:r, y], BEST[0:r, :, TOPK - 1], 0.0, None, ALU.max))
                f = "p h a b -> p h (a b)"
                link(dve.tensor_tensor(CHOSEN[0:r].rearrange(f), CAND[0:r].rearrange(f),
                                       wide(e["TAU"][0:r, y][:, :, None], [r, KH_, TOPK * TOPK]), ALU.is_ge))
                link(dve.tensor_tensor(CHOSEN[0:r], CHOSEN[0:r], CAND[0:r], ALU.mult))
                link(dve.tensor_tensor(CHOSEN[0:r], CHOSEN[0:r], wide(BEYOND[0:r, p][:, :, :, None], s), ALU.mult))
                link(dve.reduce_sum(e["EXT"][0:r, y, CHUNKS - 1:CHUNKS], CHOSEN[0:r].rearrange("p h a b -> p (h a b)"), AX.X))


def expert_layer(nc, e_down, e_up, k, e, groups, base, tag):
    PS, HT, XH, XL, S1, S2, TAU, EXT = (k["PS"], k["HT"], e["XH"], e["XL"], e["S1"], e["S2"], e["TAU"], e["EXT"])
    ET = EC // P
    NQ = 2 * len(groups)
    NZ = ET * NQ
    ROUNDS = CHUNKS // 2
    DB, GB, TB, OB = 0, 2, 3, 4
    count = [max(1, n // P) for _, n in groups]
    tiles = [range(sum(count[:g]), sum(count[:g + 1])) for g in range(len(groups))]
    assert groups[0][1] == groups[-1][1] == GRP and RPC == ET and NK == P
    with ExitStack() as ctx:
        sb = lambda n, s, d=F32: ctx.enter_context(nc.sbuf_tensor(tag + n, s, d))
        sem = signals(nc, ctx, tag)
        DR = sb("down_raw", [P, 2, D])
        UR = sb("up_raw", [P, 2, D])
        DH_ = sb("down_h", [P, 2, ET, DC, P], F32R)
        DL = sb("down_l", [P, 2, ET, DC, P], F32R)
        UH = sb("up_h", [P, 2, ET, D], F32R)
        UL = sb("up_l", [P, 2, ET, D], F32R)
        V = sb("v", [P, 2, GRP // P, KH_, P])
        G = sb("g", [P, 2, GRP // P, P])
        S = sb("silu", [P, 2, GRP])
        WF = sb("w", [P, 2, GRP])
        WH = sb("wh", [P, 2, GRP], F32R)
        WL = sb("wl", [P, 2, GRP], F32R)
        load_d, load_u = [sem("load_d0"), sem("load_d1")], [sem("load_u0"), sem("load_u1")]
        table_t, down_h, down_l, up_h, up_l = sem("table_t"), sem("down_hr"), sem("down_lr"), sem("up_hr"), sem("up_lr")
        sums, own_sums, chosen = sem("sums"), sem("own_sums"), sem("chosen")
        pool_chain, g_ready = sem("pool_chain"), sem("g_ready")
        d_done, t_done, silus, w_ready, w_high, w_low = (sem("d_done"), sem("t_done"), sem("silus"), sem("w_ready"),
                                                         sem("w_high"), sem("w_low"))
        up_done, added = sem("up_done"), sem("added")
        blk = ctx.enter_context(nc.Block())

        def item(z):
            q = z // ET
            return (q % NQ) // 2, q % 2 + 2 * (q // NQ), z % ET

        def table_at(z):
            return z if z < ET else z - (NZ - 2 * ET) if z >= NZ - ET else None

        def table_free(eng, i, x):
            eng.wait_ge(up_done, i * NZ + 2 + (0 if x < ET else NZ - 2 * ET + x % ET + 1))

        @blk.sync
        def _(sp):
            def load(x, chunk):
                r = bass.ds(chunk * EC + (x % ET) * P, P)
                sp.dma_start(DR[:, x % 2], e_down[r, :]).then_inc(load_d[x % 2], 16)
                sp.dma_start(UR[:, x % 2], e_up[r, :]).then_inc(load_u[x % 2], 16)

            for x in range(ET):
                if x >= 2:
                    sp.wait_ge(table_t, x - 1)
                    sp.wait_ge(up_l, x - 1)
                load(x, 0)
            with sp.Fori(0, ROUNDS) as i:
                for x in range(2 * ET):
                    sp.wait_ge(table_t, i * 2 * ET + ET + x - 1)
                    sp.wait_ge(up_l, i * 2 * ET + ET + x - 1)
                    load(x, 2 * i + 1 if x < ET else (2 * i + 2) % CHUNKS)

        def number(i, x):
            return x if i is None else i * 2 * ET + ET + x

        def arrived(eng, sems, i, x):
            eng.wait_ge(sems[x % 2], 16 * (x // 2 + 1) if i is None else i * 16 * ET + 16 * (ET // 2 + x // 2 + 1))

        def slot(i, x):
            return 0 if i is None or x >= ET else 1

        @blk.tensor
        def _(pe):
            for s, n in ((silus, 2), (w_ready, 2), (w_low, 2), (up_done, 2), (added, DC), (g_ready, 2), (t_done, 1)):
                pe.sem_inc(s, n)

            def table(i, x):
                arrived(pe, load_d, i, x)
                pe.wait_ge(down_l, number(i, x))
                for a in range(DC):
                    last = pe.transpose(PS[:, TB, a * P:(a + 1) * P], DR[:, x % 2, a * P:(a + 1) * P], k["ident"][:, :])
                last.then_inc(table_t, 1)

            for x in range(ET):
                table(None, x)
            with pe.Fori(0, ROUNDS) as i:
                def up(z):
                    g, s, j = item(z)
                    n = groups[g][1]
                    first, last_one = s == 0 and j == 0, s == 1 and j == ET - 1
                    pe.wait_ge(w_low, i * NZ + z + 3)
                    pe.wait_ge(up_l, i * 2 * ET + s * ET + j + 1)
                    for f in range(DC):
                        if first:
                            pe.wait_ge(added, DC * (i * NQ // 2 + g) + f + 1)
                        out = PS[:, OB + f, 0:n]
                        fs = slice(f * P, (f + 1) * P)
                        pe.matmul(out, UH[:, s, j, fs], WH[:, j % 2, 0:n], start=first, stop=False)
                        pe.matmul(out, UH[:, s, j, fs], WL[:, j % 2, 0:n], start=False, stop=False)
                        last = pe.matmul(out, UL[:, s, j, fs], WH[:, j % 2, 0:n], start=False, stop=last_one)
                    last.then_inc(up_done, 1)

                for z in range(NZ):
                    g, s, j = item(z)
                    c0, n = groups[g]

                    def weights_ready():
                        pe.wait_ge(g_ready, i * NZ + z + 3)
                        pe.wait_ge(w_ready, i * NZ + z + 2)

                    pe.wait_ge(down_l, i * 2 * ET + s * ET + j + 1)
                    pe.wait_ge(silus, i * NZ + z + 1)
                    if n < P:
                        weights_ready()
                    split_product(pe, PS[:, DB + j % 2, 0:n],
                                  [(DH_[:, s, j, a], DL[:, s, j, a], XH[:, a, c0 - base:c0 - base + n],
                                    XL[:, a, c0 - base:c0 - base + n]) for a in range(DC)]).then_inc(d_done, 1)
                    if n >= P:
                        weights_ready()
                    r = min(P, n)
                    for t in range(count[g]):
                        last = pe.transpose(PS[:, GB, t * P:t * P + r], G[0:r, j % 2, t], k["ident"][0:r, 0:r])
                    last.then_inc(t_done, 1)
                    if z:
                        up(z - 1)
                    if table_at(z) is not None:
                        table(i, table_at(z))
                up(NZ - 1)

        @blk.scalar
        def _(act):
            def table(i, x):
                act.wait_ge(table_t, number(i, x) + 1)
                if i is not None:
                    table_free(act, i, x)
                act.copy(DH_[:, slot(i, x), x % ET].rearrange("p a e -> p (a e)"), PS[:, TB]).then_inc(down_h, 1)
                arrived(act, load_u, i, x)
                act.copy(UH[:, slot(i, x), x % ET], UR[:, x % 2]).then_inc(up_h, 1)

            def pair_sums(done, z, chunk):
                g, s, j = item(z)
                r = min(P, groups[g][1])
                act.wait_ge(g_ready, done + 1)
                for t, y in enumerate(tiles[g]):
                    for h in range(KH_ - 1):
                        last = act.activation(V[0:r, j % 2, t, h], S2[0:r, y, h], ACT.Identity,
                                              bias=S1[0:r, y, h, bass.ds((chunk + s) * RPC + j, 1)])
                last.then_inc(sums, 1)

            for x in range(ET):
                table(None, x)
            for z in range(2):
                pair_sums(z, z, 0)
            with act.Fori(0, ROUNDS) as i:
                for z in range(NZ):
                    g, s, j = item(z)
                    n = groups[g][1]
                    done = i * NZ + z
                    act.wait_ge(d_done, done + 1)
                    act.wait_ge(w_ready, done + 1)
                    act.activation(S[:, j % 2, 0:n], PS[:, DB + j % 2, 0:n], ACT.Silu).then_inc(silus, 1)
                    pair_sums(done + 2, z + 2, 2 * i)
                    act.wait_ge(w_ready, done + 3)
                    act.wait_ge(up_done, done + 1)
                    act.copy(WH[:, j % 2, 0:n], WF[:, j % 2, 0:n]).then_inc(w_high, 1)
                    if table_at(z) is not None:
                        table(i, table_at(z))

        @blk.vector
        def _(dve):
            def table(i, x):
                dve.wait_ge(down_h, number(i, x) + 1)
                sl = slot(i, x)
                dve.tensor_tensor(DL[:, sl, x % ET].rearrange("p a e -> p (a e)"), PS[:, TB],
                                  DH_[:, sl, x % ET].rearrange("p a e -> p (a e)").bitcast(F32), ALU.subtract).then_inc(down_l, 1)

            def choose(done, z, chunk):
                g, s, j = item(z)
                r = min(P, groups[g][1])
                dve.wait_ge(g_ready, done + 1)
                for t, y in enumerate(tiles[g]):
                    last = dve.tensor_scalar(V[0:r, j % 2, t, KH_ - 1], S2[0:r, y, KH_ - 1],
                                             S1[0:r, y, KH_ - 1, bass.ds((chunk + s) * RPC + j, 1)], None, ALU.add)
                last.then_inc(own_sums, 1)
                dve.wait_ge(sums, done + 1)
                for h in range(KH_):
                    if h == KH_ - 1:
                        dve.wait_ge(own_sums, done + 1)
                    for t, y in enumerate(tiles[g]):
                        v = V[0:r, j % 2, t, h]
                        last = dve.scalar_tensor_tensor(v, v, TAU[0:r, y, h:h + 1], v, ALU.is_ge, ALU.mult)
                last.then_inc(chosen, 1)

            for x in range(ET):
                table(None, x)
            choose(0, 0, 0)
            with dve.Fori(0, ROUNDS) as i:
                def add(g):
                    c0, n = groups[g]
                    dve.wait_ge(up_done, i * NZ + (g + 1) * 2 * ET + 2)
                    for f in range(DC):
                        dve.tensor_tensor(HT[:, f, c0:c0 + n], HT[:, f, c0:c0 + n], PS[:, OB + f, 0:n], ALU.add).then_inc(added, 1)

                for z in range(NZ):
                    g, s, j = item(z)
                    n = groups[g][1]
                    done = i * NZ + z
                    if g and s == 0 and j == 1:
                        add(g - 1)
                    choose(done + 1, z + 1, 2 * i)
                    dve.wait_ge(silus, done + 3)
                    dve.wait_ge(t_done, done + 2)
                    dve.wait_ge(w_low, done + 1)
                    dve.tensor_tensor(WF[:, j % 2, 0:n], S[:, j % 2, 0:n], PS[:, GB, 0:n], ALU.mult).then_inc(w_ready, 1)
                    if table_at(z) is not None:
                        table(i, table_at(z))
                add(len(groups) - 1)
            dve.wait_ge(added, DC * (ROUNDS * NQ // 2 + 1))

        @blk.gpsimd
        def _(pool):
            def table(i, x):
                pool.wait_ge(up_h, number(i, x) + 1)
                sl = slot(i, x)
                pool.tensor_tensor(UL[:, sl, x % ET], UR[:, x % 2], UH[:, sl, x % ET].bitcast(F32), ALU.subtract).then_inc(up_l, 1)

            links = NZ + NZ // ET

            def add_heads(done, chained, z, chunk):
                g, s, j = item(z)
                r, nt = min(P, groups[g][1]), count[g]
                v = V[0:r, j % 2, 0:nt]
                pool.wait_ge(chosen, done + 1)
                pool.tensor_tensor(v[:, :, 0:2], v[:, :, 0:2], v[:, :, 2:4], ALU.add).then_inc(pool_chain, 1)
                pool.wait_ge(pool_chain, chained + 1)
                if j == ET - 1:
                    last = v[:, :, 0, P - 1:P]
                    pool.tensor_tensor(last, last, EXT[0:r, tiles[g][0]:tiles[g][0] + nt, bass.ds(chunk + s, 1)], ALU.add).then_inc(pool_chain, 1)
                    pool.wait_ge(pool_chain, chained + 2)
                pool.wait_ge(t_done, done)
                pool.tensor_tensor(G[0:r, j % 2, 0:nt], v[:, :, 0], v[:, :, 1], ALU.add).then_inc(g_ready, 1)

            for x in range(ET):
                table(None, x)
            pool.wait_ge(t_done, 1)
            add_heads(0, 0, 0, 0)
            with pool.Fori(0, ROUNDS) as i:
                for z in range(NZ):
                    g, s, j = item(z)
                    n = groups[g][1]
                    done = i * NZ + z
                    add_heads(done + 1, i * links + (z + 1) + (z + 1) // ET, z + 1, 2 * i)
                    pool.wait_ge(w_high, done + 1)
                    pool.tensor_tensor(WL[:, j % 2, 0:n], WF[:, j % 2, 0:n], WH[:, j % 2, 0:n].bitcast(F32), ALU.subtract).then_inc(w_low, 1)
                    if table_at(z) is not None:
                        table(i, table_at(z))
            pool.wait_ge(up_l, ROUNDS * 2 * ET + ET)
            pool.wait_ge(g_ready, ROUNDS * NZ + 3)


def store_tokens(nc, out, k):
    PS, HT = k["PS"], k["HT"]
    NT = TR // P
    OUTS = 4
    with ExitStack() as ctx:
        OUT = ctx.enter_context(nc.sbuf_tensor("o_rows", [P, OUTS, D], F32))
        sem = signals(nc, ctx)
        turned, copied = sem("o_turned"), sem("o_copied")
        stored = [sem(f"o_stored{n}") for n in range(OUTS)]
        blk = ctx.enter_context(nc.Block())

        @blk.tensor
        def _(pe):
            for y in range(NT + 1):
                r = P if y < NT else B
                if y >= 4:
                    pe.wait_ge(copied, y - 3)
                for f in range(DC):
                    last = pe.transpose(PS[0:r, y % 4, f * P:(f + 1) * P], HT[:, f, y * P:y * P + r], k["ident"][:, :])
                last.then_inc(turned, 1)

        @blk.vector
        def _(dve):
            for y in range(NT + 1):
                r = P if y < NT else B
                dve.wait_ge(turned, y + 1)
                if y >= OUTS:
                    dve.wait_ge(stored[y % OUTS], 16 * (y // OUTS))
                dve.tensor_copy(OUT[0:r, y % OUTS], PS[0:r, y % 4]).then_inc(copied, 1)

        @blk.sync
        def _(sp):
            for y in range(NT + 1):
                sp.wait_ge(copied, y + 1)
                c0 = y * P
                dst = out[c0 // NCH, 1 + c0 % NCH:1 + c0 % NCH + P, :] if y < NT else out[:, 0, :]
                sp.dma_start(dst, OUT[0:P if y < NT else B, y % OUTS]).then_inc(stored[y % OUTS], 16)
            for n in range(OUTS):
                sp.wait_ge(stored[n], 16 * ((NT + OUTS - n) // OUTS))


def tower(nc, x, cls_tok, log_dt, log_w_real, w_imag, w_qkv, w_o, w_q, keys, e_down, e_up, out):
    with ExitStack() as life:
        sb = lambda ctx, n, s, d=F32: ctx.enter_context(nc.sbuf_tensor(n, s, d))
        k = {"ident": sb(life, "ident", [P, P]), "mean_w": sb(life, "mean_w", [P, P]),
             "HT": sb(life, "tokens", [P, DC, T]),
             "PS": life.enter_context(nc.psum_tensor("psum", [P, 8, GRP], F32))}
        with ExitStack() as ctx:
            m = {"U": sb(ctx, "m_u", [P, NCH, B, DC]), "turn": sb(ctx, "m_turn", [P, NCH]),
                 "decay": sb(ctx, "m_decay", [P, NCH]), "phase": sb(ctx, "m_phase", [P, 1]),
                 "quarter": sb(ctx, "m_quarter", [P, 1]), "iota": sb(ctx, "m_iota", [P, P])}
            mixer_factors(nc, x, cls_tok, log_dt, log_w_real, w_imag, k, m)
            mixer_tokens(nc, k, m)
        with ExitStack() as ctx:
            k["XH"], k["XL"] = sb(ctx, "xh", [P, DC, T], F32R), sb(ctx, "xl", [P, DC, T], F32R)
            k["PCH"], k["PCL"] = sb(ctx, "class_ph", [P, B, NCH + 2], F32R), sb(ctx, "class_pl", [P, B, NCH + 2], F32R)
            with nc.sbuf_tensor("class_x", [P, DC, P], F32) as XB:
                layernorm(nc, k, [GROUPS[-1]] + GROUPS[:-1], k["XH"], k["XL"], "l1_", cls_copy=XB[:, :, :])
                class_rows(nc, w_qkv, k, XB)
            attention(nc, w_qkv, w_o, k)
        expert_halves(nc, w_q, keys, e_down, e_up, k)
        store_tokens(nc, out, k)


def expert_halves(nc, w_q, keys, e_down, e_up, k):
    for half, groups in enumerate((GROUPS[:NG // 2], [GROUPS[NG // 2], GROUPS[NG], GROUPS[NG // 2 + 1]])):
        with ExitStack() as ctx:
            sb = lambda n, s, d=F32: ctx.enter_context(nc.sbuf_tensor(f"h{half}_{n}", s, d))
            n = sum(n for _, n in groups)
            nt = sum(max(1, n // P) for _, n in groups)
            base = groups[0][0]
            e = {"XH": sb("xh", [P, DC, n], F32R), "XL": sb("xl", [P, DC, n], F32R),
                 "S1": sb("s1", [P, nt, KH_, ROWS_IN + RPC]), "S2": sb("s2", [P, nt, KH_, NK]),
                 "TAU": sb("tau", [P, nt, KH_]), "EXT": sb("beyond", [P, nt, CHUNKS + 1])}
            layernorm(nc, k, groups, e["XH"], e["XL"], f"l2{half}_", base)
            key_scores(nc, w_q, keys, k, e, groups, base, f"e{half}_")
            expert_layer(nc, e_down, e_up, k, e, groups, base, f"e{half}_")


def kernel(x, cls_tok, L0_tok_log_dt, L0_tok_log_w_real, L0_tok_w_imag, L0_attn_w_qkv, L0_attn_w_o,
           L0_ffn_Wq, L0_ffn_keys, L0_ffn_e_down, L0_ffn_e_up):
    import numpy as np
    import concourse.bacc as bacc
    from concourse.bass_utils import run_bass_kernel_spmd

    given = {"x": x, "cls_tok": cls_tok, "log_dt": L0_tok_log_dt, "log_w_real": L0_tok_log_w_real,
             "w_imag": L0_tok_w_imag, "w_qkv": L0_attn_w_qkv, "w_o": L0_attn_w_o, "w_q": L0_ffn_Wq,
             "keys": L0_ffn_keys, "e_down": L0_ffn_e_down, "e_up": L0_ffn_e_up}
    nc = bacc.Bacc("TRN2", target_bir_lowering=False, num_devices=1)
    arrays = {n: np.ascontiguousarray(a) for n, a in given.items()}
    ins = [nc.dram_tensor(n, a.shape, mybir.dt.from_np(a.dtype), kind="ExternalInput").ap() for n, a in arrays.items()]
    out = nc.dram_tensor("out", (B, NCH + 1, D), F32, kind="ExternalOutput").ap()
    tower(nc, *ins, out)
    r = run_bass_kernel_spmd(nc, [arrays], core_ids=[0])
    return r.results[0]["out"]
```

```python
import math
from contextlib import ExitStack

import concourse.bass as bass
from concourse import mybir

F32 = mybir.dt.float32
F32R = mybir.dt.float32r
I32 = mybir.dt.int32
U32 = mybir.dt.uint32
ALU = mybir.AluOpType
ACT = mybir.ActivationFunctionType
AX = mybir.AxisListType

P = 128
B = 8
NCH = 256
NST = 64
D = 512
DC = D // P
TR = B * NCH
T = TR + B
HEADS = 16
DH = 128
SCALE = DH ** -0.5
EPS = 1e-5
GRP = 512
NG = TR // GRP
GROUPS = [(g * GRP, GRP) for g in range(NG)] + [(TR, B)]

ROUND = 1.5 * 2.0 ** 23
TWO_PI = 6.283185
LN2_HI = 0.693145751953125
LN2_LO = 1.42860677e-06


class Chain:

    def __init__(self, eng, sem):
        self.eng, self.sem, self.n = eng, sem, 0

    def link(self, instruction):
        self.n += 1
        instruction.then_inc(self.sem, 1)
        self.eng.wait_ge(self.sem, self.n)


class Stage(ExitStack):

    def __init__(self):
        super().__init__()
        self.made = []


def signals(nc, ctx, tag=""):
    def clear():
        with nc.Block() as blk:
            @blk.sync
            def _(sp):
                for s in ctx.made:
                    sp.sem_clear(s)
        for s in ctx.made:
            nc.release_semaphore(s)

    def make(name):
        if not ctx.made:
            ctx.callback(clear)
        ctx.made.append(nc.alloc_semaphore(tag + name))
        return ctx.made[-1]

    return make


def wide(ap, shape):
    return ap.to_broadcast(list(shape))


def mixer_factors(nc, x, cls_tok, log_dt, log_w_real, w_imag, k, m):
    NA = DC - 1
    HN = 2 * NST
    CH = 16
    with Stage() as ctx:
        sb = lambda n, s, d=F32: ctx.enter_context(nc.sbuf_tensor(n, s, d))
        sem = signals(nc, ctx)
        Y = sb("a_logs", [P, 2 + HN])
        WI = sb("a_wimag", [P, HN])
        X = sb("a_x", [P, 2, B, NST, 2])
        KK = sb("a_k", [P, 2 + HN])
        RR = sb("a_r", [P, 2 + HN])
        EE = sb("a_e", [P, 2 + HN])
        II = sb("a_pow2", [P, 2 + HN], I32)
        EX = sb("a_exp", [P, 2 + HN])
        DR = sb("a_dr", [P, HN])
        DI = sb("a_di", [P, HN])
        TURN = sb("a_turn", [P, HN])
        T1 = sb("a_t1", [P, 3, HN])
        ANG = sb("a_ang", [P, 9, HN])
        SN = sb("a_sin", [P, 9, HN])
        ER = sb("a_er", [P, NA, HN])
        TH = sb("a_tanh", [P, HN])
        Q1 = sb("a_q1", [P, HN])
        Q2 = sb("a_q2", [P, HN])
        NR = sb("a_nr", [P, HN])
        NI = sb("a_ni", [P, HN])
        BR = sb("a_br", [P, 2, NST])
        BI = sb("a_bi", [P, 2, NST])
        CR = sb("a_cr", [P, 2, B, NST])
        CI = sb("a_ci", [P, 2, B, NST])
        C1 = sb("a_c1", [P, 2, B, NST])
        C2 = sb("a_c2", [P, 2, B, NST])
        PR = sb("a_pr", [P, NA, 2, NST])
        PI = sb("a_pi", [P, NA, 2, NST])
        NPR = sb("a_npr", [P, NA, 2, NST])
        M1 = sb("a_m1", [P, B, NA, NST])
        M2 = sb("a_m2", [P, B, NA, NST])
        M3 = sb("a_m3", [P, B, NA, NST])
        M4 = sb("a_m4", [P, B, NA, NST])
        UH = sb("a_uh", [P, 2, B, DC, NST, 2])
        DUP = sb("a_dup", [P, 5, NST, 2])
        IOT = sb("a_iota", [P, P], I32)
        CLS = sb("a_cls", [P, DC])
        PS = k["PS"]
        load_par = sem("a_load_par")
        load_x = sem("a_load_x")
        load_cls = sem("a_load_cls")
        ident_zero = sem("a_ident_zero")
        consts = sem("a_consts")
        iota_made = sem("a_iota_made")
        dve_chain = sem("a_dve_chain")
        args_ready = sem("a_args_ready")
        exps_ready = sem("a_exps_ready")
        sins_ready = sem("a_sins_ready")
        dup_ready = sem("a_dup_ready")
        u_ready = sem("a_u_ready")
        powers_ready = sem("a_powers_ready")
        pool_chain = sem("a_pool_chain")
        c_ready = sem("a_c_ready")
        u_real_ready = sem("a_u_real_ready")
        rows_t = sem("a_rows_t")
        u_t = sem("a_u_t")
        copied_v = sem("a_copied_v")
        copied_s = sem("a_copied_s")
        done = sem("a_done")
        blk = ctx.enter_context(nc.Block())

        @blk.sync
        def _(sp):
            sp.dma_start(Y[:, 0:2], log_dt.rearrange("(g p) -> p g", p=P), allow_slow_non_contiguous=True).then_inc(load_par, 16)
            sp.dma_start(Y[:, 2:].rearrange("p (g n) -> p g n", g=2),
                         log_w_real.rearrange("(g p) n -> p g n", p=P)).then_inc(load_par, 16)
            sp.dma_start(WI[:, :].rearrange("p (g n) -> p g n", g=2),
                         w_imag.rearrange("(g p) n -> p g n", p=P)).then_inc(load_par, 16)
            for g in range(2):
                sp.dma_start(X[:, g].rearrange("p c n r -> p c (n r)"),
                             x[:, g * P:(g + 1) * P].rearrange("c p n r -> p c (n r)")).then_inc(load_x, 16)
            sp.dma_start(CLS[:, :], cls_tok[0, 0, :].rearrange("(a p) -> p a", p=P), allow_slow_non_contiguous=True).then_inc(load_cls, 16)

        @blk.gpsimd
        def _(pool):
            pool.memset(k["ident"][:, :], 0.0).then_inc(ident_zero, 1)
            pool.iota(IOT[:, :], pattern=[[1, P]], base=0, channel_multiplier=0).then_inc(iota_made, 1)
            pool.memset(k["mean_w"][:, :], 1.0 / D).then_inc(consts, 1)
            pool.memset(DUP[:, 4, :, 0], 0.25).then_inc(consts, 1)
            pool.memset(DUP[:, 4, :, 1], 0.0).then_inc(consts, 1)
            pool.wait_ge(ident_zero, 1)
            pool.affine_select(out=k["ident"][:, :], in_=k["ident"][:, :], compare_op=ALU.not_equal, fill=1.0,
                               base=0, pattern=[[-1, P]], channel_multiplier=1).then_inc(consts, 1)
            pool.wait_ge(iota_made, 1)
            pool.tensor_copy(m["iota"][:, :], IOT[:, :]).then_inc(consts, 1)
            pool.wait_ge(load_cls, 16)
            pool.tensor_copy(k["HT"][:, :, TR:T], wide(CLS[:, :, None], [P, DC, B])).then_inc(consts, 1)
            pool.wait_ge(consts, 6)
            pool.wait_ge(load_x, 32)
            pool.wait_ge(powers_ready, 1)
            xr, xi = X[:, 1, :, :, 0], X[:, 1, :, :, 1]
            b_r, b_i = wide(BR[:, 1][:, None, :], [P, B, NST]), wide(BI[:, 1][:, None, :], [P, B, NST])
            pool.tensor_tensor(CR[:, 1], xr, b_r, ALU.mult).then_inc(pool_chain, 1)
            pool.tensor_tensor(C1[:, 1], xi, b_i, ALU.mult).then_inc(pool_chain, 1)
            pool.tensor_tensor(CI[:, 1], xr, b_i, ALU.mult).then_inc(pool_chain, 1)
            pool.tensor_tensor(C2[:, 1], xi, b_r, ALU.mult).then_inc(pool_chain, 1)
            pool.wait_ge(pool_chain, 4)
            pool.tensor_tensor(CR[:, 1], CR[:, 1], C1[:, 1], ALU.subtract).then_inc(c_ready, 1)
            pool.tensor_tensor(CI[:, 1], CI[:, 1], C2[:, 1], ALU.add).then_inc(c_ready, 1)
            pool.wait_ge(c_ready, 2)
            s = [P, B, NA, NST]
            pool.tensor_tensor(M3[:, :, :, :], wide(CR[:, 1][:, :, None, :], s), wide(PR[:, :, 1][:, None, :, :], s), ALU.mult).then_inc(pool_chain, 1)
            pool.tensor_tensor(M4[:, :, :, :], wide(CI[:, 1][:, :, None, :], s), wide(PI[:, :, 1][:, None, :, :], s), ALU.mult).then_inc(pool_chain, 1)
            pool.tensor_copy(UH[:, 1, :, 0, :, 0], CR[:, 1]).then_inc(u_real_ready, 1)
            pool.wait_ge(pool_chain, 6)
            pool.tensor_tensor(UH[:, 1, :, 1:, :, 0], M3[:, :, :, :], M4[:, :, :, :], ALU.subtract).then_inc(u_real_ready, 1)

        @blk.vector
        def _(dve):
            link = Chain(dve, dve_chain).link
            dve.wait_ge(load_par, 48)
            link(dve.tensor_scalar(KK[:, :], Y[:, :], 1 / math.log(2), ROUND, ALU.mult, ALU.add))
            link(dve.tensor_scalar(KK[:, :], KK[:, :], ROUND, -126.0, ALU.subtract, ALU.max))
            link(dve.tensor_scalar(KK[:, :], KK[:, :], 127.0, None, ALU.min))
            link(dve.scalar_tensor_tensor(RR[:, :], KK[:, :], -LN2_HI, Y[:, :], ALU.mult, ALU.add))
            link(dve.scalar_tensor_tensor(RR[:, :], KK[:, :], -LN2_LO, RR[:, :], ALU.mult, ALU.add))
            link(dve.tensor_scalar(EE[:, :], RR[:, :], 1 / 5040, None, ALU.mult))
            for c in (1 / 720, 1 / 120, 1 / 24, 1 / 6, 0.5, 1.0):
                link(dve.scalar_tensor_tensor(EE[:, :], EE[:, :], c, RR[:, :], ALU.add, ALU.mult))
            link(dve.tensor_scalar(II[:, :], KK[:, :], 127.0, 2.0 ** 23, ALU.add, ALU.mult))
            link(dve.scalar_tensor_tensor(EX[:, :], EE[:, :], 1.0, II[:, :].bitcast(F32), ALU.add, ALU.mult))
            WR = EX[:, 2:]
            for g in range(2):
                s = slice(g * NST, (g + 1) * NST)
                dve.tensor_scalar(DR[:, s], EX[:, 2 + g * NST:2 + (g + 1) * NST], EX[:, g:g + 1], -1.0,
                                  ALU.mult, ALU.mult)
                link(dve.tensor_scalar(DI[:, s], WI[:, s], EX[:, g:g + 1], None, ALU.mult))
            for a in range(NA):
                dve.tensor_scalar(ER[:, a], DR[:, :], float(P * (a + 1)), None, ALU.mult).then_inc(args_ready, 1)
            link(dve.tensor_scalar(TURN[:, :], DI[:, :], 1 / (2 * math.pi), None, ALU.mult))
            link(dve.tensor_scalar(T1[:, 0], TURN[:, :], ROUND, ROUND, ALU.add, ALU.subtract))
            link(dve.tensor_tensor(ANG[:, 0], TURN[:, :], T1[:, 0], ALU.subtract))
            link(dve.tensor_scalar(TURN[:, :], TURN[:, :], 0.5, None, ALU.mult))
            link(dve.tensor_scalar(T1[:, 0], TURN[:, :], ROUND, ROUND, ALU.add, ALU.subtract))
            link(dve.tensor_tensor(ANG[:, 2], TURN[:, :], T1[:, 0], ALU.subtract))
            for a in range(NA):
                last = dve.tensor_scalar(ANG[:, 3 + a], ANG[:, 0], float(P * (a + 1)), None, ALU.mult)
            link(last)
            link(dve.tensor_scalar(T1[:, :], ANG[:, 3:6], ROUND, ROUND, ALU.add, ALU.subtract))
            link(dve.tensor_tensor(ANG[:, 3:6], ANG[:, 3:6], T1[:, :], ALU.subtract))
            dve.tensor_scalar(ANG[:, 1], ANG[:, 0], 0.25, None, ALU.add)
            link(dve.tensor_scalar(ANG[:, 6:9], ANG[:, 3:6], 0.25, None, ALU.add))
            dve.tensor_scalar(T1[:, 0], ANG[:, 1], ROUND, ROUND, ALU.add, ALU.subtract)
            link(dve.tensor_scalar(SN[:, 0:3], ANG[:, 6:9], ROUND, ROUND, ALU.add, ALU.subtract))
            dve.tensor_tensor(ANG[:, 1], ANG[:, 1], T1[:, 0], ALU.subtract).then_inc(args_ready, 1)
            dve.tensor_tensor(ANG[:, 6:9], ANG[:, 6:9], SN[:, 0:3], ALU.subtract).then_inc(args_ready, 1)
            for g in range(2):
                dve.tensor_copy(DUP[:, g], wide(ANG[:, 0, g * NST:(g + 1) * NST][:, :, None], [P, NST, 2])).then_inc(dup_ready, 1)
                dve.tensor_copy(DUP[:, 2 + g], wide(DR[:, g * NST:(g + 1) * NST][:, :, None], [P, NST, 2])).then_inc(dup_ready, 1)
            dve.wait_ge(exps_ready, 1)
            link(dve.tensor_scalar(Q1[:, :], TH[:, :], -1.0, 1.0, ALU.mult, ALU.add))
            link(dve.reciprocal(Q2[:, :], Q1[:, :]))
            link(dve.scalar_tensor_tensor(Q1[:, :], TH[:, :], 2.0, Q2[:, :], ALU.mult, ALU.mult))
            dve.wait_ge(sins_ready, 1)
            link(dve.scalar_tensor_tensor(Q2[:, :], SN[:, 2], -2.0, SN[:, 2], ALU.mult, ALU.mult))
            link(dve.tensor_tensor(NR[:, :], Q1[:, :], SN[:, 1], ALU.mult))
            link(dve.tensor_tensor(NR[:, :], NR[:, :], Q2[:, :], ALU.add))
            link(dve.scalar_tensor_tensor(NI[:, :], Q1[:, :], 1.0, SN[:, 0], ALU.add, ALU.mult))
            link(dve.tensor_tensor(Q1[:, :], WR, WR, ALU.mult))
            link(dve.tensor_tensor(Q2[:, :], WI[:, :], WI[:, :], ALU.mult))
            link(dve.tensor_tensor(Q1[:, :], Q1[:, :], Q2[:, :], ALU.add))
            link(dve.reciprocal(Q2[:, :], Q1[:, :]))
            br = BR[:, :, :].rearrange("p g n -> p (g n)")
            bi = BI[:, :, :].rearrange("p g n -> p (g n)")
            dve.tensor_tensor(T1[:, 0], NI[:, :], WI[:, :], ALU.mult)
            link(dve.tensor_tensor(T1[:, 1], NR[:, :], WR, ALU.mult))
            link(dve.tensor_tensor(T1[:, 0], T1[:, 0], T1[:, 1], ALU.subtract))
            link(dve.scalar_tensor_tensor(br, T1[:, 0], 2.0, Q2[:, :], ALU.mult, ALU.mult))
            dve.tensor_tensor(T1[:, 0], NI[:, :], WR, ALU.mult)
            link(dve.tensor_tensor(T1[:, 1], NR[:, :], WI[:, :], ALU.mult))
            link(dve.tensor_tensor(T1[:, 0], T1[:, 0], T1[:, 1], ALU.add))
            link(dve.scalar_tensor_tensor(bi, T1[:, 0], -2.0, Q2[:, :], ALU.mult, ALU.mult))
            em = ER[:, :, :]
            pr = PR[:, :, :, :].rearrange("p a g n -> p a (g n)")
            pi = PI[:, :, :, :].rearrange("p a g n -> p a (g n)")
            npr = NPR[:, :, :, :].rearrange("p a g n -> p a (g n)")
            link(dve.tensor_tensor(pr, em, SN[:, 6:9], ALU.mult))
            dve.tensor_tensor(pi, em, SN[:, 3:6], ALU.mult).then_inc(powers_ready, 1)
            link(dve.tensor_scalar(npr, pr, -1.0, None, ALU.mult))
            dve.wait_ge(load_x, 32)
            xr, xi = X[:, 0, :, :, 0], X[:, 0, :, :, 1]
            b_r, b_i = wide(BR[:, 0][:, None, :], [P, B, NST]), wide(BI[:, 0][:, None, :], [P, B, NST])
            dve.tensor_tensor(CR[:, 0], xr, b_r, ALU.mult)
            dve.tensor_tensor(C1[:, 0], xi, b_i, ALU.mult)
            dve.tensor_tensor(CI[:, 0], xr, b_i, ALU.mult)
            link(dve.tensor_tensor(C2[:, 0], xi, b_r, ALU.mult))
            dve.tensor_tensor(CR[:, 0], CR[:, 0], C1[:, 0], ALU.subtract)
            link(dve.tensor_tensor(CI[:, 0], CI[:, 0], C2[:, 0], ALU.add))
            for g in range(2):
                s = [P, B, NA, NST]
                cr, ci = wide(CR[:, g][:, :, None, :], s), wide(CI[:, g][:, :, None, :], s)
                p_r, p_i, np_r = (wide(t[:, :, g][:, None, :, :], s) for t in (PR, PI, NPR))
                if g:
                    dve.wait_ge(u_ready, 1)
                    dve.wait_ge(c_ready, 2)
                else:
                    dve.tensor_copy(UH[:, g, :, 0, :, 0], CR[:, g])
                    dve.tensor_tensor(M1[:, :, :, :], cr, p_r, ALU.mult)
                    link(dve.tensor_tensor(M2[:, :, :, :], ci, p_i, ALU.mult))
                    link(dve.tensor_tensor(UH[:, g, :, 1:, :, 0], M1[:, :, :, :], M2[:, :, :, :], ALU.subtract))
                dve.tensor_scalar(UH[:, g, :, 0, :, 1], CI[:, g], -1.0, None, ALU.mult)
                dve.tensor_tensor(M1[:, :, :, :], ci, np_r, ALU.mult)
                link(dve.tensor_tensor(M2[:, :, :, :], cr, p_i, ALU.mult))
                dve.tensor_tensor(UH[:, g, :, 1:, :, 1], M1[:, :, :, :], M2[:, :, :, :], ALU.subtract).then_inc(u_ready, 1)
            dve.wait_ge(rows_t, 5)
            dve.tensor_copy(m["turn"][:, :], PS[:, 0, 0:NCH]).then_inc(done, 1)
            dve.tensor_copy(m["decay"][:, :], PS[:, 0, NCH:2 * NCH]).then_inc(done, 1)
            dve.tensor_copy(m["quarter"][:, :], PS[:, 1, 0:1]).then_inc(done, 1)
            dve.tensor_scalar(m["phase"][:, :], PS[:, 1, 0:1], TWO_PI, None, ALU.mult).then_inc(done, 1)
            for i in range(0, CH, 2):
                g, c = i // B, i % B
                dve.wait_ge(u_t, i + 1)
                dve.tensor_copy(m["U"][:, g * P:(g + 1) * P, c, :],
                                PS[:, 2 + i % 6, :].rearrange("p (a h) -> p h a", a=DC)).then_inc(copied_v, 1)
            dve.wait_ge(copied_v, CH // 2)
            dve.wait_ge(done, 4)

        @blk.scalar
        def _(act):
            act.wait_ge(args_ready, 3)
            act.activation(TH[:, :], DR[:, :], ACT.Tanh, scale=0.5).then_inc(exps_ready, 1)
            act.activation(ER[:, :, :], ER[:, :, :], ACT.Exp)
            act.wait_ge(args_ready, 5)
            act.activation(SN[:, :, :], ANG[:, :, :], ACT.Sin, scale=TWO_PI).then_inc(sins_ready, 1)
            for i in range(1, CH, 2):
                g, c = i // B, i % B
                act.wait_ge(u_t, i + 1)
                act.copy(m["U"][:, g * P:(g + 1) * P, c, :],
                         PS[:, 2 + i % 6, :].rearrange("p (a h) -> p h a", a=DC)).then_inc(copied_s, 1)
            act.wait_ge(copied_s, CH // 2)

        @blk.tensor
        def _(pe):
            pe.wait_ge(consts, 6)
            pe.wait_ge(dup_ready, 4)
            for i in range(4):
                pe.transpose(PS[:, 0, i * P:(i + 1) * P], DUP[:, i].rearrange("p n r -> p (n r)"), k["ident"][:, :]).then_inc(rows_t, 1)
            pe.transpose(PS[:, 1, 0:P], DUP[:, 4].rearrange("p n r -> p (n r)"), k["ident"][:, :]).then_inc(rows_t, 1)
            for i in range(CH):
                g, c = i // B, i % B
                pe.wait_ge(u_ready, g + 1)
                if g:
                    pe.wait_ge(u_real_ready, 2)
                if i >= 6:
                    pe.wait_ge(copied_s if i % 2 else copied_v, (i - 6) // 2 + 1)
                for a in range(DC):
                    last = pe.transpose(PS[:, 2 + i % 6, a * P:(a + 1) * P],
                                        UH[:, g, c, a].rearrange("p n r -> p (n r)"), k["ident"][:, :])
                last.then_inc(u_t, 1)


def mixer_tokens(nc, k, m):
    CPC = 16
    SLOTS = 8
    HALF = CPC * SLOTS
    PS, HT = k["PS"], k["HT"]
    with Stage() as ctx:
        sb = lambda n, s, d=F32: ctx.enter_context(nc.sbuf_tensor(n, s, d))
        sem = signals(nc, ctx)
        Z = sb("z_pow", [P, SLOTS, CPC, P])
        AS = 4
        A = sb("z_turn", [P, AS, CPC, P])
        K = sb("z_round", [P, 2, CPC, P])
        decay_arg = sem("z_decay_arg")
        decays = sem("z_decays")
        turns = sem("z_turns")
        turn_chain = sem("z_turn_chain")
        turns_reduced = sem("z_turns_reduced")
        pool_turns = sem("z_pool_turns")
        first_args = sem("z_first_args")
        rotations = sem("z_rotations")
        powers = sem("z_powers")
        summed = sem("z_summed")
        stored = sem("z_stored")
        blk = ctx.enter_context(nc.Block())

        QUARTER = SLOTS // 2
        DVE_TURNS = (0, 4)
        assert AS == QUARTER

        @blk.gpsimd
        def _(pool):
            def argument(j, done, h0):
                pool.wait_ge(summed, done)
                s = [P, CPC, P]
                pool.tensor_tensor(Z[:, j], wide(m["decay"][:, bass.ds(h0, CPC)][:, :, None], s),
                                   wide(m["iota"][:, None, :], s), ALU.mult).then_inc(decay_arg, 1)

            def turn(j, n, h0):
                pool.wait_ge(powers, n)
                s = [P, CPC, P]
                pool.tensor_tensor(A[:, j % AS], wide(m["turn"][:, bass.ds(h0, CPC)][:, :, None], s),
                                   wide(m["iota"][:, None, :], s), ALU.mult).then_inc(pool_turns, 1)

            for j in range(QUARTER):
                if j not in DVE_TURNS:
                    turn(j, j + 1, j * CPC)
                if j < QUARTER // 2:
                    argument(j, j + 1, j * CPC)
            with pool.Fori(0, 2) as hf:
                for j in range(SLOTS):
                    x, half = (j + QUARTER) % SLOTS, hf if j < QUARTER else (hf + 1) % 2
                    argument(x, hf * SLOTS + j + QUARTER + 1, half * HALF + x * CPC)
                    if x not in DVE_TURNS:
                        turn(x, hf * SLOTS + j + QUARTER + 1, half * HALF + x * CPC)
            pool.wait_ge(decays, 2 * SLOTS + QUARTER)
            pool.wait_ge(pool_turns, 2 * (SLOTS - len(DVE_TURNS)) + QUARTER - len(DVE_TURNS) // 2)

        @blk.scalar
        def _(act):
            def decay(j, n, args=decay_arg):
                act.wait_ge(args, n)
                act.activation(Z[:, j], Z[:, j], ACT.Exp).then_inc(decays, 1)

            def rotation(j, n):
                act.wait_ge(turns_reduced, n)
                act.activation(A[:, j % AS], A[:, j % AS], ACT.Sin, bias=m["phase"][:, 0:1], scale=-TWO_PI).then_inc(rotations, 1)

            for j in range(QUARTER // 2):
                decay(j + QUARTER // 2, j + 1, first_args)
            for j in range(QUARTER // 2):
                decay(j, j + 1)
            with act.Fori(0, 2) as hf:
                def store(j):
                    act.wait_ge(summed, hf * SLOTS + SLOTS + j + 1)
                    h0 = hf * HALF + j * CPC
                    dst = HT[:, :, 0:TR].rearrange("p a (c h) -> p c a h", c=B)[:, :, :, bass.ds(h0, CPC)]
                    act.copy(dst, PS[:, j % 4].rearrange("p (h c a) -> p c a h", c=B, a=DC)).then_inc(stored, 1)

                for q in range(2):
                    for j in range(q * QUARTER, (q + 1) * QUARTER):
                        rotation(j, hf * SLOTS + j + 1)
                        if j >= 2:
                            store(j - 2)
                    for j in range(QUARTER):
                        decay(j + QUARTER * (1 - q), hf * SLOTS + q * QUARTER + QUARTER // 2 + j + 1)
                store(SLOTS - 2)
                store(SLOTS - 1)
            act.wait_ge(stored, 2 * SLOTS + 4)

        @blk.vector
        def _(dve):
            for j in range(QUARTER // 2, QUARTER):
                s = [P, CPC, P]
                dve.tensor_tensor(Z[:, j], wide(m["decay"][:, j * CPC:(j + 1) * CPC][:, :, None], s),
                                  wide(m["iota"][:, None, :], s), ALU.mult).then_inc(first_args, 1)
            with dve.Fori(0, 2) as hf:
                def multiply(j):
                    dve.wait_ge(decays, hf * SLOTS + j + 1)
                    dve.wait_ge(rotations, hf * SLOTS + j + 1)
                    dve.tensor_tensor(Z[:, j], Z[:, j], A[:, j % AS], ALU.mult).then_inc(powers, 1)

                for j in range(SLOTS + 1):
                    if j < SLOTS:
                        s = [P, CPC, P]
                        n = hf * (SLOTS + len(DVE_TURNS)) + j + sum(x < j for x in DVE_TURNS)
                        if j in DVE_TURNS:
                            dve.wait_ge(powers, hf * SLOTS + j + 1)
                            dve.tensor_tensor(A[:, j % AS], wide(m["turn"][:, bass.ds(hf * HALF + j * CPC, CPC)][:, :, None], s),
                                              wide(m["iota"][:, None, :], s), ALU.mult).then_inc(turn_chain, 1)
                            n = n + 1
                            dve.wait_ge(turn_chain, n)
                        else:
                            dve.wait_ge(pool_turns, hf * (SLOTS - len(DVE_TURNS)) + j + 1 - sum(x < j for x in DVE_TURNS))
                        dve.tensor_scalar(K[:, j % 2], A[:, j % AS], m["quarter"][:, 0:1], ROUND, ALU.add, ALU.add).then_inc(turn_chain, 1)
                        dve.wait_ge(turn_chain, n + 1)
                        dve.scalar_tensor_tensor(A[:, j % AS].rearrange("p h b -> p (h b)"), K[:, j % 2].rearrange("p h b -> p (h b)"), ROUND,
                                                 A[:, j % AS].rearrange("p h b -> p (h b)"), ALU.subtract, ALU.subtract).then_inc(turns_reduced, 1)
                    if j >= 1:
                        multiply(j - 1)
            dve.wait_ge(powers, 2 * SLOTS + AS)

        @blk.tensor
        def _(pe):
            pe.sem_inc(summed, SLOTS)
            pe.sem_inc(stored, 4)
            pe.sem_inc(powers, AS)
            with pe.Fori(0, 2) as hf:
                for j in range(SLOTS):
                    pe.wait_ge(powers, hf * SLOTS + AS + j + 1)
                    pe.wait_ge(stored, hf * SLOTS + j + 1)
                    for i in range(CPC):
                        last = pe.matmul(PS[:, j % 4, i * 32:(i + 1) * 32], Z[:, j, i],
                                         m["U"][:, hf * HALF + j * CPC + i].rearrange("p c a -> p (c a)"),
                                         start=True, stop=True)
                    last.then_inc(summed, 1)


def split_product(pe, out, terms):
    n = 0
    for w_hi, w_lo, x_hi, x_lo in terms:
        for w, v in ((w_hi, x_hi), (w_hi, x_lo), (w_lo, x_hi)):
            n += 1
            last = pe.matmul(out, w, v, start=n == 1, stop=n == 3 * len(terms))
    return last


def layernorm(nc, ctx, blk, k, groups, XH, XL, tag, at, cls_copy=None, spread=False, beside=None, bank=0):
    HT, PS = k["HT"], k["PS"]
    NGR = len(groups)
    XCS = 3
    sb = lambda n, s, d=F32: ctx.enter_context(nc.sbuf_tensor(tag + n, s, d))
    sem = signals(nc, ctx, tag)
    XC = sb("n_centred", [P, XCS, DC, GRP])
    SQ = sb("n_squares", [P, 2, DC, GRP])
    VE = sb("n_var", [P, 2, GRP])
    RS = sb("n_rstd", [P, 2, GRP])
    RT = sb("n_newton", [P, 2, GRP])
    means = sem("n_means")
    centred = sem("n_centred_ready")
    squares = sem("n_squares_ready")
    variances = sem("n_variances")
    var_eps = sem("n_var_eps")
    guess = sem("n_guess")
    guess_sq = sem("n_guess_sq")
    dve_chain = sem("n_dve_chain")
    act_chain = sem("n_act_chain")
    normed = sem("n_normed")
    highs = sem("n_highs")
    lows = sem("n_lows")
    zeroed = sem("n_zeroed")
    if spread:
        XW = sb("n_spread", [P, DC, P // 32, 32])

    def result(j):
        n = groups[j][1]
        if spread and n < P:
            return XW[:, :, :, :].rearrange("p a j c -> p a (j c)"), slice(at[j], at[j] + P)
        return XC[:, j % XCS, :, 0:n], slice(at[j], at[j] + n)

    if beside:
        @blk.sync
        def _(sp):
            beside.sync(sp)

    @blk.tensor
    def _(pe):
        def mean(j):
            c0, n = groups[j]
            if j >= 2:
                pe.wait_ge(centred, j - 1)
            for a in range(DC):
                last = pe.matmul(PS[:, bank + j % 2, 0:n], k["mean_w"][:, :], HT[:, a, c0:c0 + n], start=a == 0, stop=a == DC - 1)
            last.then_inc(means, 1)

        def variance(j):
            n = groups[j][1]
            pe.wait_ge(squares, j + 1)
            if j >= 2:
                pe.wait_ge(var_eps, j - 1)
            for a in range(DC):
                last = pe.matmul(PS[:, bank + 2 + j % 2, 0:n], k["mean_w"][:, :], SQ[:, j % 2, a, 0:n], start=a == 0, stop=a == DC - 1)
            last.then_inc(variances, 1)

        mean(0), mean(1), variance(0)
        for j in range(NGR):
            if j + 2 < NGR:
                mean(j + 2)
            if j + 1 < NGR:
                variance(j + 1)
            if beside:
                beside.tensor(pe, j)

    @blk.vector
    def _(dve):
        link = Chain(dve, dve_chain).link

        def centre(j):
            c0, n = groups[j]
            dve.wait_ge(means, j + 1)
            if j >= XCS:
                dve.wait_ge(lows, j - XCS + 1)
            dve.tensor_tensor(XC[:, j % XCS, :, 0:n], HT[:, :, c0:c0 + n],
                              wide(PS[:, bank + j % 2, 0:n][:, None, :], [P, DC, n]), ALU.subtract).then_inc(centred, 1)

        def scale(j):
            c0, n = groups[j]
            ve, rs, rt = VE[:, j % 2, 0:n], RS[:, j % 2, 0:n], RT[:, j % 2, 0:n]
            dve.wait_ge(variances, j + 1)
            dve.tensor_scalar(ve, PS[:, bank + 2 + j % 2, 0:n], EPS, None, ALU.add).then_inc(var_eps, 1)
            if beside:
                beside.while_guessed(dve, j)
            dve.wait_ge(guess_sq, j + 1)
            link(dve.tensor_tensor(rt, rt, ve, ALU.mult))
            link(dve.tensor_scalar(rt, rt, -0.5, 1.5, ALU.mult, ALU.add))
            link(dve.tensor_tensor(rs, rs, rt, ALU.mult))
            if spread and n < P:
                dve.wait_ge(zeroed, 1)
                for q in range(P // 32):
                    last = dve.tensor_tensor(XW[:, :, q, 0:n], XC[:, j % XCS, :, 0:n], wide(rs[:, None, :], [P, DC, n]), ALU.mult)
                last.then_inc(normed, 1)
            else:
                dve.tensor_tensor(XC[:, j % XCS, :, 0:n], XC[:, j % XCS, :, 0:n], wide(rs[:, None, :], [P, DC, n]),
                                  ALU.mult).then_inc(normed, 1)
            if c0 == TR and cls_copy is not None:
                dve.wait_ge(normed, j + 1)
                dve.tensor_copy(cls_copy[0], wide(XC[:, j % XCS, :, 0:1], [P, DC, P])).then_inc(cls_copy[1], 1)

        centre(0), centre(1)
        for j in range(NGR):
            scale(j)
            if j + 2 < NGR:
                centre(j + 2)
            if j == 0 and beside:
                beside.vector(dve)

    @blk.scalar
    def _(act):
        def high(j):
            x, c = result(j)
            act.wait_ge(normed, j + 1)
            act.copy(XH[:, :, c], x).then_inc(highs, 1)

        def square(j):
            n = groups[j][1]
            act.wait_ge(centred, j + 1)
            if j >= 2:
                act.wait_ge(variances, j - 1)
            act.activation(SQ[:, j % 2, :, 0:n], XC[:, j % XCS, :, 0:n], ACT.Square).then_inc(squares, 1)

        square(0), square(1)
        if beside:
            beside.scalar(act)
        for j in range(NGR):
            n = groups[j][1]
            ve, rs, rt = VE[:, j % 2, 0:n], RS[:, j % 2, 0:n], RT[:, j % 2, 0:n]
            act.wait_ge(var_eps, j + 1)
            act.activation(rs, ve, ACT.Ln).then_inc(act_chain, 1)
            act.wait_ge(act_chain, 2 * j + 1)
            act.activation(rs, rs, ACT.Exp, scale=-0.5).then_inc(act_chain, 1)
            act.wait_ge(act_chain, 2 * j + 2)
            act.activation(rt, rs, ACT.Square).then_inc(guess_sq, 1)
            high(j)
            if j + 2 < NGR:
                square(j + 2)

    @blk.gpsimd
    def _(pool):
        if spread:
            pool.memset(XW[:, :, :, :], 0.0).then_inc(zeroed, 1)
        if beside:
            beside.gpsimd(pool)
        for j in range(NGR):
            x, c = result(j)
            pool.wait_ge(highs, j + 1)
            pool.tensor_tensor(XL[:, :, c], x, XH[:, :, c].bitcast(F32), ALU.subtract).then_inc(lows, 1)
        pool.wait_ge(lows, NGR)
    return {"normed": lows, "banks": var_eps, "groups": NGR}


class Beside:

    def sync(self, sp):
        pass

    def tensor(self, pe, j):
        pass

    def scalar(self, act):
        pass

    def vector(self, dve):
        pass

    def while_guessed(self, dve, j):
        pass

    def gpsimd(self, pool):
        pass


class ClassQueries(Beside):

    def __init__(self, nc, ctx, w_qkv, k):
        self.w_qkv, self.PS = w_qkv, k["PS"]
        self.W = ctx.enter_context(nc.sbuf_tensor("c_w", [P, DC, HEADS * DH], F32))
        self.XB = ctx.enter_context(nc.sbuf_tensor("class_x", [P, DC, P], F32))
        sem = signals(nc, ctx)
        self.loaded_q, self.loaded_k = ([sem(f"c_load_{x}{n}") for n in range(DC)] for x in "qk")
        self.copied, self.q_ready, self.chain = sem("c_copied"), sem("c_q_ready"), sem("c_u_chain")
        self.UQ = ctx.enter_context(nc.sbuf_tensor("c_u", [P, DC, P], F32))

    def sync(self, sp):
        for part, loaded in enumerate((self.loaded_q, self.loaded_k)):
            for n in range(DC):
                if part:
                    sp.wait_ge(self.q_ready, n + 1)
                c = slice(n * GRP, (n + 1) * GRP)
                source = self.w_qkv[:, part * HEADS * DH + n * GRP:part * HEADS * DH + (n + 1) * GRP]
                sp.dma_start(self.W[:, :, c], source.rearrange("(a p) n -> p a n", p=P)).then_inc(loaded[n], 16)

    def tensor(self, pe, j):
        if j >= DC:
            return
        pe.wait_ge(self.loaded_q[j], 16)
        pe.wait_ge(self.copied, 1)
        for a in range(DC):
            last = pe.matmul(self.PS[:, 4 + j], self.XB[:, a], self.W[:, a, j * GRP:(j + 1) * GRP], start=a == 0, stop=a == DC - 1)
        last.then_inc(self.q_ready, 1)

    def while_guessed(self, dve, j):
        if j == 0:
            dve.memset(self.UQ[:, :, :], 0.0).then_inc(self.chain, 1)
        if j >= 2:
            self.keys_by_query(dve, j - 2)

    def keys_by_query(self, dve, n):
        c = slice(n * GRP, (n + 1) * GRP)
        wk = self.W[:, :, c]
        dve.wait_ge(self.q_ready, n + 1)
        dve.wait_ge(self.loaded_k[n], 16)
        dve.tensor_tensor(wk, wk, wide(self.PS[:, 4 + n][:, None, :], [P, DC, GRP]), ALU.mult).then_inc(self.chain, 1)
        dve.wait_ge(self.chain, 2 * n + 2)
        dve.reduce_sum(self.UQ[:, :, 4 * n:4 * n + 4], wk.rearrange("p a (h d) -> p a h d", h=4), AX.X).then_inc(self.chain, 1)


def class_rows(nc, ctx, blk, k, queries, tokens):
    XH, XL, PS = k["XH"], k["XL"], k["PS"]
    HD = HEADS * DH
    sb = lambda n, s, d=F32: ctx.enter_context(nc.sbuf_tensor(n, s, d))
    sem = signals(nc, ctx)
    UQ = queries.UQ
    UQH = sb("c_uh", [P, DC, P], F32R)
    UQL = sb("c_ul", [P, DC, P], F32R)
    SC = sb("c_scores", [P, 2, NCH + 2])
    MX = sb("c_max", [P, 2])
    RC = sb("c_sum", [P, 2])
    dve_chain = sem("c_dve_chain")
    u_high = sem("c_u_high")
    u_ready = sem("c_u_ready")
    scored = sem("c_scored")
    scores_in = sem("c_scores_in")
    shifted = sem("c_shifted")
    exps = sem("c_exps")
    probs = sem("c_probs")
    highs = sem("c_highs")
    lows = sem("c_lows")

    @blk.tensor
    def _(pe):
        pe.wait_ge(u_ready, 1)
        pe.wait_ge(tokens["normed"], tokens["groups"])
        pe.wait_ge(tokens["banks"], tokens["groups"])
        for j, (c0, n) in enumerate(GROUPS):
            if j >= 4:
                pe.wait_ge(scores_in, j - 3)
            split_product(pe, PS[:, j % 4, 0:n], [(UQH[:, a], UQL[:, a], XH[:, a, c0:c0 + n], XL[:, a, c0:c0 + n])
                                                  for a in range(DC)]).then_inc(scored, 1)

    @blk.vector
    def _(dve):
        link = Chain(dve, dve_chain).link
        for n in range(NG - 1, DC):
            queries.keys_by_query(dve, n)
        dve.wait_ge(queries.chain, 2 * DC + 1)
        for g in range(1, NG):
            last = dve.tensor_copy(UQ[:, :, 32 * g:32 * g + HEADS], UQ[:, :, 0:HEADS])
        link(last)
        link(dve.tensor_copy(UQH[:, :, :], UQ[:, :, :]))
        dve.tensor_tensor(UQL[:, :, :], UQ[:, :, :], UQH[:, :, :].bitcast(F32), ALU.subtract).then_inc(u_ready, 1)
        dve.wait_ge(scores_in, NG + 1)
        link(dve.reduce_max(MX[:, :], SC[:, :, 0:NCH + 1], AX.X))
        dve.tensor_tensor(SC[:, :, 0:NCH + 1], SC[:, :, 0:NCH + 1], wide(MX[:, :, None], [P, 2, NCH + 1]),
                          ALU.subtract).then_inc(shifted, 1)
        dve.wait_ge(exps, 1)
        link(dve.reduce_sum(RC[:, :], SC[:, :, 0:NCH + 1], AX.X))
        link(dve.reciprocal(MX[:, :], RC[:, :]))
        dve.tensor_tensor(SC[:, :, :], SC[:, :, :], wide(MX[:, :, None], [P, 2, NCH + 2]), ALU.mult).then_inc(probs, 1)
        dve.wait_ge(highs, 1)
        dve.tensor_tensor(k["PCL"][:, :, :], SC[:, :, :], k["PCH"][:, :, :].bitcast(F32), ALU.subtract).then_inc(lows, 1)
        dve.wait_ge(lows, 1)

    @blk.scalar
    def _(act):
        for j, (c0, n) in enumerate(GROUPS):
            act.wait_ge(scored, j + 1)
            if n == GRP:
                r = slice(32 * j, 32 * j + 32)
                act.copy(SC[r, :, 0:NCH], PS[r, j % 4].rearrange("p (b n) -> p b n", b=2)).then_inc(scores_in, 1)
                continue
            for g in range(NG):
                r = slice(32 * g, 32 * g + 32)
                last = act.copy(SC[r, :, NCH:NCH + 2], wide(PS[r, j % 4, 2 * g:2 * g + 2][:, :, None], [32, 2, 2]))
            last.then_inc(scores_in, 1)
        act.wait_ge(shifted, 1)
        act.activation(SC[:, :, 0:NCH + 1], SC[:, :, 0:NCH + 1], ACT.Exp, scale=SCALE).then_inc(exps, 1)
        act.wait_ge(probs, 1)
        act.copy(k["PCH"][:, :, :], SC[:, :, :]).then_inc(highs, 1)
        act.wait_ge(highs, 1)


def attention(nc, w_qkv, w_o, k):
    HT, XH, XL, PS = k["HT"], k["XH"], k["XL"], k["PS"]
    HD = HEADS * DH
    R = NCH + 2
    UNITS = 2 * NG
    ROUNDS = HEADS // 2
    OUTS = DC * NG
    QB, KB, VB, CB, SB = 0, 1, 2, 3, 4
    OUT_BANKS = (VB, QB, KB)
    PARTS = [(1, 0), (1, 1), (1, 2), (0, 3), (1, 3), (0, 0), (0, 1), (0, 2)]
    FIRST = [(0, 0), (0, 1), (0, 2)]
    NP, NF = len(PARTS), len(FIRST)
    SUMS_AFTER = {3: 0, 7: 1}
    PREP = {0: [0, 1], 1: [2, 3], 2: [4], 4: [5], 5: [6], 6: [7]}
    with Stage() as ctx:
        sb = lambda n, s, d=F32: ctx.enter_context(nc.sbuf_tensor(n, s, d))
        sem = signals(nc, ctx)
        RAW = sb("t_wraw", [P, 2, D])
        WH = sb("t_wh", [P, 2, 4, D], F32R)
        WL = sb("t_wl", [P, 2, 4, D], F32R)
        QH = sb("t_qh", [P, GRP], F32R)
        QL = sb("t_ql", [P, GRP], F32R)
        KH = sb("t_kh", [P, 2, R], F32R)
        KL = sb("t_kl", [P, 2, R], F32R)
        KVC = sb("t_kvc", [P, 2, 4])
        KVR = sb("t_kv_row", [2, 2, DH])
        CO = sb("t_class_out", [B, D])
        REP = sb("t_rep", [P, HEADS])
        VS = sb("t_v", [P, 2, 2, NCH])
        E = sb("t_e", [P, 4, R])
        EPH = sb("t_eph", [P, 2, R], F32R)
        EPL = sb("t_epl", [P, 2, R], F32R)
        VT = sb("t_vt", [P, 2, NCH + 1])
        VTH = sb("t_vth", [P, 2, B, R], F32R)
        VTL = sb("t_vtl", [P, 2, B, R], F32R)
        SEL = sb("t_sel", [P, 2, P], F32R)
        ONES = sb("t_ones", [P, P], F32R)
        MX = sb("t_max", [P, 4])
        NB = sb("t_bias", [P, 4])
        RS = sb("t_rowsum", [P, 4])
        RC = sb("t_rowinv", [P, 4])
        first_raw = [RAW[:, 0], RAW[:, 1], VS[:, 0].rearrange("p b n -> p (b n)")]
        loads = [sem("t_load0"), sem("t_load1"), sem("t_load2")]
        wh, wl = sem("t_wh_ready"), sem("t_wl_ready")
        setup = sem("t_setup")
        sel_ready = sem("t_sel_ready")
        kvr_done, kvr_in, kvc_done, kvc_in = sem("t_kvr_done"), sem("t_kvr_in"), sem("t_kvc_done"), sem("t_kvc_in")
        rep_made, class_out, class_added, turned_out = sem("t_rep_made"), sem("t_class_out_done"), sem("t_class_added"), sem("t_turned_out")
        q_done, k_done, v_done = sem("t_q_done"), sem("t_k_done"), sem("t_v_done")
        qh, ql, kh, kl, vs = sem("t_qh_ready"), sem("t_ql_ready"), sem("t_kh_ready"), sem("t_kl_ready"), sem("t_v_in")
        s_done, maxed, nmax, exps = sem("t_s_done"), sem("t_maxed"), sem("t_bias_ready"), sem("t_exps")
        inv, scaled, ep, eph, epl = sem("t_inv"), sem("t_scaled"), sem("t_ep"), sem("t_eph_ready"), sem("t_epl_ready")
        c_done, vt, vth, vtl = sem("t_c_done"), sem("t_vt_ready"), sem("t_vth_ready"), sem("t_vtl_ready")
        wo_done, hadd = sem("t_wo_done"), sem("t_hadd")
        blk = ctx.enter_context(nc.Block())

        def source(part, head):
            if part < 3:
                return w_qkv[:, bass.ds(head * DH + part * HD, DH)].rearrange("(a p) n -> p a n", p=P)
            return w_o[bass.ds(head * DH, DH), :]

        def as_loaded(raw, part):
            return raw.rearrange("p (a n) -> p a n", a=DC) if part < 3 else raw

        @blk.sync
        def _(sp):
            for x, (s, part) in enumerate(FIRST):
                sp.dma_start(as_loaded(first_raw[x], part), source(part, 0)).then_inc(loads[x], 16)
            with sp.Fori(0, ROUNDS) as i:
                for x, (s, part) in enumerate(PARTS):
                    slot = (NF + x) % 2
                    head = (2 * i + 2) % HEADS if x >= NP - NF else 2 * i + s
                    sp.wait_ge(wl, i * NP + NF + x - 1)
                    sp.dma_start(as_loaded(RAW[:, slot], part), source(part, head)).then_inc(loads[slot], 16)

        def loaded(eng, i, x):
            if i is None:
                eng.wait_ge(loads[x], 16)
            else:
                slot = (NF + x) % 2
                eng.wait_ge(loads[slot], i * 16 * NP // 2 + 16 * (x // 2 + 2))

        def slot_free(eng, i, x):
            if x < 3:
                eng.wait_ge(v_done, i * UNITS + 1)
            elif x < 5:
                eng.wait_ge(class_out, i + 1)
            else:
                eng.wait_ge(v_done, i * UNITS + NG + 1)

        @blk.gpsimd
        def _(pool):
            def low(i, x, s, part):
                if i is None:
                    pool.wait_ge(wh, x + 1)
                    raw = first_raw[x]
                else:
                    pool.wait_ge(wh, i * NP + NF + x + 1)
                    slot_free(pool, i, x)
                    raw = RAW[:, (NF + x) % 2]
                pool.tensor_tensor(WL[:, s, part], raw, WH[:, s, part].bitcast(F32), ALU.subtract).then_inc(wl, 1)

            pool.memset(ONES[:, :].bitcast(F32), 1.0).then_inc(setup, 1)
            pool.memset(E[:, :, R - 1:R], 0.0).then_inc(setup, 1)
            pool.tensor_copy(REP[:, :], k["ident"][:, 0:HEADS]).then_inc(rep_made, 1)
            for g in range(1, NG):
                pool.wait_ge(rep_made, g)
                pool.tensor_tensor(REP[:, :], REP[:, :], k["ident"][:, 32 * g:32 * g + HEADS], ALU.add).then_inc(rep_made, 1)
            pool.wait_ge(rep_made, NG)
            for x, (s, part) in enumerate(FIRST):
                low(None, x, s, part)
            with pool.Fori(0, ROUNDS) as i:
                def value_low(u, b):
                    s, g = u // NG, u % NG
                    n = i * 2 * UNITS + 2 * u + b
                    pool.wait_ge(vth, n + 1)
                    pool.wait_ge(class_out, i + 1)
                    pool.tensor_tensor(VTL[:, s, 2 * g + b, 0:NCH + 1], VT[:, b], VTH[:, s, 2 * g + b, 0:NCH + 1].bitcast(F32),
                                       ALU.subtract).then_inc(vtl, 1)

                pool.wait_ge(c_done, i * 2 * UNITS + 2)
                for s in range(2):
                    pool.tensor_copy(SEL[:, s], wide(REP[:, bass.ds(2 * i + s, 1)], [P, P])).then_inc(sel_ready, 1)
                for u in range(UNITS + 1):
                    for x in PREP.get(u, []):
                        low(i, x, *PARTS[x])
                    if u >= 1:
                        value_low(u - 1, 0)
                        value_low(u - 1, 1)

        @blk.scalar
        def _(act):
            def high(i, x, s, part):
                loaded(act, i, x)
                if i is not None:
                    slot_free(act, i, x)
                raw = first_raw[x] if i is None else RAW[:, (NF + x) % 2]
                act.copy(WH[:, s, part], raw).then_inc(wh, 1)

            act.wait_ge(setup, 2)
            for x, (s, part) in enumerate(FIRST):
                high(None, x, s, part)
            def class_row(n):
                act.wait_ge(kvr_done, n + 1)
                act.copy(KVR[:, :, :], PS[0:2, QB, 0:2 * DH].rearrange("p (j d) -> p j d", j=2)).then_inc(kvr_in, 1)

            def class_columns(n, s):
                act.wait_ge(kvc_done, n + 1)
                act.copy(KVC[:, s], PS[:, KB, 0:4]).then_inc(kvc_in, 1)

            class_row(0)
            class_columns(0, 0)
            with act.Fori(0, ROUNDS) as i:
                def value_high(u, b):
                    s, g = u // NG, u % NG
                    act.wait_ge(vt, i * 2 * UNITS + 2 * u + b + 2)
                    act.wait_ge(class_out, i + 1)
                    act.copy(VTH[:, s, 2 * g + b, 0:NCH + 1], VT[:, b]).then_inc(vth, 1)

                for u in range(UNITS):
                    n = i * UNITS + u
                    for x in PREP.get(u, []):
                        high(i, x, *PARTS[x])
                    act.wait_ge(q_done, n + 1)
                    act.wait_ge(s_done, 4 * n + 1)
                    act.copy(QH[:, :], PS[:, QB]).then_inc(qh, 1)
                    if u % NG == 0:
                        act.wait_ge(kvc_in, i * 2 + u // NG + 1)
                        act.copy(KH[:, :, NCH:R], wide(KVC[:, u // NG, 0:1][:, :, None], [P, 2, 2]))
                    act.wait_ge(k_done, n + 1)
                    act.copy(KH[:, :, 0:NCH], PS[:, KB].rearrange("p (b n) -> p b n", b=2)).then_inc(kh, 1)
                    if u >= 1:
                        value_high(u - 1, 0)
                    act.wait_ge(v_done, n + 2)
                    act.copy(VS[:, u % 2], PS[:, VB].rearrange("p (b n) -> p b n", b=2)).then_inc(vs, 1)
                    if u >= 1:
                        value_high(u - 1, 1)

                    def exp(t):
                        act.wait_ge(nmax, 4 * n + t + 1)
                        act.wait_ge(epl, 2 * n + 1)
                        act.activation(E[:, t, 0:NCH + 1], PS[:, SB + t, 0:NCH + 1], ACT.Exp, bias=NB[:, t:t + 1],
                                       scale=SCALE, accum_out=RS[:, t:t + 1]).then_inc(exps, 1)

                    def high_probs(b):
                        act.wait_ge(ep, 2 * n + b + 1)
                        act.wait_ge(c_done, 2 * n + b + 1)
                        act.copy(EPH[:, b], E[:, 2 * b]).then_inc(eph, 1)

                    if u % NG == NG - 1:
                        class_row(i * 2 + u // NG + 1)
                    exp(0), exp(1), exp(2)
                    if u % NG == NG - 1:
                        class_columns(i * 2 + u // NG + 1, 1 - u // NG)
                    high_probs(0), exp(3), high_probs(1)
                value_high(UNITS - 1, 0)
                value_high(UNITS - 1, 1)

        @blk.vector
        def _(dve):
            dve.memset(CO[:, :], 0.0).then_inc(class_added, 1)
            with dve.Fori(0, ROUNDS) as i:
                def values(u, b):
                    n = i * 2 * UNITS + 2 * u + b
                    dve.wait_ge(c_done, n + 3)
                    dve.wait_ge(vs, i * UNITS + u + 2)
                    dve.wait_ge(vtl, n + 1)
                    dve.tensor_tensor(VT[:, b, 0:NCH], VS[:, u % 2, b], PS[:, CB, 0:NCH], ALU.mult)
                    dve.tensor_tensor(VT[:, b, NCH:NCH + 1], KVC[:, u // NG, 2:3], PS[:, CB, NCH:NCH + 1], ALU.mult).then_inc(vt, 1)

                def add_output(j):
                    g, f = j // DC, j % DC
                    c0, n = GROUPS[g]
                    dve.wait_ge(wo_done, i * OUTS + j + 2)
                    dve.tensor_tensor(HT[:, f, c0:c0 + n], HT[:, f, c0:c0 + n], PS[:, OUT_BANKS[j % 3]], ALU.add).then_inc(hadd, 1)

                for u in range(UNITS):
                    n = i * UNITS + u
                    dve.wait_ge(qh, n + 1)
                    dve.wait_ge(s_done, 4 * n + 1)
                    dve.tensor_tensor(QL[:, :], PS[:, QB], QH[:, :].bitcast(F32), ALU.subtract).then_inc(ql, 1)
                    dve.wait_ge(kh, n + 1)
                    if u % NG == 0:
                        dve.tensor_tensor(KL[:, :, NCH:R], wide(KVC[:, u // NG, 0:1][:, :, None], [P, 2, 2]), KH[:, :, NCH:R].bitcast(F32), ALU.subtract)
                    dve.tensor_tensor(KL[:, :, 0:NCH], PS[:, KB].rearrange("p (b n) -> p b n", b=2),
                                      KH[:, :, 0:NCH].bitcast(F32), ALU.subtract).then_inc(kl, 1)
                    if u >= 1:
                        values(u - 1, 0)
                        values(u - 1, 1)

                    def row_max(t):
                        dve.wait_ge(s_done, 4 * n + t + 2)
                        dve.reduce_max(MX[:, t:t + 1], PS[:, SB + t, 0:NCH + 1], AX.X).then_inc(maxed, 1)
                        dve.wait_ge(maxed, 4 * n + t + 1)
                        dve.tensor_scalar(NB[:, t:t + 1], MX[:, t:t + 1], -SCALE, None, ALU.mult).then_inc(nmax, 1)

                    def merge(b):
                        dve.wait_ge(exps, 4 * n + 2 * b + 2 + 4)
                        dve.reciprocal(RC[:, 2 * b:2 * b + 2], RS[:, 2 * b:2 * b + 2]).then_inc(inv, 1)
                        dve.wait_ge(inv, 2 * n + b + 1)
                        dve.tensor_scalar(E[:, 2 * b], E[:, 2 * b], RC[:, 2 * b:2 * b + 1], None, ALU.mult).then_inc(scaled, 1)
                        dve.wait_ge(scaled, 2 * n + b + 1)
                        dve.scalar_tensor_tensor(E[:, 2 * b], E[:, 2 * b + 1], RC[:, 2 * b + 1:2 * b + 2], E[:, 2 * b],
                                                 ALU.mult, ALU.add).then_inc(ep, 1)

                    def low_probs(b):
                        dve.wait_ge(eph, 2 * n + b + 1)
                        dve.tensor_tensor(EPL[:, b], E[:, 2 * b], EPH[:, b].bitcast(F32), ALU.subtract).then_inc(epl, 1)

                    row_max(0), row_max(1), row_max(2), merge(0), row_max(3), low_probs(0)
                    if u == UNITS - 1:
                        add_output(0)
                    merge(1)
                    if u == UNITS - 1:
                        add_output(1)
                    low_probs(1)
                for j in range(2, OUTS):
                    add_output(j)
                    if j in SUMS_AFTER:
                        values(UNITS - 1, SUMS_AFTER[j])
                dve.wait_ge(class_out, i + 2)
                dve.wait_ge(class_added, i + 1)
                dve.tensor_tensor(CO[:, :], CO[:, :], PS[0:B, CB], ALU.add).then_inc(class_added, 1)
            dve.wait_ge(hadd, ROUNDS * OUTS + 1)
            dve.wait_ge(turned_out, 1)
            dve.tensor_tensor(HT[:, :, TR:T], HT[:, :, TR:T], PS[:, QB, 0:DC * B].rearrange("p (f b) -> p f b", f=DC),
                              ALU.add).then_inc(hadd, 1)
            dve.wait_ge(hadd, ROUNDS * OUTS + 2)

        @blk.tensor
        def _(pe):
            pe.sem_inc(exps, 4)
            pe.sem_inc(c_done, 2)
            pe.sem_inc(vtl, 2)
            for s in (epl, s_done, v_done, wo_done, hadd, kl, ql, vs, vt, class_out):
                pe.sem_inc(s, 1)
            pe.wait_ge(setup, 2)

            def class_product(s):
                out = PS[0:2, QB, 0:2 * DH].rearrange("p (j d) -> p j d", j=2)
                c = slice(TR, TR + 2)
                split_product(pe, out, [(XH[:, a, c], XL[:, a, c], WH[:, s, 1:3, a * P:(a + 1) * P], WL[:, s, 1:3, a * P:(a + 1) * P])
                                        for a in range(DC)]).then_inc(kvr_done, 1)

            def class_turn():
                for j in range(2):
                    last = pe.transpose(PS[:, KB, 2 * j:2 * j + 2], KVR[:, j], k["ident"][0:2, 0:2])
                last.then_inc(kvc_done, 1)

            pe.wait_ge(wl, NF)
            class_product(0)
            pe.wait_ge(kvr_in, 1)
            class_turn()
            with pe.Fori(0, ROUNDS) as i:
                def project(u, part, bank, done):
                    s, g = u // NG, u % NG
                    c = slice(g * GRP, (g + 1) * GRP)
                    split_product(pe, PS[:, bank], [(WH[:, s, part, a * P:(a + 1) * P], WL[:, s, part, a * P:(a + 1) * P],
                                                     XH[:, a, c], XL[:, a, c]) for a in range(DC)]).then_inc(done, 1)

                def column_sums(u, b):
                    s, g = u // NG, u % NG
                    n = i * 2 * UNITS + 2 * u + b
                    pe.wait_ge(epl, n + 2)
                    if u == 0 and b == 0:
                        pe.wait_ge(class_added, i + 1)
                    pe.wait_ge(sel_ready, i * 2 + s + 1)
                    pe.wait_ge(vt, n + 1)
                    out = PS[:, CB, 0:R]
                    pe.matmul(out, ONES[:, :], EPH[:, b], start=True, stop=False)
                    pe.matmul(out, ONES[:, :], EPL[:, b], start=False, stop=False)
                    r = slice(32 * g, 32 * g + 32)
                    pe.matmul(out, SEL[r, s], k["PCH"][r, b], start=False, stop=False)
                    pe.matmul(out, SEL[r, s], k["PCL"][r, b], start=False, stop=True).then_inc(c_done, 1)

                def output(j):
                    g, f = j // DC, j % DC
                    c0, n = GROUPS[g]
                    pe.wait_ge(vtl, i * 2 * UNITS + 2 * (NG + g + 1) + 2)
                    if j >= 3:
                        pe.wait_ge(hadd, i * OUTS + j - 2 + 1)
                    if j == 2:
                        pe.wait_ge(kvc_in, i * 2 + 3)
                    v = [t[:, s, 2 * g:2 * g + 2, 0:NCH] for s in range(2) for t in (VTH, VTL)]
                    fs = slice(f * P, (f + 1) * P)
                    split_product(pe, PS[:, OUT_BANKS[j % 3]], [(WH[:, s, 3, fs], WL[:, s, 3, fs], v[2 * s], v[2 * s + 1])
                                                                for s in range(2)]).then_inc(wo_done, 1)

                for u in range(UNITS):
                    n = i * UNITS + u
                    s = u // NG
                    if u % NG == 0:
                        pe.wait_ge(wl, i * NP + (NF if s == 0 else NF + 3))
                    if u == 0:
                        pe.wait_ge(hadd, i * OUTS + 1)
                    pe.wait_ge(ql, n + 1)
                    project(u, 0, QB, q_done)
                    pe.wait_ge(kl, n + 1)
                    if u % NG == 0:
                        pe.wait_ge(kvc_in, i * 2 + s + 1)
                    project(u, 1, KB, k_done)
                    if u >= 1:
                        column_sums(u - 1, 0)
                    pe.wait_ge(vs, n + 1)
                    project(u, 2, VB, v_done)
                    if u >= 1:
                        column_sums(u - 1, 1)
                    pe.wait_ge(ql, n + 2)
                    pe.wait_ge(kl, n + 2)
                    if u % NG == NG - 1:
                        pe.wait_ge(wl, i * NP + (NF + 3 if s == 0 else NF + NP))
                        class_product(1 - s)
                    for t in range(4):
                        b = t // 2
                        pe.wait_ge(exps, 4 * n + t + 1)
                        if t == 3 and u % NG == NG - 1:
                            pe.wait_ge(kvr_in, i * 2 + s + 2)
                        split_product(pe, PS[:, SB + t, 0:R], [(QH[:, t * P:(t + 1) * P], QL[:, t * P:(t + 1) * P],
                                                                KH[:, b], KL[:, b])]).then_inc(s_done, 1)
                    if u % NG == NG - 1:
                        class_turn()
                pe.wait_ge(wl, i * NP + NF + 5)
                pe.wait_ge(vs, (i + 1) * UNITS + 1)
                for j in range(OUTS):
                    output(j)
                    if j in SUMS_AFTER:
                        column_sums(UNITS - 1, SUMS_AFTER[j])
                pe.wait_ge(vt, (i + 1) * 2 * UNITS + 1)
                split_product(pe, PS[0:B, CB], [(VTH[:, s, :, NCH], VTL[:, s, :, NCH], WH[:, s, 3], WL[:, s, 3])
                                                for s in range(2)]).then_inc(class_out, 1)
            pe.wait_ge(class_added, ROUNDS + 1)
            pe.wait_ge(hadd, ROUNDS * OUTS + 1)
            for f in range(DC):
                last = pe.transpose(PS[:, QB, f * B:(f + 1) * B], CO[:, f * P:(f + 1) * P], k["ident"][0:B, 0:B])
            last.then_inc(turned_out, 1)


KH_ = 4
NK = 128
TOPK = 8
EXPERTS = 4096
ROWS_IN = EXPERTS // NK
EC = 512
CHUNKS = EXPERTS // EC
RPC = EC // NK


class KeyWeights(Beside):

    def __init__(self, nc, ctx, w_q, keys, k, tag):
        sb = lambda n, s, d=F32: ctx.enter_context(nc.sbuf_tensor(tag + n, s, d))
        sem = signals(nc, ctx, tag)
        self.w_q, self.keys, self.k = w_q, keys, k
        self.WR = sb("s_wraw", [P, DC, D])
        self.WH = sb("s_wh", [P, DC, D], F32R)
        self.WL = sb("s_wl", [P, DC, D], F32R)
        self.KR = sb("s_keys", [P, KH_, 2, NST])
        self.KT = sb("s_keys_t", [P, KH_, 2, NK])
        self.load_w, self.load_k = sem("s_load_w"), sem("s_load_k")
        self.w_high, self.w_low = sem("s_w_high"), sem("s_w_low")
        self.zeroed, self.keys_t, self.keys_in = sem("s_keys_zeroed"), sem("s_keys_t_done"), sem("s_keys_in")

    def sync(self, sp):
        sp.dma_start(self.KR[:, :, :, :], self.keys.rearrange("h k j d -> k h j d")).then_inc(self.load_k, 16)
        sp.dma_start(self.WR[:, :, :], self.w_q.rearrange("(a p) n -> p a n", p=P)).then_inc(self.load_w, 16)

    def tensor(self, pe, j):
        if j:
            return
        pe.wait_ge(self.load_k, 16)
        for h in range(KH_):
            last = pe.transpose(self.k["PS"][:, 0, h * P:(h + 1) * P], self.KR[:, h].rearrange("p j d -> p (j d)"), self.k["ident"][:, :])
        last.then_inc(self.keys_t, 1)

    def scalar(self, act):
        act.wait_ge(self.load_w, 16)
        act.copy(self.WH[:, :, :], self.WR[:, :, :]).then_inc(self.w_high, 1)

    def vector(self, dve):
        dve.memset(self.KT[:, :, :, :], 0.0).then_inc(self.zeroed, 1)
        dve.wait_ge(self.zeroed, 1)
        dve.wait_ge(self.keys_t, 1)
        for j in range(2):
            r = slice(j * NST, (j + 1) * NST)
            dve.tensor_copy(self.KT[r, :, j, :], self.k["PS"][r, 0, :].rearrange("p (h k) -> p h k", h=KH_)).then_inc(self.keys_in, 1)

    def gpsimd(self, pool):
        pool.wait_ge(self.w_high, 1)
        pool.tensor_tensor(self.WL[:, :, :], self.WR[:, :, :], self.WH[:, :, :].bitcast(F32), ALU.subtract).then_inc(self.w_low, 1)


def key_scores(nc, ctx, blk, weights, k, e, groups, tokens, tag):
    PS, XH, XL = k["PS"], e["XH"], e["XL"]
    tiles = [(g, t) for g, (c0, n) in enumerate(groups) for t in range(n // P)]
    NGR = len(groups)
    sb = lambda n, s, d=F32: ctx.enter_context(nc.sbuf_tensor(tag + n, s, d))
    sem = signals(nc, ctx, tag)
    WH, WL, KT = weights.WH, weights.WL, weights.KT
    QF = sb("s_q", [P, 2, KH_, 2 * P])
    SF = sb("s_first", [P, 2, KH_, NK])
    TOP = sb("s_top", [P, 2, KH_, 2, TOPK])
    IDX = sb("s_index", [P, 2, KH_, TOPK], U32)
    BEYOND = sb("s_beyond", [P, 2, KH_, TOPK])
    CAND = sb("s_pairs", [P, 2, KH_, TOPK, TOPK])
    CHOSEN = sb("s_chosen", [P, 2, KH_, TOPK, TOPK])
    BEST = sb("s_best", [P, 2, KH_, TOPK])
    zeroed = sem("s_zeroed")
    marked, pairs_chosen, pairs_summed, pool_chain = sem("s_marked"), sem("s_pairs_chosen"), sem("s_pairs_summed"), sem("s_pool_chain")
    q_done, q_in = sem("s_q_done"), sem("s_q_in")
    sims, sims_in, sims_read = sem("s_sims"), sem("s_sims_in"), sem("s_sims_read")
    tops, cands, bests, taus = sem("s_tops"), sem("s_cands"), sem("s_bests"), sem("s_taus")

    @blk.gpsimd
    def _(pool):
        pool.memset(e["EXT"][:, :, :], 0.0).then_inc(zeroed, 1)
        pool.memset(e["S1"][:, :, :, ROWS_IN:], 0.0).then_inc(zeroed, 1)
        pool.memset(e["S1C"][:, :, CHUNKS:], 0.0).then_inc(zeroed, 1)
        pool.wait_ge(zeroed, 3)
        for y in range(len(tiles)):
            p = y % 2
            c, ch = CAND[:, p], CHOSEN[:, p]
            pool.wait_ge(marked, y + 1)
            pool.tensor_tensor(ch, ch, c, ALU.mult).then_inc(pool_chain, 1)
            pool.wait_ge(pool_chain, y + 1)
            pool.tensor_tensor(ch, ch, wide(BEYOND[:, p][:, :, :, None], [P, KH_, TOPK, TOPK]), ALU.mult).then_inc(pairs_chosen, 1)

    @blk.tensor
    def _(pe):
        pe.wait_ge(weights.w_low, 1)
        pe.wait_ge(weights.keys_in, 2)
        for g, (c0, n) in enumerate(groups):
            pe.wait_ge(tokens["normed"], c0 // GRP + 1)
            for h in range(KH_):
                if g:
                    pe.wait_ge(q_in, (g - 1) * KH_ + h + 1)
                split_product(pe, PS[:, h, 0:n], [(WH[:, a, h * P:(h + 1) * P], WL[:, a, h * P:(h + 1) * P],
                                                   XH[:, a, c0:c0 + n], XL[:, a, c0:c0 + n])
                                                  for a in range(DC)]).then_inc(q_done, 1)
            pe.wait_ge(q_in, (g + 1) * KH_)
            if g == 0:
                pe.wait_ge(tokens["banks"], tokens["groups"])
            for y, (gt, t) in enumerate(tiles):
                if gt != g:
                    continue
                if y >= 2:
                    pe.wait_ge(sims_in, y - 1)
                for h in range(KH_):
                    last = pe.matmul(PS[:, 4 + 2 * (y % 2) + h // 2, (h % 2) * 2 * NK:(h % 2 + 1) * 2 * NK],
                                     QF[:, g % 2, h, t * P:(t + 1) * P], KT[:, h].rearrange("p j k -> p (j k)"),
                                     start=True, stop=True)
                last.then_inc(sims, 1)

    def sim_rows(y):
        b = 4 + 2 * (y % 2)
        return PS[:, b:b + 2].rearrange("p b (h j k) -> p (b h) j k", h=2, j=2)

    @blk.scalar
    def _(act):
        def queries(g):
            n = groups[g][1]
            for h in range(KH_):
                act.wait_ge(q_done, g * KH_ + h + 1)
                act.copy(QF[:, g % 2, h, 0:n], PS[:, h, 0:n]).then_inc(q_in, 1)

        for g in range(NGR):
            queries(g)
            for y, (gt, t) in enumerate(tiles):
                if gt == g:
                    act.wait_ge(sims, y + 1)
                    if y >= 2:
                        act.wait_ge(sims_read, y - 1)
                    act.copy(SF[:, y % 2], sim_rows(y)[:, :, 0, :])
                    act.copy(e["S2"][:, y], sim_rows(y)[:, :, 1, :]).then_inc(sims_in, 1)
        act.wait_ge(sims_in, len(tiles))

    @blk.vector
    def _(dve):
        dve.wait_ge(zeroed, 3)

        def sum_beyond(y):
            dve.wait_ge(pairs_chosen, y + 1)
            dve.reduce_sum(e["EXT"][:, y, CHUNKS - 1:CHUNKS], CHOSEN[:, y % 2].rearrange("p h a b -> p (h a b)"),
                           AX.X).then_inc(pairs_summed, 1)

        def best_keys(y):
            p = y % 2
            dve.wait_ge(sims_in, y + 1)
            if groups[tiles[y][0]][1] > P:
                dve.tensor_copy(e["S1"][:, y, :, 0:ROWS_IN], SF[:, p, :, 0:ROWS_IN])
            else:
                for j in range(RPC):
                    r = slice(32 * j, 32 * j + 32)
                    dve.tensor_copy(e["S1C"][r, :, 0:CHUNKS], SF[r, p, :, j:ROWS_IN:RPC])
            for h in range(KH_):
                dve.max(out=TOP[:, p, h, 1], in_=e["S2"][:, y, h])
                last = dve.max(out=TOP[:, p, h, 0], in_=SF[:, p, h])
            last.then_inc(tops, 1)

        def first_indices(y):
            p = y % 2
            dve.wait_ge(tops, y + 1)
            for h in range(KH_):
                last = dve.max_index(out=IDX[:, p, h], in_max=TOP[:, p, h, 0], in_values=SF[:, p, h])
            last.then_inc(sims_read, 1)

        def pair_scores(y):
            p = y % 2
            if y >= 2:
                sum_beyond(y - 2)
            s = [P, KH_, TOPK, TOPK]
            dve.tensor_tensor(CAND[:, p], wide(TOP[:, p, :, 0][:, :, :, None], s),
                              wide(TOP[:, p, :, 1][:, :, None, :], s), ALU.add).then_inc(cands, 1)
            dve.wait_ge(sims_read, y + 1)
            dve.tensor_scalar(BEYOND[:, p], IDX[:, p], float(ROWS_IN), None, ALU.is_ge)

        def best_pairs(y):
            dve.wait_ge(cands, y + 1)
            for h in range(KH_):
                last = dve.max(out=BEST[:, y % 2, h], in_=CAND[:, y % 2, h].rearrange("p a b -> p (a b)"))
            last.then_inc(bests, 1)

        def threshold(y):
            dve.wait_ge(bests, y + 1)
            dve.tensor_scalar(e["TAU"][:, y], BEST[:, y % 2, :, TOPK - 1], 0.0, None, ALU.max).then_inc(taus, 1)

        def mark(y):
            f = "p h a b -> p h (a b)"
            dve.wait_ge(taus, y + 1)
            if y >= 2:
                dve.wait_ge(pairs_summed, y - 1)
            dve.tensor_tensor(CHOSEN[:, y % 2].rearrange(f), CAND[:, y % 2].rearrange(f),
                              wide(e["TAU"][:, y][:, :, None], [P, KH_, TOPK * TOPK]), ALU.is_ge).then_inc(marked, 1)

        for y in range(0, len(tiles), 2):
            for work in (best_keys, first_indices, pair_scores, best_pairs, threshold, mark):
                for z in range(y, min(y + 2, len(tiles))):
                    work(z)
        for y in range(len(tiles) - 2, len(tiles)):
            sum_beyond(y)
        dve.wait_ge(pairs_summed, len(tiles))


def expert_layer(nc, e_down, e_up, k, e, groups, columns, tag):
    PS, HT, XH, XL, S1, S2, TAU, EXT = (k["PS"], k["HT"], e["XH"], e["XL"], e["S1"], e["S2"], e["TAU"], e["EXT"])
    ET = EC // P
    NGR = len(groups)
    NZ = NGR * 2 * ET
    CLASS_AT = {ET: 0, 2 * ET: 1} if len(columns) > NGR else {}
    y_cls = columns[-1][0] // P
    ROUNDS = CHUNKS // 2
    DB, GB, TB, OB = 0, 2, 3, 4
    tiles = [range(c0 // P, (c0 + n) // P) for c0, n in columns]
    assert RPC == ET and NK == P and NZ == 4 * ET
    with Stage() as ctx:
        sb = lambda n, s, d=F32: ctx.enter_context(nc.sbuf_tensor(tag + n, s, d))
        sem = signals(nc, ctx, tag)
        DR = sb("down_raw", [P, 2, D])
        UR = sb("up_raw", [P, 2, D])
        DH_ = sb("down_h", [P, 2, ET, DC, P], F32R)
        DL = sb("down_l", [P, 2, ET, DC, P], F32R)
        UH = sb("up_h", [P, 2, ET, D], F32R)
        UL = sb("up_l", [P, 2, ET, D], F32R)
        V = sb("v", [P, 2, GRP // P, KH_, P])
        G = sb("g", [P, 2, GRP // P, P])
        S = sb("silu", [P, 2, GRP])
        WF = sb("w", [P, 2, GRP])
        WH = sb("wh", [P, 2, GRP], F32R)
        WL = sb("wl", [P, 2, GRP], F32R)
        first_d = [DR[:, 0], DR[:, 1], S[:, 0], S[:, 1]]
        first_u = [UR[:, 0], UR[:, 1], WF[:, 0], WF[:, 1]]
        assert len(first_d) == ET and GRP == D
        load_first = [sem(f"load_first{x}") for x in range(ET)]
        load_d, load_u = [sem("load_d0"), sem("load_d1")], [sem("load_u0"), sem("load_u1")]
        table_t, down_h, down_l, up_h, up_l = sem("table_t"), sem("down_hr"), sem("down_lr"), sem("up_hr"), sem("up_lr")
        sums, own_sums, chosen = sem("sums"), sem("own_sums"), sem("chosen")
        pool_chain, g_ready = sem("pool_chain"), sem("g_ready")
        d_done, t_done, silus, w_ready, w_high, w_low = (sem("d_done"), sem("t_done"), sem("silus"), sem("w_ready"),
                                                         sem("w_high"), sem("w_low"))
        up_done, added, zeroed = sem("up_done"), sem("added"), sem("zeroed")
        if CLASS_AT:
            CV, CG, CS, CW = sb("cls_v", [P, KH_, P]), sb("cls_g", [P, P]), sb("cls_silu", [P, P]), sb("cls_w", [P, P])
            CWH, CWL = sb("cls_wh", [P, P], F32R), sb("cls_wl", [P, P], F32R)
            CO = sb("cls_out", [B, D])
            cls = {n: sem("cls_" + n) for n in ("sums", "own_sums", "chosen", "chain", "gates", "down", "silus", "w",
                                                "turned", "wh", "wl", "up", "added", "out")}
        blk = ctx.enter_context(nc.Block())

        def item(z):
            return z % NZ // (2 * ET), z % (2 * ET) // ET + 2 * (z // NZ), z % ET

        def table_at(z):
            return z if z < ET else z - (NZ - 2 * ET) if z >= NZ - ET else None

        def own_heads(t):
            return KH_ - 1 + (t == 1)

        def tables_behind(z):
            return [table_at(y) for y in ([z - 1, z] if z == NZ - 1 else [z - 1] if z else []) if table_at(y) is not None]

        def table_free(eng, i, x):
            eng.wait_ge(up_done, i * NZ + 2 + (0 if x < ET else NZ - 2 * ET + x % ET + 1))

        @blk.sync
        def _(sp):
            def load(x, chunk):
                r = bass.ds(chunk * EC + (x % ET) * P, P)
                sp.dma_start(DR[:, x % 2], e_down[r, :]).then_inc(load_d[x % 2], 16)
                sp.dma_start(UR[:, x % 2], e_up[r, :]).then_inc(load_u[x % 2], 16)

            for x in range(ET):
                sp.dma_start(first_d[x], e_down[x * P:(x + 1) * P, :]).then_inc(load_first[x], 16)
                sp.dma_start(first_u[x], e_up[x * P:(x + 1) * P, :]).then_inc(load_first[x], 16)
            with sp.Fori(0, ROUNDS) as i:
                for x in range(2 * ET):
                    sp.wait_ge(table_t, i * 2 * ET + ET + x - 1)
                    sp.wait_ge(up_l, i * 2 * ET + ET + x - 1)
                    load(x, 2 * i + 1 if x < ET else (2 * i + 2) % CHUNKS)

        def number(i, x):
            return x if i is None else i * 2 * ET + ET + x

        def arrived(eng, sems, i, x):
            if i is None:
                eng.wait_ge(load_first[x], 32)
            else:
                eng.wait_ge(sems[x % 2], i * 16 * ET + 16 * (x // 2 + 1))

        def raw(i, x, which):
            if i is None:
                return (first_d, first_u)[which][x]
            return (DR, UR)[which][:, x % 2]

        def turn_bank(i, x):
            return OB + x if i is None else TB

        def slot(i, x):
            return 0 if i is None or x >= ET else 1

        @blk.tensor
        def _(pe):
            for s, n in ((silus, 2), (w_ready, 2), (w_low, 2), (up_done, 1), (g_ready, 4), (t_done, 1)):
                pe.sem_inc(s, n)
            if CLASS_AT:
                for s in ("gates", "w", "turned", "up"):
                    pe.sem_inc(cls[s], 1)

            def table(i, x):
                arrived(pe, load_d, i, x)
                if i is not None:
                    pe.wait_ge(down_l, number(i, x))
                for a in range(DC):
                    last = pe.transpose(PS[:, turn_bank(i, x), a * P:(a + 1) * P], raw(i, x, 0)[:, a * P:(a + 1) * P], k["ident"][:, :])
                last.then_inc(table_t, 1)

            def up_products(z, wait=lambda f: None):
                g, s, j = item(z)
                for f in range(DC):
                    wait(f)
                    fs = slice(f * P, (f + 1) * P)
                    pe.matmul(PS[:, OB + f], UH[:, s, j, fs], WH[:, z % 2], start=s == 0 and j == 0, stop=False)
                    pe.matmul(PS[:, OB + f], UH[:, s, j, fs], WL[:, z % 2], start=False, stop=False)
                    last = pe.matmul(PS[:, OB + f], UL[:, s, j, fs], WH[:, z % 2], start=False, stop=s == 1 and j == ET - 1)
                last.then_inc(up_done, 1)

            def class_down(i, s):
                if s == 0:
                    pe.wait_ge(down_l, i * 2 * ET + 2 * ET)
                pe.wait_ge(cls["added"], 2 * i + s + 1)
                c = columns[-1][0]
                split_product(pe, PS[:, TB], [(XH[:, a, c:c + P], XL[:, a, c:c + P], DH_[:, s, :, a], DL[:, s, :, a])
                                              for a in range(DC)]).then_inc(cls["down"], 1)

            def class_turn(i, s):
                pe.wait_ge(cls["w"], 2 * i + s + 2)
                pe.transpose(PS[:, TB, 0:P], CW[:, :], k["ident"][:, :]).then_inc(cls["turned"], 1)

            def class_up(i, s):
                pe.wait_ge(cls["wl"], 2 * i + s + 1)
                pe.wait_ge(up_l, i * 2 * ET + (s + 1) * ET)
                split_product(pe, PS[0:B, TB], [(CWH[:, 32 * q:32 * q + B], CWL[:, 32 * q:32 * q + B], UH[:, s, q], UL[:, s, q])
                                                for q in range(ET)]).then_inc(cls["up"], 1)

            for x in range(ET):
                table(None, x)
            pe.wait_ge(zeroed, 4)
            pe.wait_ge(down_l, ET)
            for f in range(DC):
                pe.matmul(PS[:, OB + f], UH[:, 1, ET - 1, f * P:(f + 1) * P], WH[:, 1], start=True, stop=False)
            with pe.Fori(0, ROUNDS) as i:
                def up(z):
                    g, s, j = item(z)
                    pe.wait_ge(w_low, i * NZ + z + 3)
                    pe.wait_ge(up_l, i * 2 * ET + s * ET + j + 1)
                    if s == 0 and j == 0:
                        up_products(z, lambda f: pe.wait_ge(added, DC * (i * NGR + g) + f + 1))
                    else:
                        up_products(z)

                for z in range(NZ):
                    g, s, j = item(z)
                    c = slice(columns[g][0], columns[g][0] + GRP)
                    pe.wait_ge(down_l, i * 2 * ET + s * ET + j + 1)
                    pe.wait_ge(silus, i * NZ + z + 1)
                    split_product(pe, PS[:, DB + z % 2], [(DH_[:, s, j, a], DL[:, s, j, a], XH[:, a, c], XL[:, a, c])
                                                          for a in range(DC)]).then_inc(d_done, 1)
                    pe.wait_ge(w_ready, i * NZ + z + 2)
                    for t in range(GRP // P):
                        if t % 2 == 0:
                            pe.wait_ge(g_ready, 2 * (i * NZ + z + 2) + t // 2 + 1)
                        last = pe.transpose(PS[:, GB, t * P:(t + 1) * P], G[:, z % 2, t], k["ident"][:, :])
                    last.then_inc(t_done, 1)
                    if z:
                        up(z - 1)
                    else:
                        pe.wait_ge(w_low, i * NZ + 2)
                        up_products(NZ - 1)
                    for step, work in enumerate((class_down, class_turn, class_up)):
                        if z - step in CLASS_AT:
                            work(i, CLASS_AT[z - step])
                    if table_at(z) is not None:
                        if CLASS_AT and z == NZ - ET:
                            pe.wait_ge(cls["added"], 2 * i + 3)
                        table(i, table_at(z))
            pe.wait_ge(w_low, ROUNDS * NZ + 2)
            up_products(NZ - 1)
            if CLASS_AT:
                pe.wait_ge(down_l, ROUNDS * 2 * ET + ET)
                pe.wait_ge(cls["added"], 2 * ROUNDS + 1)
                for f in range(DC):
                    last = pe.transpose(PS[:, TB, f * B:(f + 1) * B], CO[:, f * P:(f + 1) * P], k["ident"][0:B, 0:B])
                last.then_inc(cls["out"], 1)

        @blk.scalar
        def _(act):
            def table(i, x):
                act.wait_ge(table_t, number(i, x) + 1)
                if i is not None:
                    table_free(act, i, x)
                act.copy(DH_[:, slot(i, x), x % ET].rearrange("p a e -> p (a e)"), PS[:, turn_bank(i, x)]).then_inc(down_h, 1)
                arrived(act, load_u, i, x)
                act.copy(UH[:, slot(i, x), x % ET], raw(i, x, 1)).then_inc(up_h, 1)

            def pair_sums(done, z, chunk):
                g, s, j = item(z)
                for t, y in enumerate(tiles[g]):
                    if t % 2 == 0:
                        act.wait_ge(g_ready, 2 * done + t // 2 + 1)
                    for h in range(own_heads(t)):
                        last = act.activation(V[:, z % 2, t, h], S2[:, y, h], ACT.Identity,
                                              bias=S1[:, y, h, bass.ds((chunk + s) * RPC + j, 1)])
                    if t % 2:
                        last.then_inc(sums, 1)

            def class_sums(i, s):
                act.wait_ge(cls["gates"], 2 * i + s + 1)
                for h in range(KH_ - 1):
                    last = act.activation(CV[:, h], S2[:, y_cls, h], ACT.Identity, bias=e["S1C"][:, h, bass.ds(2 * i + s, 1)])
                last.then_inc(cls["sums"], 1)

            def class_silu(i, s):
                act.wait_ge(cls["down"], 2 * i + s + 1)
                act.wait_ge(cls["w"], 2 * i + s + 1)
                for q in range(ET):
                    r = slice(32 * q, 32 * q + 32)
                    last = act.activation(CS[r], PS[r, TB, q * P:(q + 1) * P], ACT.Silu)
                last.then_inc(cls["silus"], 1)

            def class_high(i, s):
                act.wait_ge(cls["turned"], 2 * i + s + 2)
                act.wait_ge(cls["up"], 2 * i + s + 1)
                act.copy(CWH[:, :], PS[:, TB, 0:P]).then_inc(cls["wh"], 1)

            pair_sums(0, 0, 0)
            for x in range(ET):
                table(None, x)
            pair_sums(1, 1, 0)
            with act.Fori(0, ROUNDS) as i:
                for z in range(NZ):
                    done = i * NZ + z
                    act.wait_ge(d_done, done + 1)
                    act.wait_ge(w_ready, done + 1)
                    act.activation(S[:, z % 2], PS[:, DB + z % 2], ACT.Silu).then_inc(silus, 1)
                    if z - 2 in CLASS_AT:
                        class_high(i, CLASS_AT[z - 2])
                    pair_sums(done + 2, z + 2, 2 * i)
                    act.wait_ge(w_ready, done + 3)
                    act.wait_ge(up_done, done + 1)
                    act.copy(WH[:, z % 2], WF[:, z % 2]).then_inc(w_high, 1)
                    if z + 1 in CLASS_AT:
                        class_sums(i, CLASS_AT[z + 1])
                    if z in CLASS_AT:
                        class_silu(i, CLASS_AT[z])
                    if table_at(z) is not None:
                        table(i, table_at(z))

        @blk.vector
        def _(dve):
            def table(i, x):
                dve.wait_ge(down_h, number(i, x) + 1)
                sl = slot(i, x)
                dve.tensor_tensor(DL[:, sl, x % ET].rearrange("p a e -> p (a e)"), PS[:, turn_bank(i, x)],
                                  DH_[:, sl, x % ET].rearrange("p a e -> p (a e)").bitcast(F32), ALU.subtract).then_inc(down_l, 1)

            def choose(done, z, chunk, half):
                g, s, j = item(z)
                pair = list(enumerate(tiles[g]))[2 * half:2 * half + 2]
                n = 2 * done + half + 1
                dve.wait_ge(g_ready, n)
                h = KH_ - 1
                for t, y in [(t, y) for t, y in pair if own_heads(t) < KH_]:
                    last = dve.tensor_scalar(V[:, z % 2, t, h], S2[:, y, h], S1[:, y, h, bass.ds((chunk + s) * RPC + j, 1)], None, ALU.add)
                last.then_inc(own_sums, 1)
                dve.wait_ge(sums, n)
                for h in range(KH_):
                    if h == KH_ - 1:
                        dve.wait_ge(own_sums, n)
                    for t, y in pair:
                        v = V[:, z % 2, t, h]
                        last = dve.scalar_tensor_tensor(v, v, TAU[:, y, h:h + 1], v, ALU.is_ge, ALU.mult)
                last.then_inc(chosen, 1)

            def class_choose(i, s):
                n, h = 2 * i + s, KH_ - 1
                dve.wait_ge(cls["gates"], n + 1)
                dve.tensor_scalar(CV[:, h], S2[:, y_cls, h], e["S1C"][:, h, bass.ds(n, 1)], None, ALU.add).then_inc(cls["own_sums"], 1)
                dve.wait_ge(cls["sums"], n + 1)
                dve.wait_ge(cls["own_sums"], n + 1)
                for h in range(KH_):
                    last = dve.scalar_tensor_tensor(CV[:, h], CV[:, h], TAU[:, y_cls, h:h + 1], CV[:, h], ALU.is_ge, ALU.mult)
                last.then_inc(cls["chosen"], 1)

            def class_weights(i, s):
                n = 2 * i + s
                dve.wait_ge(cls["silus"], n + 1)
                dve.wait_ge(cls["gates"], n + 2)
                dve.wait_ge(cls["turned"], n + 1)
                dve.tensor_tensor(CW[:, :], CS[:, :], CG[:, :], ALU.mult).then_inc(cls["w"], 1)

            def class_low(i, s):
                dve.wait_ge(cls["wh"], 2 * i + s + 1)
                dve.wait_ge(cls["up"], 2 * i + s + 1)
                dve.tensor_tensor(CWL[:, :], PS[:, TB, 0:P], CWH[:, :].bitcast(F32), ALU.subtract).then_inc(cls["wl"], 1)

            def class_add(i, s):
                n = 2 * i + s
                dve.wait_ge(cls["up"], n + 2)
                dve.wait_ge(cls["added"], n + 1)
                dve.tensor_tensor(CO[:, :], CO[:, :], PS[0:B, TB], ALU.add).then_inc(cls["added"], 1)

            def add(g, ended):
                c0, n = groups[g]
                dve.wait_ge(up_done, ended)
                for f in range(DC):
                    dve.tensor_tensor(HT[:, f, c0:c0 + n], HT[:, f, c0:c0 + n], PS[:, OB + f, 0:n], ALU.add).then_inc(added, 1)

            choose(0, 0, 0, 0), table(None, 0), choose(0, 0, 0, 1)
            for x in range(1, ET):
                table(None, x)
            dve.wait_ge(up_l, ET)
            if CLASS_AT:
                dve.memset(CO[:, :], 0.0).then_inc(cls["added"], 1)
            with dve.Fori(0, ROUNDS) as i:
                for z in range(NZ):
                    done = i * NZ + z
                    if z % (2 * ET) == 1:
                        add((item(z)[0] - 1) % NGR, i * NZ + z - 1 + 2)
                    if z - 2 in CLASS_AT:
                        class_low(i, CLASS_AT[z - 2])
                    choose(done + 1, z + 1, 2 * i, 0)
                    behind = tables_behind(z)
                    if behind:
                        table(i, behind[0])
                    choose(done + 1, z + 1, 2 * i, 1)
                    if z - 3 in CLASS_AT:
                        class_add(i, CLASS_AT[z - 3])
                    dve.wait_ge(silus, done + 3)
                    dve.wait_ge(t_done, done + 2)
                    dve.wait_ge(w_low, done + 1)
                    dve.tensor_tensor(WF[:, z % 2], S[:, z % 2], PS[:, GB], ALU.mult).then_inc(w_ready, 1)
                    if z in CLASS_AT:
                        class_choose(i, CLASS_AT[z])
                    if z - 1 in CLASS_AT:
                        class_weights(i, CLASS_AT[z - 1])
                    for x in behind[1:]:
                        table(i, x)
            add(NGR - 1, ROUNDS * NZ + 2)
            if CLASS_AT:
                dve.wait_ge(cls["out"], 1)
                dve.tensor_tensor(HT[:, :, TR:T], HT[:, :, TR:T], PS[:, TB, 0:DC * B].rearrange("p (f b) -> p f b", f=DC), ALU.add)
            dve.wait_ge(added, DC * (ROUNDS * NGR + 1))

        @blk.gpsimd
        def _(pool):
            def table(i, x):
                pool.wait_ge(up_h, number(i, x) + 1)
                sl = slot(i, x)
                pool.tensor_tensor(UL[:, sl, x % ET], raw(i, x, 1), UH[:, sl, x % ET].bitcast(F32), ALU.subtract).then_inc(up_l, 1)

            links = 2 * (NZ + NZ // ET)

            def add_heads(done, chained, z, chunk):
                g, s, j = item(z)
                for half in range(2):
                    tt = slice(2 * half, 2 * half + 2)
                    v = V[:, z % 2, tt]
                    pool.wait_ge(chosen, 2 * done + half + 1)
                    pool.tensor_tensor(v[:, :, 0:2], v[:, :, 0:2], v[:, :, 2:4], ALU.add).then_inc(pool_chain, 1)
                    chained = chained + 1
                    pool.wait_ge(pool_chain, chained)
                    if j == ET - 1:
                        last = v[:, :, 0, P - 1:P]
                        y = tiles[g][2 * half]
                        pool.tensor_tensor(last, last, EXT[:, y:y + 2, bass.ds(chunk + s, 1)], ALU.add).then_inc(pool_chain, 1)
                        chained = chained + 1
                        pool.wait_ge(pool_chain, chained)
                    if half == 0:
                        pool.wait_ge(t_done, done)
                    pool.tensor_tensor(G[:, z % 2, tt], v[:, :, 0], v[:, :, 1], ALU.add).then_inc(g_ready, 1)

            def class_gates(i, s):
                n = 2 * i + s
                pool.wait_ge(cls["chosen"], n + 1)
                pool.tensor_tensor(CV[:, 0:2], CV[:, 0:2], CV[:, 2:4], ALU.add).then_inc(cls["chain"], 1)
                pool.wait_ge(cls["chain"], 2 * n + 1)
                r = slice(P - 32, P)
                pool.tensor_tensor(CV[r, 0, P - 1:P], CV[r, 0, P - 1:P], EXT[r, y_cls, bass.ds(n, 1)], ALU.add).then_inc(cls["chain"], 1)
                pool.wait_ge(cls["chain"], 2 * n + 2)
                pool.wait_ge(cls["w"], n + 1)
                pool.tensor_tensor(CG[:, :], CV[:, 0], CV[:, 1], ALU.add).then_inc(cls["gates"], 1)

            pool.memset(WH[:, 1].bitcast(F32), 0.0).then_inc(zeroed, 1)
            pool.memset(WL[:, 1].bitcast(F32), 0.0).then_inc(zeroed, 1)
            pool.memset(UH[:, 1, ET - 1].bitcast(F32), 0.0).then_inc(zeroed, 1)
            pool.memset(UL[:, 1, ET - 1].bitcast(F32), 0.0).then_inc(zeroed, 1)
            table(None, 0)
            pool.wait_ge(t_done, 1)
            add_heads(0, 0, 0, 0)
            for x in range(1, ET):
                table(None, x)
            with pool.Fori(0, ROUNDS) as i:
                for z in range(NZ):
                    done = i * NZ + z
                    behind = tables_behind(z)
                    if behind:
                        table(i, behind[0])
                    add_heads(done + 1, i * links + 2 * (z + 1 + (z + 1) // ET), z + 1, 2 * i)
                    pool.wait_ge(w_high, done + 1)
                    pool.tensor_tensor(WL[:, z % 2], WF[:, z % 2], WH[:, z % 2].bitcast(F32), ALU.subtract).then_inc(w_low, 1)
                    if z in CLASS_AT:
                        class_gates(i, CLASS_AT[z])
                    for x in behind[1:]:
                        table(i, x)
            pool.wait_ge(up_l, ROUNDS * 2 * ET + ET)
            pool.wait_ge(g_ready, 2 * (ROUNDS * NZ + 3))


def store_tokens(nc, out, k):
    PS, HT = k["PS"], k["HT"]
    NT = TR // P
    OUTS = 4
    with Stage() as ctx:
        OUT = ctx.enter_context(nc.sbuf_tensor("o_rows", [P, OUTS, D], F32))
        sem = signals(nc, ctx)
        turned, copied = sem("o_turned"), sem("o_copied")
        stored = [sem(f"o_stored{n}") for n in range(OUTS)]
        blk = ctx.enter_context(nc.Block())

        @blk.tensor
        def _(pe):
            for y in range(NT + 1):
                r = P if y < NT else B
                if y >= 4:
                    pe.wait_ge(copied, y - 3)
                for f in range(DC):
                    last = pe.transpose(PS[0:r, y % 4, f * P:(f + 1) * P], HT[:, f, y * P:y * P + r], k["ident"][:, :])
                last.then_inc(turned, 1)

        @blk.vector
        def _(dve):
            for y in range(NT + 1):
                r = P if y < NT else B
                dve.wait_ge(turned, y + 1)
                if y >= OUTS:
                    dve.wait_ge(stored[y % OUTS], 16 * (y // OUTS))
                dve.tensor_copy(OUT[0:r, y % OUTS], PS[0:r, y % 4]).then_inc(copied, 1)

        @blk.sync
        def _(sp):
            for y in range(NT + 1):
                sp.wait_ge(copied, y + 1)
                c0 = y * P
                dst = out[c0 // NCH, 1 + c0 % NCH:1 + c0 % NCH + P, :] if y < NT else out[:, 0, :]
                sp.dma_start(dst, OUT[0:P if y < NT else B, y % OUTS]).then_inc(stored[y % OUTS], 16)
            for n in range(OUTS):
                sp.wait_ge(stored[n], 16 * ((NT + OUTS - n) // OUTS))


def tower(nc, x, cls_tok, log_dt, log_w_real, w_imag, w_qkv, w_o, w_q, keys, e_down, e_up, out):
    with ExitStack() as life:
        sb = lambda ctx, n, s, d=F32: ctx.enter_context(nc.sbuf_tensor(n, s, d))
        k = {"ident": sb(life, "ident", [P, P]), "mean_w": sb(life, "mean_w", [P, P]),
             "HT": sb(life, "tokens", [P, DC, T]),
             "PS": life.enter_context(nc.psum_tensor("psum", [P, 8, GRP], F32))}
        with ExitStack() as ctx:
            m = {"U": sb(ctx, "m_u", [P, NCH, B, DC]), "turn": sb(ctx, "m_turn", [P, NCH]),
                 "decay": sb(ctx, "m_decay", [P, NCH]), "phase": sb(ctx, "m_phase", [P, 1]),
                 "quarter": sb(ctx, "m_quarter", [P, 1]), "iota": sb(ctx, "m_iota", [P, P])}
            mixer_factors(nc, x, cls_tok, log_dt, log_w_real, w_imag, k, m)
            mixer_tokens(nc, k, m)
        with ExitStack() as ctx:
            k["XH"], k["XL"] = sb(ctx, "xh", [P, DC, T], F32R), sb(ctx, "xl", [P, DC, T], F32R)
            k["PCH"], k["PCL"] = sb(ctx, "class_ph", [P, 2, NCH + 2], F32R), sb(ctx, "class_pl", [P, 2, NCH + 2], F32R)
            with Stage() as stage:
                groups = [GROUPS[-1]] + GROUPS[:-1]
                queries = ClassQueries(nc, stage, w_qkv, k)
                with nc.Block() as blk:
                    tokens = layernorm(nc, stage, blk, k, groups, k["XH"], k["XL"], "l1_", [c0 for c0, _ in groups],
                                       cls_copy=(queries.XB[:, :, :], queries.copied), beside=queries)
                    class_rows(nc, stage, blk, k, queries, tokens)
            attention(nc, w_qkv, w_o, k)
        expert_halves(nc, w_q, keys, e_down, e_up, k)
        store_tokens(nc, out, k)


def expert_halves(nc, w_q, keys, e_down, e_up, k):
    for half, groups in enumerate((GROUPS[:NG // 2], GROUPS[NG // 2:])):
        with ExitStack() as ctx:
            sb = lambda n, s, d=F32: ctx.enter_context(nc.sbuf_tensor(f"h{half}_{n}", s, d))
            widths = [max(n, P) for _, n in groups]
            at = [sum(widths[:g]) for g in range(len(groups))]
            columns = list(zip(at, widths))
            n, nt = sum(widths), sum(widths) // P
            e = {"XH": sb("xh", [P, DC, n], F32R), "XL": sb("xl", [P, DC, n], F32R),
                 "S1": sb("s1", [P, nt, KH_, ROWS_IN + RPC]), "S1C": sb("s1_class", [P, KH_, CHUNKS + 1]),
                 "S2": sb("s2", [P, nt, KH_, NK]), "TAU": sb("tau", [P, nt, KH_]), "EXT": sb("beyond", [P, nt, CHUNKS + 1])}
            with Stage() as stage:
                weights = KeyWeights(nc, stage, w_q, keys, k, f"e{half}_")
                with nc.Block() as blk:
                    tokens = layernorm(nc, stage, blk, k, groups, e["XH"], e["XL"], f"l2{half}_", at, spread=half == 1, beside=weights, bank=KH_)
                    parts = [(c0 + c, min(n, 2 * P)) for c0, n in columns for c in range(0, n, 2 * P)]
                    key_scores(nc, stage, blk, weights, k, e, parts, tokens, f"e{half}_")
            expert_layer(nc, e_down, e_up, k, e, groups[:NG // 2], columns, f"e{half}_")


def kernel(x, cls_tok, L0_tok_log_dt, L0_tok_log_w_real, L0_tok_w_imag, L0_attn_w_qkv, L0_attn_w_o,
           L0_ffn_Wq, L0_ffn_keys, L0_ffn_e_down, L0_ffn_e_up):
    import numpy as np
    import concourse.bacc as bacc
    from concourse.bass_utils import run_bass_kernel_spmd

    given = {"x": x, "cls_tok": cls_tok, "log_dt": L0_tok_log_dt, "log_w_real": L0_tok_log_w_real,
             "w_imag": L0_tok_w_imag, "w_qkv": L0_attn_w_qkv, "w_o": L0_attn_w_o, "w_q": L0_ffn_Wq,
             "keys": L0_ffn_keys, "e_down": L0_ffn_e_down, "e_up": L0_ffn_e_up}
    nc = bacc.Bacc("TRN2", target_bir_lowering=False, num_devices=1)
    arrays = {n: np.ascontiguousarray(a) for n, a in given.items()}
    ins = [nc.dram_tensor(n, a.shape, mybir.dt.from_np(a.dtype), kind="ExternalInput").ap() for n, a in arrays.items()]
    out = nc.dram_tensor("out", (B, NCH + 1, D), F32, kind="ExternalOutput").ap()
    tower(nc, *ins, out)
    r = run_bass_kernel_spmd(nc, [arrays], core_ids=[0])
    return r.results[0]["out"]
```
